# Optimizing a Trainium2 kernel written in Bass

```python
import numpy as np
import jax
import jax.numpy as jnp

def _softmax(x, axis=-1):
    return jax.nn.softmax(x, axis=axis)

def _gelu(x):
    return jax.nn.gelu(x, approximate=True)

def _silu(x):
    return jax.nn.silu(x)

def _sigmoid(x):
    return jax.nn.sigmoid(x)

def _layernorm(x, axis=-1, eps=1e-05):
    m = jnp.mean(x, axis=axis, keepdims=True)
    v = jnp.var(x, axis=axis, keepdims=True)
    return (x - m) / jnp.sqrt(v + eps)

def _scatter_add(tgt, idx, src, axis=0):
    return tgt.at[idx].add(src)

def _segment_sum(src, seg, n):
    return jax.ops.segment_sum(src, seg, n)
kernel_name = 'mk_perceiver_d1_seqx_r4_47a45c'

def setup_inputs(seed: int=0):
    np.random.seed(seed)
    _w = jnp.asarray

    def _rec_inputs():
        import jax
        import jax.numpy as jnp
        _rk = jax.random.key(seed)
        x = -0.0002928 + 1 * jax.random.normal(jax.random.fold_in(_rk, 1), (16, 64, 256), jnp.float32)
        _lenS = 64 - jax.random.randint(jax.random.fold_in(_rk, 7), (16,), 0, max(1, 64 // 4) + 1, jnp.int32)
        _lenS2 = 256 - jax.random.randint(jax.random.fold_in(_rk, 8), (16,), 0, max(1, 256 // 4) + 1, jnp.int32)
        _ctx_1024P = jax.random.normal(jax.random.fold_in(_rk, 11), (16, 16, 256), jnp.float32)
        _ctx_1024c = jax.random.dirichlet(jax.random.fold_in(_rk, 511), 0.3 * jnp.ones((16,), jnp.float32), (16, 256))
        _ctx_1024t = jnp.einsum('bsk,bkd->bsd', _ctx_1024c, _ctx_1024P)
        _ctx_1024t = _ctx_1024t * jax.lax.rsqrt(jnp.mean(jnp.square(_ctx_1024t)) + 1e-12) * 0.953939
        ctx_1024 = -1.39393e-06 + 0.999914 * (_ctx_1024t + 0.3 * jax.random.normal(jax.random.fold_in(_rk, 611), (16, 256, 256), jnp.float32))
        return (x, ctx_1024)
    x, ctx_1024 = _rec_inputs()

    def _L0_xattn_setup():
        import jax, jax.numpy as jnp
        import numpy as np
        D_MODEL = 256
        N_HEADS = 16
        HEAD_DIM = D_MODEL // N_HEADS

        def sparsemax(x):
            x = x - jnp.max(x, axis=-1, keepdims=True)
            zs = -jnp.sort(-x, axis=-1)
            L = x.shape[-1]
            rho = jnp.arange(1, L + 1, dtype=x.dtype)
            cssv = jnp.cumsum(zs, axis=-1) - 1.0
            support = zs > cssv / rho
            k = jnp.maximum(jnp.sum(support, axis=-1, keepdims=True), 1)
            tau = jnp.take_along_axis(cssv, k - 1, axis=-1) / k.astype(x.dtype)
            return jnp.clip(x - tau, 0.0)

        def _split_heads(x):
            B, L, _ = x.shape
            return x.reshape(B, L, N_HEADS, HEAD_DIM).transpose(0, 2, 1, 3)
        key = jax.random.key(seed)
        ks = jax.random.split(key, 11)
        B, L = (2, 512)
        s = 0.02
        inp = {'q': jax.random.normal(ks[0], (B, L, D_MODEL), jnp.float32), 'k': jax.random.normal(ks[1], (B, L, D_MODEL), jnp.float32), 'v': jax.random.normal(ks[2], (B, L, D_MODEL), jnp.float32), 'Wq': jax.random.normal(ks[3], (D_MODEL, D_MODEL), jnp.float32) * s, 'bq': jnp.zeros((D_MODEL,), jnp.float32), 'Wk': jax.random.normal(ks[4], (D_MODEL, D_MODEL), jnp.float32) * s, 'bk': jnp.zeros((D_MODEL,), jnp.float32), 'Wv': jax.random.normal(ks[5], (D_MODEL, D_MODEL), jnp.float32) * s, 'bv': jnp.zeros((D_MODEL,), jnp.float32), 'Wo': jax.random.normal(ks[6], (D_MODEL, D_MODEL), jnp.float32) * s, 'bo': jnp.zeros((D_MODEL,), jnp.float32)}
        return inp
    _L0_xattn_all = _L0_xattn_setup()
    _L0_xattn_in = {k: v for k, v in _L0_xattn_all.items() if k in ('Wq', 'bq', 'Wk', 'bk', 'Wv', 'bv', 'Wo', 'bo')}
    del _L0_xattn_all

    def _L0_attn_setup():
        import jax, jax.numpy as jnp
        import numpy as np
        NUM_HEADS = 16
        WINDOW = 7

        def _window_indices(seq_len, window):
            half = window // 2
            idx = np.zeros((seq_len, window), dtype=np.int32)
            for i in range(seq_len):
                start = max(0, i - half)
                end = min(seq_len, i + half + 1)
                win = np.arange(start, end, dtype=np.int32)
                pad = window - len(win)
                if pad > 0:
                    if start == 0:
                        win = np.concatenate([win, np.full(pad, seq_len - 1, dtype=np.int32)])
                    else:
                        win = np.concatenate([np.zeros(pad, dtype=np.int32), win])
                idx[i] = win
            return jnp.asarray(idx)
        key = jax.random.key(seed)
        ks = jax.random.split(key, 7)
        B, S, E = (4, 512, 256)
        D = E // NUM_HEADS
        s_e = 1.0 / np.sqrt(E)
        s_d = 1.0 / np.sqrt(D)
        return {'x': jax.random.normal(ks[0], (B, S, E), jnp.float32), 'W_qkv': jax.random.normal(ks[1], (3 * E, E), jnp.float32) * s_e, 'b_qkv': jnp.zeros((3 * E,), jnp.float32), 'W_lat': jax.random.normal(ks[2], (D, D), jnp.float32) * s_d, 'b_lat': jnp.zeros((D,), jnp.float32), 'W_proj': jax.random.normal(ks[3], (E, E), jnp.float32) * s_e, 'b_proj': jnp.zeros((E,), jnp.float32)}
    _L0_attn_all = _L0_attn_setup()
    _L0_attn_in = {k: v for k, v in _L0_attn_all.items() if k in ('W_qkv', 'b_qkv', 'W_lat', 'b_lat', 'W_proj', 'b_proj')}
    del _L0_attn_all

    def _L0_ffn_setup():
        import jax, jax.numpy as jnp
        import numpy as np
        D_MODEL = 256
        N_EXPERTS = 8
        TOP_K = 2
        key = jax.random.key(seed)
        k1, k2, k3, k4 = jax.random.split(key, 4)
        B, S, D, E = (4, 512, D_MODEL, N_EXPERTS)
        dff = 4 * D
        lim = float(np.sqrt(6.0 / (D + dff)))
        return {'x': jax.random.normal(k1, (B, S, D), dtype=jnp.float32), 'router_w': jax.random.normal(k2, (D, E), dtype=jnp.float32) * (1.0 / np.sqrt(D)), 'router_b': jnp.zeros((E,), dtype=jnp.float32), 'expert_up': jax.random.uniform(k3, (E, dff, D), dtype=jnp.float32, minval=-lim, maxval=lim), 'expert_down': jax.random.uniform(k4, (E, D, dff), dtype=jnp.float32, minval=-lim, maxval=lim)}
    _L0_ffn_all = _L0_ffn_setup()
    _L0_ffn_in = {k: v for k, v in _L0_ffn_all.items() if k in ('router_w', 'router_b', 'expert_up', 'expert_down')}
    del _L0_ffn_all
    return {'x': x, 'ctx_1024': ctx_1024, 'L0_xattn_Wq': _L0_xattn_in['Wq'], 'L0_xattn_bq': _L0_xattn_in['bq'], 'L0_xattn_Wk': _L0_xattn_in['Wk'], 'L0_xattn_bk': _L0_xattn_in['bk'], 'L0_xattn_Wv': _L0_xattn_in['Wv'], 'L0_xattn_bv': _L0_xattn_in['bv'], 'L0_xattn_Wo': _L0_xattn_in['Wo'], 'L0_xattn_bo': _L0_xattn_in['bo'], 'L0_attn_W_qkv': _L0_attn_in['W_qkv'], 'L0_attn_b_qkv': _L0_attn_in['b_qkv'], 'L0_attn_W_lat': _L0_attn_in['W_lat'], 'L0_attn_b_lat': _L0_attn_in['b_lat'], 'L0_attn_W_proj': _L0_attn_in['W_proj'], 'L0_attn_b_proj': _L0_attn_in['b_proj'], 'L0_ffn_router_w': _L0_ffn_in['router_w'], 'L0_ffn_router_b': _L0_ffn_in['router_b'], 'L0_ffn_expert_up': _L0_ffn_in['expert_up'], 'L0_ffn_expert_down': _L0_ffn_in['expert_down']}

def reference(x, ctx_1024, L0_xattn_Wq, L0_xattn_bq, L0_xattn_Wk, L0_xattn_bk, L0_xattn_Wv, L0_xattn_bv, L0_xattn_Wo, L0_xattn_bo, L0_attn_W_qkv, L0_attn_b_qkv, L0_attn_W_lat, L0_attn_b_lat, L0_attn_W_proj, L0_attn_b_proj, L0_ffn_router_w, L0_ffn_router_b, L0_ffn_expert_up, L0_ffn_expert_down):
    import jax
    import jax.numpy as jnp

    def _L0_xattn_ref(q, k, v, Wq, bq, Wk, bk, Wv, bv, Wo, bo):
        import jax, jax.numpy as jnp
        import numpy as np
        D_MODEL = 256
        N_HEADS = 16
        HEAD_DIM = D_MODEL // N_HEADS

        def sparsemax(x):
            x = x - jnp.max(x, axis=-1, keepdims=True)
            zs = -jnp.sort(-x, axis=-1)
            L = x.shape[-1]
            rho = jnp.arange(1, L + 1, dtype=x.dtype)
            cssv = jnp.cumsum(zs, axis=-1) - 1.0
            support = zs > cssv / rho
            k = jnp.maximum(jnp.sum(support, axis=-1, keepdims=True), 1)
            tau = jnp.take_along_axis(cssv, k - 1, axis=-1) / k.astype(x.dtype)
            return jnp.clip(x - tau, 0.0)

        def _split_heads(x):
            B, L, _ = x.shape
            return x.reshape(B, L, N_HEADS, HEAD_DIM).transpose(0, 2, 1, 3)
        qh = _split_heads(q @ Wq + bq)
        kh = _split_heads(k @ Wk + bk)
        vh = _split_heads(v @ Wv + bv)
        scale = HEAD_DIM ** (-0.5)
        scores = jnp.einsum('bhqd,bhkd->bhqk', qh, kh) * scale
        attn = sparsemax(scores)
        out = jnp.einsum('bhqk,bhkd->bhqd', attn, vh)
        B, L = (q.shape[0], q.shape[1])
        out = out.transpose(0, 2, 1, 3).reshape(B, L, D_MODEL)
        return out @ Wo + bo

    def _L0_attn_ref(x, W_qkv, b_qkv, W_lat, b_lat, W_proj, b_proj):
        import jax, jax.numpy as jnp
        import numpy as np
        NUM_HEADS = 16
        WINDOW = 7

        def _window_indices(seq_len, window):
            half = window // 2
            idx = np.zeros((seq_len, window), dtype=np.int32)
            for i in range(seq_len):
                start = max(0, i - half)
                end = min(seq_len, i + half + 1)
                win = np.arange(start, end, dtype=np.int32)
                pad = window - len(win)
                if pad > 0:
                    if start == 0:
                        win = np.concatenate([win, np.full(pad, seq_len - 1, dtype=np.int32)])
                    else:
                        win = np.concatenate([np.zeros(pad, dtype=np.int32), win])
                idx[i] = win
            return jnp.asarray(idx)
        B, S, E = x.shape
        H = NUM_HEADS
        D = E // H
        qkv = (x @ W_qkv.T + b_qkv).reshape(B, S, 3, H, D).transpose(2, 0, 3, 1, 4)
        q, k, v = (qkv[0], qkv[1], qkv[2])
        k_lat = k @ W_lat.T + b_lat
        v_lat = v @ W_lat.T + b_lat
        widx = _window_indices(S, WINDOW)
        kw = k_lat[:, :, widx, :]
        vw = v_lat[:, :, widx, :]
        scale = 1.0 / np.sqrt(D)
        attn = jnp.einsum('bhsd,bhswd->bhsw', q, kw) * scale
        attn = jax.nn.softmax(attn, axis=-1)
        out = jnp.einsum('bhsw,bhswd->bhsd', attn, vw)
        out = out.transpose(0, 2, 1, 3).reshape(B, S, E)
        return out @ W_proj.T + b_proj

    def _L0_ffn_ref(x, router_w, router_b, expert_up, expert_down):
        import jax, jax.numpy as jnp
        import numpy as np
        D_MODEL = 256
        N_EXPERTS = 8
        TOP_K = 2
        B, S, D = x.shape
        E = expert_up.shape[0]
        x_flat = x.reshape(-1, D)
        logits = x_flat @ router_w + router_b
        probs = jax.nn.softmax(logits, axis=-1)
        top_w, top_idx = jax.lax.top_k(probs, TOP_K)
        comb = jnp.sum(top_w[..., None] * jax.nn.one_hot(top_idx, E, dtype=x.dtype), axis=1)
        output = jnp.zeros_like(x_flat)
        for e in range(E):
            h = jax.nn.gelu(x_flat @ expert_up[e].T, approximate=False)
            out_e = h @ expert_down[e].T
            output = output + comb[:, e:e + 1] * out_e
        return output.reshape(B, S, D)
    x = x + _L0_xattn_ref(_layernorm(x, axis=-1), ctx_1024, ctx_1024, L0_xattn_Wq, L0_xattn_bq, L0_xattn_Wk, L0_xattn_bk, L0_xattn_Wv, L0_xattn_bv, L0_xattn_Wo, L0_xattn_bo)
    x = x + _L0_attn_ref(_layernorm(x, axis=-1), L0_attn_W_qkv, L0_attn_b_qkv, L0_attn_W_lat, L0_attn_b_lat, L0_attn_W_proj, L0_attn_b_proj)
    x = x + _L0_ffn_ref(_layernorm(x, axis=-1), L0_ffn_router_w, L0_ffn_router_b, L0_ffn_expert_up, L0_ffn_expert_down)
    return x

_drawn_inputs = setup_inputs


def setup_inputs(seed=0):
    import zlib

    import numpy as np

    out = dict(_drawn_inputs(seed))
    spreads = {'L0_xattn_bq': (0.0, 0.1),
     'L0_xattn_bk': (0.0, 0.8),
     'L0_xattn_bv': (0.0, 0.1),
     'L0_xattn_bo': (0.0, 0.1),
     'L0_attn_b_qkv': (0.0, 0.1),
     'L0_attn_b_lat': (0.0, 0.1),
     'L0_attn_b_proj': (0.0, 0.1),
     'L0_ffn_router_b': (0.0, 0.283)}
    factors = {}
    for name, (base, spread) in spreads.items():
        noise = np.random.default_rng([zlib.crc32(name.encode()), seed]).standard_normal(out[name].shape)
        drawn = base * np.exp(spread * noise) if base else spread * noise
        out[name] = jnp.asarray(drawn.astype(out[name].dtype))
    for name, factor in factors.items():
        out[name] = (out[name] * factor).astype(out[name].dtype)
    return out
```

```python
from contextlib import ExitStack

import numpy as np

import concourse.bass as bass
from concourse import mybir

F32 = mybir.dt.float32
BF16 = mybir.dt.bfloat16
U32 = mybir.dt.uint32
ALU = mybir.AluOpType
ACT = mybir.ActivationFunctionType
AX_X = mybir.AxisListType.X

P = 128
B, L, D = 16, 64, 256
LC = 256
H = 16
HD = D // H
T = B * L // P
BT = P // L
KC = D // P
G = 4
NJ = KC * G
E, DFF = 8, 1024
FC = DFF // P
EPS = 1e-5
SCALE = HD ** -0.5
MASKED = -1e30
EVALS = 6
JD = 3
NEWTON = 24
OFF_BY = 1e-6
C3 = 3.0

FILLS = {
    0: ["xnT", "v0", "s2", "s6"],
    1: ["q", "v1", "s3", "s7"],
    2: ["k0", "s0", "s4"],
    3: ["k1", "s1", "s5"],
    4: ["t0", "t4", "av", "v", "l1", "u1", "pr"],
    5: ["t1", "t5", "wo", "kl", "l2", "u2", "x3T"],
    6: ["t2", "t6", "x2T", "vl", "l3", "u3", "rt"],
    7: ["t3", "t7", "qk", "l0", "u0", "av2"],
}
WHERE = {name: (bank, i, len(names)) for bank, names in FILLS.items() for i, name in enumerate(names)}

LEVELS = [3] + [10] * (EVALS - 1)


def level(it, b, k):
    return sum(2 * LEVELS[i] for i in range(it)) + b * LEVELS[it] + k + 1


PER = {"update_step": 2 * sum(LEVELS), "start_step": 2 * 8, "stats": 2, "clip": 2,
       "sum_act": 2 * EVALS, "sum_dve": 2 * EVALS, "router_step": 11, "off_step": 4}
ZEROED = 5
A0, A1, A2 = -0.0272, 1.527, 1.368
SLOPE = 24.0

SLOTS = [[("B", "weights")], [("B", "out")],  [("F", "norm"), ("B", "norm2")], [("F", "qk"), ("B", "qkv")],
         [("F", "v"), ("B", "latent")], [("F", "scores0"), ("B", "scores2")], [("F", "scores1"), ("B", "exp2")],
         [], [("B", "sum2")], [("B", "attend2")], [], [("B", "proj")], [("B", "router"), ("B", "top2")]]


def program(nc, a, out, debug=None):
    with ExitStack() as ctx:
        def sb(name, shape, dt=F32):
            return ctx.enter_context(nc.sbuf_tensor(name, shape, dt))

        sems = {}

        def sem(name):
            if name not in sems:
                sems[name] = ctx.enter_context(nc.semaphore(name))
            return sems[name]

        def due(name, t, k=1):
            return sem(name), PER.get(name, 1) * t + k

        bank = [ctx.enter_context(nc.psum_tensor(f"bank{i}", [P, 512], F32)) for i in range(8)]

        def ps(name):
            return bank[WHERE[name][0]]

        def full(name, t):
            i, k, n = WHERE[name]
            return sem(f"bank{i}_full"), n * t + k + 1

        def filled(name):
            return sem(f"bank{WHERE[name][0]}_full"), 1

        def emptied(name):
            return sem(f"bank{WHERE[name][0]}_free"), 1

        def read_out(name, t):
            i, k, n = WHERE[name]
            return sem(f"bank{i}_free"), n * t + k + 1

        def wait_free(pe, name, t):
            i, k, n = WHERE[name]
            v = n * t + k
            if not (isinstance(v, int) and v == 0):
                pe.wait_ge(sem(f"bank{i}_free"), v)

        wq = sb("wq", [P, KC, D])
        wk = sb("wk", [P, KC, D])
        wv = sb("wv", [P, KC, D])
        wo = sb("wo", [P, KC, D])
        wqkv = sb("wqkv", [P, KC, 3 * D])
        wproj = sb("wproj", [P, KC, D])
        wlat = sb("wlat", [P, P])
        wr = sb("wr", [P, KC, E])
        bqk = sb("bqk", [P, 2 * KC])
        bqkv = sb("bqkv", [P, 3 * KC])
        blatk = sb("blatk", [P, 1])
        bvr = sb("bvr", [P, D])
        bor = sb("bor", [P, D])
        blatv = sb("blatv", [P, D])
        bpr = sb("bpr", [P, D])
        brr = sb("brr", [P, E])
        ident = sb("ident", [P, P])
        parity = sb("parity", [P, 2])
        wbias = sb("wbias", [P, L])
        iota8 = sb("iota8", [P, E])
        nhalf = sb("nhalf", [P, 1])
        phalf = sb("phalf", [P, NJ])
        zeros = sb("zeros", [P, LC])
        xin = [sb(f"xin{i}", [P, D]) for i in range(2)]
        xb = [sb(f"xb{i}", [P, D]) for i in range(2)]
        ctxT = [sb(f"ctxT{i}", [P, KC, BT * LC]) for i in range(2)]
        xn1 = sb("xn1", [P, D])
        xn1T = sb("xn1T", [P, KC, P])
        q_bd = sb("q_bd", [P, KC, BT, 2, L])
        kT = sb("kT", [P, KC, BT * LC])
        vz = [sb(f"vz{i}", [P, 2 * BT, 2, D]) for i in range(2)]
        s_sb = [sb(f"scores{i}", [P, BT, NJ, LC]) for i in range(2)]
        ln = [{n: sb(f"{n}{i}", [P, w]) for n, w in (("st", 6), ("mv", 2), ("ve", 1), ("rstd", 1))}
              for i in range(3)]
        st = sb("st_scores", [P, BT, NJ, 6])
        guess = sb("guess", [P, BT, 8, NJ])
        u_it = sb("u_it", [P, EVALS + 1, BT, NJ])
        f_it = sb("f_it", [P, EVALS, BT, NJ])
        phi = sb("phi", [P, EVALS, BT, NJ])
        tmp = sb("tmp", [P, BT, 10, NJ])
        junk = sb("junk", [P, BT, NJ, LC], BF16)
        off = sb("off", [P, 1])
        off16 = sb("off16", [P, BT * NJ])
        off16b = sb("off16b", [P, BT * NJ])
        offmax = sb("offmax", [P, 1])
        flag = sb("flag", [P, 1], U32)
        aT = sb("aT", [P, BT * G, KC, 2, P])
        oT = sb("oT", [P, KC, P])
        x1 = sb("x1", [P, D])
        x1b = sb("x1b", [P, D])
        xn2 = sb("xn2", [P, D])
        xn2T = sb("xn2T", [P, KC, P])
        q2 = sb("q2", [P, KC, BT, 2, L])
        k2T = sb("k2T", [P, KC, P])
        v2T = sb("v2T", [P, KC, P])
        klT = sb("klT", [P, KC, P])
        vz2 = sb("vz2", [L, BT, 2, D])
        a2 = sb("a2", [P, G, BT * KC, L])
        mx2 = sb("mx2", [P, G, BT * KC])
        e2 = sb("e2", [P, G, BT * KC, L])
        sm2 = sb("sm2", [P, G, BT * KC])
        rs2 = sb("rs2", [P, G, BT * KC])
        a2T = sb("a2T", [L, G, BT * KC, P])
        o2T = sb("o2T", [P, KC, P])
        x2 = sb("x2", [P, D])
        xn3 = sb("xn3", [P, D])
        xn3T = sb("xn3T", [P, KC, P])
        lg = sb("lg", [P, E])
        top = sb("top", [P, 8])
        nmx = sb("nmx", [P, 1])
        ex = sb("ex", [P, E])
        den = sb("den", [P, 1])
        rden = sb("rden", [P, 1])
        pr = sb("pr", [P, E])
        tp = sb("tp", [P, 8])
        ti = sb("ti", [P, 8], U32)
        tif = sb("tif", [P, 8])
        oh = sb("oh", [P, 2, E])
        x_all = sb("x_all", [P, T * D])
        xT_all = sb("xT_all", [P, KC, T * P])
        cw = sb("cw", [P, E])
        comb = sb("comb", [P, T * E])
        wup = [sb(f"wup{i}", [P, KC, DFF]) for i in range(2)]
        wdn = [sb(f"wdn{i}", [P, FC, D]) for i in range(2)]

        x_d = a["x"].rearrange("(t p) d -> t p d", p=P)
        c_d = a["ctxT"].rearrange("(c p) n -> p c n", p=P)
        out_d = out.rearrange("(t p) d -> p t d", p=P)
        up_d = a["upT"].rearrange("e (c p) f -> p c e f", p=P)
        dn_d = a["downT"].rearrange("e (c p) d -> p c e d", p=P)

        def w_d(name):
            return a[name].rearrange("(c p) n -> p c n", p=P)

        loads_q = [(wq, w_d("wq")), (bqk, a["bqk"]), (parity, a["parity"]), (ident, a["ident"]), (bor, a["bo"])]
        loads_kv = [(wk, w_d("wk")), (wv, w_d("wv")), (bvr, a["bv"])]
        loads_back = [(wo, w_d("wo")), (wqkv, w_d("wqkv")), (wproj, w_d("wproj")), (wlat, a["wlat"]),
                      (wr, w_d("wr")), (bqkv, a["bqkv"]), (blatk, a["blatk"]), (blatv, a["blatv"]),
                      (bpr, a["bproj"]), (brr, a["br"]), (wbias, a["wbias"]), (iota8, a["iota8"])]

        block = ctx.enter_context(nc.Block())

        def whole(x):
            return x[tuple(slice(None) for _ in x.shape)]

        def sp_front(sp, n, i):
            t = 2 * n + i
            if not (isinstance(n, int) and n == 0):
                sp.wait_ge(*due("xb", t - 2))
                sp.wait_ge(*due("xn1", t - 2))
                sp.wait_ge(*full("v1", t - 2))
            sp.dma_start(xin[i][:, :], x_d[bass.ds(t, 1), :, :].rearrange("t p d -> p (t d)")).then_inc(sem(f"x_in{i}"), 16)
            sp.dma_start(ctxT[i][:, :, :], c_d[:, :, bass.ds(t * (BT * LC), BT * LC)]).then_inc(sem(f"ctx_in{i}"), 16)

        def ln_stats(dve, n, x, t):
            dve.bn_stats(out=ln[n]["st"][:, :], in_=x).then_inc(sem(f"ln{n}_stats"), 1)
            dve.wait_ge(*due(f"ln{n}_stats", t))
            parted(dve)
            dve.bn_aggr(out=ln[n]["mv"][:, :], in_=ln[n]["st"][:, :]).then_inc(sem(f"ln{n}_mean"), 1)

        def ln_rstd(pool, n, t):
            pool.wait_ge(*due(f"ln{n}_mean", t))
            parted(pool)
            pool.tensor_scalar(ln[n]["ve"][:, :], ln[n]["mv"][:, 1:2], EPS, 1.0, ALU.add, ALU.mult).then_inc(sem(f"ln{n}_var"), 1)
            pool.wait_ge(*due(f"ln{n}_var", t))
            pool.tensor_tensor(ln[n]["rstd"][:, :], ln[n]["ve"][:, :], nhalf[:, :], op=ALU.pow).then_inc(sem(f"ln{n}_rstd"), 1)

        def ln_apply(dve, n, y, x, t, done):
            dve.wait_ge(*due(f"ln{n}_rstd", t))
            dve.tensor_scalar(y, x, ln[n]["mv"][:, 0:1], ln[n]["rstd"][:, :], ALU.subtract, ALU.mult).then_inc(sem(done), 1)

        def after_first(t):
            return not (isinstance(t, int) and t == 0)

        mm = nc.tensor.matmul

        def transposed(dst, src):
            for c in range(KC):
                last = nc.tensor.transpose(dst[:, c * P:(c + 1) * P], src[:, c * P:(c + 1) * P], ident[:, :])
            return last

        def times(dst, xT, w, width=D):
            for c in range(KC):
                last = mm(dst[:, 0:width], xT[:, c, :], w[:, c, :], start=(c == 0), stop=(c == KC - 1))
            return last

        def parted(eng):
            eng.sem_inc(sem(f"parted_{eng.engine.name}"), 1)

        def pe_front(pe, step, t, n, i):
            if step == "norm":
                pe.wait_ge(*due("xn1", t))
                wait_free(pe, "xnT", t)
                transposed(ps("xnT"), xn1).then_inc(*filled("xnT"))
            if step == "qk":
                pe.wait_ge(*read_out("xnT", t))
                wait_free(pe, "q", t)
                for c in range(KC):
                    for kk in range(KC):
                        last = mm(ps("q")[:, c * P:(c + 1) * P], wq[:, kk, c * P:(c + 1) * P], xn1T[:, kk, :],
                                  start=(kk == 0), stop=(kk == KC - 1))
                last.then_inc(*filled("q"))
                pe.wait_ge(sem(f"ctx_in{i}"), n * 16 + 16)
                for c in range(KC):
                    wait_free(pe, f"k{c}", t)
                    for kk in range(KC):
                        last = mm(ps(f"k{c}")[:, :], wk[:, kk, c * P:(c + 1) * P], ctxT[i][:, kk, :],
                                  start=(kk == 0), stop=(kk == KC - 1))
                    last.then_inc(*filled(f"k{c}"))
            if step == "v":
                for b in range(BT):
                    wait_free(pe, f"v{b}", t)
                    for j in range(2):
                        n = (2 * b + j) * P
                        for kk in range(KC):
                            last = mm(ps(f"v{b}")[:, j * D:(j + 1) * D], ctxT[i][:, kk, n:n + P], wv[:, kk, :],
                                      start=(kk == 0), stop=(kk == KC - 1))
                    last.then_inc(*filled(f"v{b}"))
            if step in ("scores0", "scores1"):
                b = int(step[-1])
                if b == 0:
                    pe.wait_ge(*read_out("q", t))
                    pe.wait_ge(*read_out("k0", t))
                    pe.wait_ge(*read_out("k1", t))
                for g in range(G):
                    f = f"s{b * G + g}"
                    wait_free(pe, f, t)
                    for c in range(KC):
                        last = mm(ps(f)[:, c * LC:(c + 1) * LC],
                                  q_bd[32 * g:32 * g + 32, c, b, :, :].rearrange("p h q -> p (h q)"),
                                  kT[32 * g:32 * g + 32, c, b * LC:(b + 1) * LC], start=True, stop=True)
                    last.then_inc(*filled(f))

        def pe_back(pe, step, t, i):
            if step == "weights":
                for m in range(BT * G):
                    b, g = divmod(m, G)
                    if g == 0:
                        pe.wait_ge(*due("clip", t, b + 1))
                    wait_free(pe, f"t{m}", t)
                    for c in range(KC):
                        for kk in range(2):
                            n = (c * 2 + kk) * P
                            last = nc.tensor.transpose(ps(f"t{m}")[:, n:n + P],
                                                       s_sb[i][:, b, 2 * g + c, kk * P:(kk + 1) * P], ident[:, :])
                    last.then_inc(*filled(f"t{m}"))
                for m in range(G, 2 * G):
                    pe.wait_ge(*read_out(f"t{m}", t))
                wait_free(pe, "av", t)
                for b in range(BT):
                    for c in range(KC):
                        for g in range(G):
                            for par in range(2):
                                for kk in range(2):
                                    last = mm(ps("av")[32 * g:32 * g + 32, c * P + b * L:c * P + (b + 1) * L],
                                              vz[i][:, 2 * b + kk, par, c * P + 32 * g:c * P + 32 * g + 32],
                                              aT[:, b * G + g, c, kk, par * L:(par + 1) * L],
                                              start=(par + kk == 0), stop=(par + kk == 2))
                last.then_inc(*filled("av"))
            if step == "out":
                pe.wait_ge(*read_out("av", t))
                wait_free(pe, "wo", t)
                times(ps("wo"), oT, wo).then_inc(*filled("wo"))
            if step == "norm2":
                pe.wait_ge(*due("xn2", t))
                wait_free(pe, "x2T", t)
                transposed(ps("x2T"), xn2).then_inc(*filled("x2T"))
            if step == "qkv":
                pe.wait_ge(*read_out("x2T", t))
                for f, first, count in (("qk", 0, 2 * KC), ("v", 2 * KC, KC)):
                    wait_free(pe, f, t)
                    for n in range(count):
                        for kk in range(KC):
                            last = mm(ps(f)[:, n * P:(n + 1) * P], wqkv[:, kk, (first + n) * P:(first + n + 1) * P],
                                      xn2T[:, kk, :], start=(kk == 0), stop=(kk == KC - 1))
                    last.then_inc(*filled(f))
            if step == "latent":
                pe.wait_ge(*read_out("qk", t))
                wait_free(pe, "kl", t)
                mm(ps("kl")[:, 0:D], wlat[:, :], k2T[:, :, :].rearrange("p c n -> p (c n)"),
                   start=True, stop=True).then_inc(*filled("kl"))
                pe.wait_ge(*read_out("v", t))
                wait_free(pe, "vl", t)
                for b in range(BT):
                    for c in range(KC):
                        n = b * D + c * P
                        last = mm(ps("vl")[0:L, n:n + P], v2T[:, c, b * L:(b + 1) * L], wlat[:, :], start=True, stop=True)
                last.then_inc(*filled("vl"))
            if step == "scores2":
                pe.wait_ge(*read_out("qk", t))
                pe.wait_ge(*read_out("kl", t))
                for g in range(G):
                    wait_free(pe, f"l{g}", t)
                    for b in range(BT):
                        for c in range(KC):
                            n = (b * KC + c) * L
                            last = mm(ps(f"l{g}")[:, n:n + L],
                                      q2[32 * g:32 * g + 32, c, b, :, :].rearrange("p h q -> p (h q)"),
                                      klT[32 * g:32 * g + 32, c, b * L:(b + 1) * L], start=True, stop=True)
                    last.then_inc(*filled(f"l{g}"))
            if step == "attend2":
                pe.wait_ge(*due("weights2", t))
                parted(pe)
                for g in range(G):
                    wait_free(pe, f"u{g}", t)
                    parted(pe)
                    for n in range(BT * KC):
                        last = nc.tensor.transpose(ps(f"u{g}")[0:L, n * P:(n + 1) * P], a2[:, g, n, :], ident[:, :])
                    last.then_inc(*filled(f"u{g}"))
                pe.wait_ge(*read_out("vl", t))
                parted(pe)
                for g in range(G):
                    pe.wait_ge(*read_out(f"u{g}", t))
                wait_free(pe, "av2", t)
                parted(pe)
                for b in range(BT):
                    for c in range(KC):
                        for g in range(G):
                            for par in range(2):
                                last = mm(ps("av2")[32 * g:32 * g + 32, c * P + b * L:c * P + (b + 1) * L],
                                          vz2[:, b, par, c * P + 32 * g:c * P + 32 * g + 32],
                                          a2T[:, g, b * KC + c, par * L:(par + 1) * L],
                                          start=(par == 0), stop=(par == 1))
                last.then_inc(*filled("av2"))
            if step == "proj":
                pe.wait_ge(*read_out("av2", t))
                wait_free(pe, "pr", t)
                times(ps("pr"), o2T, wproj).then_inc(*filled("pr"))
            if step == "router":
                pe.wait_ge(*due("xn3", t))
                wait_free(pe, "x3T", t)
                transposed(ps("x3T"), xn3).then_inc(*filled("x3T"))
                pe.wait_ge(*read_out("x3T", t))
                wait_free(pe, "rt", t)
                times(ps("rt"), xn3T, wr, E).then_inc(*filled("rt"))

        def flat(x):
            return x.rearrange("p a b -> p (a b)")

        def flat3(x):
            return x.rearrange("p a b c -> p (a b c)")

        def act_front(act, step, t, i):
            if step == "norm":
                act.wait_ge(*full("xnT", t))
                if after_first(t):
                    act.wait_ge(*full("q", t - 1))
                act.activation(flat(xn1T[:, :, :]), ps("xnT")[:, 0:D], ACT.Copy).then_inc(*emptied("xnT"))
            if step == "qk":
                for c in range(KC):
                    act.wait_ge(*full(f"k{c}", t))
                    if c == 0 and after_first(t):
                        for f in ("s4", "s5", "s6", "s7"):
                            act.wait_ge(*full(f, t - 1))
                    act.activation(kT[:, c, :], ps(f"k{c}")[:, :], ACT.Identity, bias=bqk[:, KC + c:KC + c + 1]).then_inc(*emptied(f"k{c}"))
            if step in ("scores0", "scores1"):
                b = int(step[-1])
                for g in range(G):
                    f = f"s{b * G + g}"
                    act.wait_ge(*full(f, t))
                    if g == 0 and b == 0 and after_first(t):
                        pass
                    act.activation(flat(s_sb[i][:, b, 2 * g:2 * g + 2, :]), ps(f)[:, :], ACT.Copy).then_inc(*emptied(f))

        def act_back(act, step, t, i):
            if step == "weights":
                for m in range(0, BT * G, 2):
                    act.wait_ge(*full(f"t{m}", t))
                    if m == 0 and after_first(t):
                        act.wait_ge(*full("av", t - 1))
                    act.activation(flat3(aT[:, m, :, :, :]), ps(f"t{m}")[:, :], ACT.Copy).then_inc(*emptied(f"t{m}"))
                act.wait_ge(*full("av", t))
                if after_first(t):
                    act.wait_ge(*full("wo", t - 1))
                act.activation(flat(oT[:, :, :]), ps("av")[:, 0:D], ACT.Copy).then_inc(*emptied("av"))
            if step == "norm2":
                act.wait_ge(*full("x2T", t))
                if after_first(t):
                    act.wait_ge(*full("v", t - 1))
                act.activation(flat(xn2T[:, :, :]), ps("x2T")[:, 0:D], ACT.Copy).then_inc(*emptied("x2T"))
            if step == "qkv":
                act.wait_ge(*full("v", t))
                if after_first(t):
                    act.wait_ge(*full("vl", t - 1))
                for c in range(KC):
                    last = act.activation(v2T[:, c, :], ps("v")[:, c * P:(c + 1) * P], ACT.Identity,
                                          bias=bqkv[:, 2 * KC + c:2 * KC + c + 1])
                last.then_inc(*emptied("v"))
            if step == "latent":
                act.wait_ge(*full("kl", t))
                if after_first(t):
                    for g in range(G):
                        act.wait_ge(*full(f"l{g}", t - 1))
                act.activation(flat(klT[:, :, :]), ps("kl")[:, 0:D], ACT.Identity, bias=blatk[:, :]).then_inc(*emptied("kl"))
            if step == "exp2":
                act.wait_ge(*due("shifted2", t))
                act.activation(flat3(e2[:, :, :, :]), flat3(e2[:, :, :, :]), ACT.Exp).then_inc(sem("exp2"), 1)
            if step == "attend2":
                for g in range(G):
                    act.wait_ge(*full(f"u{g}", t))
                    if g == 0 and after_first(t):
                        act.wait_ge(*full("av2", t - 1))
                    act.activation(flat(a2T[:, g, :, :]), ps(f"u{g}")[0:L, :], ACT.Copy).then_inc(*emptied(f"u{g}"))
                act.wait_ge(*full("av2", t))
                if after_first(t):
                    act.wait_ge(*full("pr", t - 1))
                act.activation(flat(o2T[:, :, :]), ps("av2")[:, 0:D], ACT.Copy).then_inc(*emptied("av2"))
            if step == "router":
                act.wait_ge(*full("x3T", t))
                if after_first(t):
                    act.wait_ge(*full("rt", t - 1))
                    act.wait_ge(*due("xT_kept", t - 1))
                act.activation(flat(xn3T[:, :, :]), ps("x3T")[:, 0:D], ACT.Copy).then_inc(*emptied("x3T"))
            if step == "top2":
                act.wait_ge(*due("router_step", t, 2))
                act.activation(ex[:, :], lg[:, :], ACT.Exp, bias=nmx[:, :], accum_out=den[:, :]).then_inc(sem("router_exp"), 1)

        def act_evals(act, it, b, t, i):
            if it == 0:
                act.wait_ge(*due("start_step", t, 8 * b + 8))
            else:
                act.wait_ge(*due("update_step", t, level(it - 1, b, LEVELS[it - 1] - 1)))
            for j in range(JD, NJ):
                last = act.activation(junk[:, b, j, :], s_sb[i][:, b, j, :], ACT.Relu, bias=u_it[:, it, b, j:j + 1],
                                      accum_out=f_it[:, it, b, j:j + 1])
            last.then_inc(sem("sum_act"), 1)

        def masked_queries(dve, dst, name, bias):
            for c in range(KC):
                for par in range(2):
                    last = dve.tensor_scalar(dst[:, c, :, par, :], ps(name)[:, c * P:(c + 1) * P].rearrange("p (b q) -> p b q", b=BT),
                                             bias[:, c:c + 1], parity[:, par:par + 1], ALU.add, ALU.mult)
            return last

        def heads_of(x, par):
            return x.rearrange("p (h two d) -> p h two d", two=2, d=HD)[:, :, par, :]

        def dve_front(dve, step, t, n, i):
            if step == "norm":
                dve.wait_ge(sem(f"x_in{i}"), n * 16 + 16)
                ln_stats(dve, 0, xin[i][:, :], t)
                if after_first(t):
                    dve.wait_ge(*full("xnT", t - 1))
                ln_apply(dve, 0, xn1[:, :], xin[i][:, :], t, "xn1")
            if step == "qk":
                dve.wait_ge(*full("q", t))
                if after_first(t):
                    for f in ("s4", "s5", "s6", "s7"):
                        dve.wait_ge(*full(f, t - 1))
                masked_queries(dve, q_bd, "q", bqk).then_inc(*emptied("q"))
            if step == "v":
                for b in range(BT):
                    dve.wait_ge(*full(f"v{b}", t))
                    for par in range(2):
                        for j in range(2):
                            last = dve.tensor_tensor(heads_of(vz[i][:, 2 * b + j, par, :], par),
                                                     heads_of(ps(f"v{b}")[:, j * D:(j + 1) * D], par),
                                                     heads_of(bvr[:, :], par), op=ALU.add)
                    last.then_inc(*emptied(f"v{b}"))

        def dve_back(dve, step, t, n, i):
            if step == "weights":
                for m in range(1, BT * G, 2):
                    dve.wait_ge(*full(f"t{m}", t))
                    if m == 1 and after_first(t):
                        dve.wait_ge(*full("av", t - 1))
                    dve.tensor_copy(flat3(aT[:, m, :, :, :]), ps(f"t{m}")[:, :]).then_inc(*emptied(f"t{m}"))
            if step == "out":
                dve.wait_ge(*full("wo", t))
                dve.wait_ge(*due("xb", t))
                dve.tensor_tensor(x1[:, :], ps("wo")[:, 0:D], xb[i][:, :], op=ALU.add).then_inc(*emptied("wo"))
                dve.wait_ge(*read_out("wo", t))
                ln_stats(dve, 1, x1[:, :], t)
            if step == "norm2":
                ln_apply(dve, 1, xn2[:, :], x1[:, :], t, "xn2")
            if step == "qkv":
                dve.wait_ge(*full("qk", t))
                masked_queries(dve, q2, "qk", bqkv)
                for c in range(KC):
                    last = dve.tensor_scalar(k2T[:, c, :], ps("qk")[:, (KC + c) * P:(KC + c + 1) * P],
                                             bqkv[:, KC + c:KC + c + 1], 0.0, ALU.add, ALU.add)
                last.then_inc(*emptied("qk"))
            if step == "latent":
                dve.wait_ge(*full("vl", t))
                for b in range(BT):
                    for par in range(2):
                        last = dve.tensor_tensor(heads_of(vz2[:, b, par, :], par), heads_of(ps("vl")[0:L, b * D:(b + 1) * D], par),
                                                 heads_of(blatv[0:L, :], par), op=ALU.add)
                last.then_inc(*emptied("vl"))
            if step == "scores2":
                for g in range(G):
                    dve.wait_ge(*full(f"l{g}", t))
                    if after_first(t):
                        dve.wait_ge(*full(f"u{g}", t - 1))
                    dve.tensor_tensor(a2[:, g, :, :], ps(f"l{g}")[:, 0:BT * KC * L].rearrange("p (n k) -> p n k", k=L),
                                      wbias[:, :].unsqueeze(1).to_broadcast([P, BT * KC, L]), op=ALU.add).then_inc(*emptied(f"l{g}"))
                for g in range(G):
                    dve.wait_ge(*read_out(f"l{g}", t))
                dve.tensor_reduce(mx2[:, :, :], a2[:, :, :, :], axis=AX_X, op=ALU.max).then_inc(sem("max2"), 1)
            if step == "sum2":
                dve.wait_ge(*due("exp2", t))
                dve.tensor_reduce(sm2[:, :, :], e2[:, :, :, :], axis=AX_X, op=ALU.add).then_inc(sem("sum2"), 1)
                dve.wait_ge(*due("sum2", t))
                dve.reciprocal(rs2[:, :, :], sm2[:, :, :]).then_inc(sem("rsum2"), 1)
            if step == "proj":
                dve.wait_ge(*full("pr", t))
                dve.wait_ge(*due("x1b", t))
                if after_first(t):
                    dve.wait_ge(*due("x_kept", t - 1))
                dve.tensor_tensor(x2[:, :], ps("pr")[:, 0:D], x1b[:, :], op=ALU.add).then_inc(*emptied("pr"))
                dve.wait_ge(*read_out("pr", t))
                ln_stats(dve, 2, x2[:, :], t)
            if step == "router":
                ln_apply(dve, 2, xn3[:, :], x2[:, :], t, "xn3")
            if step == "top2":
                def link(k, ins):
                    ins.then_inc(sem("router_step"), 1)
                    dve.wait_ge(*due("router_step", t, k))
                    parted(dve)

                dve.wait_ge(*full("rt", t))
                dve.tensor_tensor(lg[:, :], ps("rt")[:, 0:E], brr[:, :], op=ALU.add).then_inc(*emptied("rt"))
                dve.wait_ge(*read_out("rt", t))
                parted(dve)
                link(1, dve.max(out=top[:, :], in_=lg[:, :]))
                link(2, dve.tensor_scalar(nmx[:, :], top[:, 0:1], -1.0, 0.0, ALU.mult, ALU.add))
                dve.wait_ge(*due("router_exp", t))
                link(3, dve.reciprocal(rden[:, :], den[:, :]))
                link(4, dve.tensor_scalar(pr[:, :], ex[:, :], rden[:, :], 0.0, ALU.mult, ALU.add))
                link(5, dve.max(out=tp[:, :], in_=pr[:, :]))
                link(6, dve.max_index(out=ti[:, :], in_max=tp[:, :], in_values=pr[:, :]))
                link(7, dve.tensor_copy(tif[:, :], ti[:, :]))
                for k in range(2):
                    link(8 + k, dve.tensor_scalar(oh[:, k, :], iota8[:, :], tif[:, k:k + 1], tp[:, k:k + 1], ALU.is_equal, ALU.mult))
                link(10, dve.tensor_tensor(cw[:, :], oh[:, 0, :], oh[:, 1, :], op=ALU.add))
                dve.tensor_copy(comb[:, bass.ds(t * E, E)], cw[:, :]).then_inc(sem("router_step"), 1)

        def dve_stats(dve, b, t, i):
            for g in range(G):
                dve.wait_ge(*read_out(f"s{b * G + g}", t))
            for j in range(NJ):
                last = dve.bn_stats(out=st[:, b, j, :], in_=s_sb[i][:, b, j, :])
            last.then_inc(sem("stats"), 1)

        def dve_eval(dve, it, b, j, t, i):
            if j == 0:
                if it == 0:
                    dve.wait_ge(*due("start_step", t, 8 * b + 8))
                else:
                    dve.wait_ge(*due("update_step", t, level(it - 1, b, LEVELS[it - 1] - 1)))
            ins = dve.scalar_tensor_tensor(out=junk[:, b, j, :], in0=s_sb[i][:, b, j, :], scalar=u_it[:, it, b, j:j + 1],
                                           in1=zeros[:, :], op0=ALU.add, op1=ALU.max, accum_out=f_it[:, it, b, j:j + 1])
            if j == JD - 1:
                ins.then_inc(sem("sum_dve"), 1)

        def dve_update(dve, it, b, k, t):
            u, f, ph = u_it[:, it, b, :], f_it[:, it, b, :], phi[:, it, b, :]
            w = [tmp[:, b, m, :] for m in range(10)]
            if k == 0:
                dve.wait_ge(*due("sum_dve", t, 2 * it + b + 1))
                dve.wait_ge(*due("sum_act", t, 2 * it + b + 1))
            else:
                dve.wait_ge(*due("update_step", t, level(it, b, k - 1)))
            if k == 0:
                if it == 0:
                    dve.tensor_scalar(w[1], f, 1.0, 1.0, ALU.subtract, ALU.mult)
                else:
                    dve.tensor_tensor(w[1], u, u_it[:, it - 1, b, :], op=ALU.subtract)
                last = dve.tensor_scalar(w[0], f, C3, 1.0, ALU.add, ALU.mult)
            elif k == 1:
                last = dve.reciprocal(w[2], w[0])
            elif k == 2:
                if it == 0:
                    dve.scalar_tensor_tensor(out=u_it[:, 1, b, :], in0=w[1], scalar=-1.0 / SLOPE, in1=u, op0=ALU.mult, op1=ALU.add)
                last = dve.scalar_tensor_tensor(out=ph, in0=f, scalar=-1.0, in1=w[2], op0=ALU.add, op1=ALU.mult)
            elif k == 3:
                last = dve.tensor_tensor(w[3], ph, phi[:, it - 1, b, :], op=ALU.subtract)
            elif k == 4:
                dve.tensor_tensor(w[4], w[3], w[1], op=ALU.mult)
                last = dve.tensor_tensor(w[5], w[3], w[3], op=ALU.mult)
            elif k == 5:
                last = dve.tensor_scalar(w[6], w[5], 1e-30, 1.0, ALU.add, ALU.mult)
            elif k == 6:
                last = dve.reciprocal(w[7], w[6])
            elif k == 7:
                last = dve.tensor_tensor(w[8], ph, w[4], op=ALU.mult)
            elif k == 8:
                last = dve.tensor_tensor(w[9], w[8], w[7], op=ALU.mult)
            elif k == 9:
                last = dve.tensor_tensor(u_it[:, it + 1, b, :], u, w[9], op=ALU.subtract)
            last.then_inc(sem("update_step"), 1)

        def dve_general(dve, t, i):
            dve.wait_ge(*due("update_step", t, level(EVALS - 1, 1, LEVELS[-1] - 1)))
            dve.tensor_scalar(off16[:, :], f_it[:, EVALS - 1, :, :].rearrange("p b j -> p (b j)"), 1.0, 1.0, ALU.subtract, ALU.mult).then_inc(sem("off_step"), 1)
            dve.wait_ge(*due("off_step", t, 1))
            dve.tensor_tensor(off16b[:, :], off16[:, :], off16[:, :], op=ALU.mult).then_inc(sem("off_step"), 1)
            dve.wait_ge(*due("off_step", t, 2))
            dve.tensor_reduce(off[:, :], off16b[:, :], axis=AX_X, op=ALU.max).then_inc(sem("off_step"), 1)

        def dve_general_run(dve, t, i):
            dve.wait_ge(*due("off_all", t))
            dve.tensor_scalar(flag[:, :], offmax[:, :], OFF_BY, 1.0, ALU.is_gt, ALU.mult).then_inc(sem("off_step"), 1)
            dve.wait_ge(*due("off_step", t, 4))
            parted(dve)
            far = dve.value_load(flag[0:1, 0:1], min_val=0, max_val=1)
            with dve.If(far > 0):
                u = u_it[:, EVALS, :, :].rearrange("p b j -> p (b j)")
                s = s_sb[i][:, :, :, :].rearrange("p b j k -> p (b j) k")
                jk = junk[:, :, :, :].rearrange("p b j k -> p (b j) k")
                gt = tmp[:, 0, :, :].rearrange("p m j -> p (m j)")
                dve.tensor_tensor(gt[:, 0:BT * NJ], st[:, :, :, 1].rearrange("p b j -> p (b j)"), st[:, :, :, 4].rearrange("p b j -> p (b j)"), op=ALU.add)
                dve.drain()
                dve.tensor_scalar(u, gt[:, 0:BT * NJ], -0.5, 1.0 / LC, ALU.mult, ALU.add)
                dve.drain()
                with dve.Fori(0, NEWTON):
                    for j in range(BT * NJ):
                        dve.scalar_tensor_tensor(out=jk[:, j, :], in0=s[:, j, :], scalar=u[:, j:j + 1], in1=zeros[:, :],
                                                 op0=ALU.add, op1=ALU.max, accum_out=gt[:, j:j + 1])
                    dve.drain()
                    for j in range(BT * NJ):
                        dve.tensor_scalar(jk[:, j, :], jk[:, j, :], 0.0, 0.0, ALU.is_gt, ALU.add, accum_out=gt[:, 16 + j:17 + j])
                    dve.drain()
                    dve.tensor_scalar(gt[:, 32:48], gt[:, 16:32], 1.0, 1.0, ALU.max, ALU.mult)
                    dve.drain()
                    dve.reciprocal(gt[:, 48:64], gt[:, 32:48])
                    dve.drain()
                    dve.scalar_tensor_tensor(out=gt[:, 64:80], in0=gt[:, 0:16], scalar=-1.0, in1=gt[:, 48:64], op0=ALU.add, op1=ALU.mult)
                    dve.drain()
                    dve.tensor_tensor(u, u, gt[:, 64:80], op=ALU.subtract)
                    dve.drain()

        def dve_clip(dve, b, t, i):
            for j in range(NJ):
                last = dve.tensor_scalar(s_sb[i][:, b, j, :], s_sb[i][:, b, j, :], u_it[:, EVALS, b, j:j + 1], 0.0, ALU.add, ALU.max)
            last.then_inc(sem("clip"), 1)

        def pool_start(pool, b, t):
            def link(k, ins):
                ins.then_inc(sem("start_step"), 1)
                pool.wait_ge(*due("start_step", t, 8 * b + k))
                parted(pool)

            w = [guess[:, b, m, :] for m in range(8)]
            pool.wait_ge(*due("stats", t, b + 1))
            link(1, pool.tensor_tensor(w[0], st[:, b, :, 1], st[:, b, :, 4], op=ALU.add))
            link(2, pool.tensor_tensor(w[1], st[:, b, :, 2], st[:, b, :, 5], op=ALU.add))
            link(3, pool.tensor_tensor(w[2], w[1], phalf[:, :], op=ALU.pow))
            link(4, pool.tensor_scalar(w[3], w[1], -A2 / LC, -A0, ALU.mult, ALU.add))
            link(5, pool.tensor_scalar(w[4], w[0], -0.5, 0.0, ALU.mult, ALU.add))
            link(6, pool.tensor_tensor(w[5], w[3], w[4], op=ALU.add))
            link(7, pool.tensor_scalar(w[6], w[2], -A1 / LC ** 0.5, 0.0, ALU.mult, ALU.add))
            pool.tensor_tensor(u_it[:, 0, b, :], w[5], w[6], op=ALU.add).then_inc(sem("start_step"), 1)

        def pool_front(pool, step, t, n, i):
            if step == "norm":
                pool.wait_ge(sem(f"x_in{i}"), n * 16 + 16)
                ln_rstd(pool, 0, t)
                if not (isinstance(n, int) and n == 0):
                    pool.wait_ge(*read_out("wo", t - 2))
                pool.tensor_tensor(xb[i][:, :], xin[i][:, :], bor[:, :], op=ALU.add).then_inc(sem("xb"), 1)

        def pool_back(pool, step, t, n, i):
            if step == "out":
                ln_rstd(pool, 1, t)
                pool.tensor_tensor(x1b[:, :], x1[:, :], bpr[:, :], op=ALU.add).then_inc(sem("x1b"), 1)
            if step == "scores2":
                pool.wait_ge(*due("max2", t))
                pool.tensor_tensor(e2[:, :, :, :].rearrange("p g n k -> p (g n) k"), a2[:, :, :, :].rearrange("p g n k -> p (g n) k"),
                                   mx2[:, :, :].rearrange("p g n -> p (g n)").unsqueeze(2).to_broadcast([P, G * BT * KC, L]),
                                   op=ALU.subtract).then_inc(sem("shifted2"), 1)
            if step == "sum2":
                pool.wait_ge(*due("rsum2", t))
                pool.tensor_tensor(a2[:, :, :, :].rearrange("p g n k -> p (g n) k"), e2[:, :, :, :].rearrange("p g n k -> p (g n) k"),
                                   rs2[:, :, :].rearrange("p g n -> p (g n)").unsqueeze(2).to_broadcast([P, G * BT * KC, L]),
                                   op=ALU.mult).then_inc(sem("weights2"), 1)
            if step == "proj":
                ln_rstd(pool, 2, t)
                pool.tensor_copy(x_all[:, bass.ds(t * D, D)], x2[:, :]).then_inc(sem("x_kept"), 1)
            if step == "router":
                pool.wait_ge(*read_out("x3T", t))
                pool.tensor_copy(xT_all[:, :, bass.ds(t * P, P)], xn3T[:, :, :]).then_inc(sem("xT_kept"), 1)

        def pool_off(pool, t):
            pool.wait_ge(*due("off_step", t, 3))
            parted(pool)
            pool.partition_all_reduce(offmax[:, :], off[:, :], P, bass.bass_isa.ReduceOp.max).then_inc(sem("off_all"), 1)

        def pe_pass(pe, front, main, back):
            for steps in SLOTS:
                for stage, step in steps:
                    if stage == "F" and front:
                        pe_front(pe, step, 2 * front[0] + front[1], front[0], front[1])
                    if stage == "B" and back:
                        pe_back(pe, step, 2 * back[0] + back[1], back[1])

        def act_pass(act, front, main, back):
            for slot, steps in enumerate(SLOTS):
                if main and slot < 2 * EVALS:
                    act_evals(act, slot // 2, slot % 2, 2 * main[0] + main[1], main[1])
                for stage, step in steps:
                    if stage == "F" and front:
                        act_front(act, step, 2 * front[0] + front[1], front[1])
                    if stage == "B" and back:
                        act_back(act, step, 2 * back[0] + back[1], back[1])

        def dve_pass(dve, front, main, back):
            if main:
                t, i = 2 * main[0] + main[1], main[1]
                for b in range(BT):
                    dve_stats(dve, b, t, i)
            for slot, steps in enumerate(SLOTS):
                if main and slot <= 2 * EVALS:
                    it, b = divmod(slot, 2)
                    uit, ub = divmod(slot - 1, 2)
                    evals = JD if slot < 2 * EVALS else 0
                    done = 0
                    for k in range(LEVELS[uit] if slot else 0):
                        if done < evals and k % 3 == 1:
                            dve_eval(dve, it, b, done, t, i)
                            done += 1
                        dve_update(dve, uit, ub, k, t)
                    for j in range(done, evals):
                        dve_eval(dve, it, b, j, t, i)
                    if slot == 2 * EVALS:
                        dve_general(dve, t, i)
                for stage, step in steps:
                    if stage == "F" and front:
                        dve_front(dve, step, 2 * front[0] + front[1], front[0], front[1])
                    if stage == "B" and back:
                        dve_back(dve, step, 2 * back[0] + back[1], back[0], back[1])
            if main:
                dve_general_run(dve, t, i)
                for b in range(BT):
                    dve_clip(dve, b, t, i)

        def pool_pass(pool, front, main, back):
            if main:
                for b in range(BT):
                    pool_start(pool, b, 2 * main[0] + main[1])
            for steps in SLOTS:
                for stage, step in steps:
                    if stage == "F" and front:
                        pool_front(pool, step, 2 * front[0] + front[1], front[0], front[1])
                    if stage == "B" and back:
                        pool_back(pool, step, 2 * back[0] + back[1], back[0], back[1])
            if main:
                pool_off(pool, 2 * main[0] + main[1])

        def passes(eng, one_pass):
            one_pass(eng, (0, 0), None, None)
            one_pass(eng, (0, 1), (0, 0), None)
            one_pass(eng, (1, 0), (0, 1), (0, 0))
            with eng.Fori(1, T // 2 - 1) as n:
                one_pass(eng, (n, 1), (n, 0), (n - 1, 1))
                one_pass(eng, (n + 1, 0), (n, 1), (n, 0))
            last = T // 2 - 1
            one_pass(eng, (last, 1), (last, 0), (last - 1, 1))
            one_pass(eng, None, (last, 1), (last, 0))
            one_pass(eng, None, None, (last, 1))

        HT = T // 2
        hT = [s_sb[i][:, :, :, :].rearrange("p b j k -> p (b j k)").rearrange("p (f n) -> p f n", f=FC) for i in range(2)]

        def expert_loop(eng, half_up, half_down):
            def two(r, first):
                for i in range(2):
                    for h in range(2):
                        half_up(eng, r, i, h)
                        if h == 1:
                            half_down(eng, r, i, 0)
                        elif i == 1:
                            half_down(eng, r, 0, 1)
                        elif not first:
                            half_down(eng, r - 1, 1, 1)
            two(0, True)
            with eng.Fori(1, E // 2) as r:
                two(r, False)
            half_down(eng, E // 2 - 1, 1, 1)

        def pe_up(pe, r, i, h):
            q = 4 * r + (2 * i + h)
            first = isinstance(r, int) and i == 0 and h == 0
            if h == 0:
                pe.wait_ge(sem(f"w_exp{i}"), r * 32 + 32)
            for f in range(FC):
                if not (first and f < 4):
                    pe.wait_ge(sem("hidden"), q * FC + (f - 3))
                for kk in range(KC):
                    last = mm(bank[f % 4][:, :], wup[i][:, kk, f * P:(f + 1) * P], xT_all[:, kk, h * 512:(h + 1) * 512],
                              start=(kk == 0), stop=(kk == KC - 1))
                last.then_inc(sem("up"), 1)

        def pe_down(pe, r, i, h):
            q = 4 * r + (2 * i + h)
            pe.wait_ge(sem("hidden"), q * FC + FC)
            for m in range(HT):
                if not (isinstance(q, int) and q == 0):
                    pe.wait_ge(sem("acc_done"), q * HT + (m - HT + 1))
                for f in range(FC):
                    last = mm(bank[4 + m][:, 0:D], hT[h][:, f, m * P:(m + 1) * P], wdn[i][:, f, :],
                              start=(f == 0), stop=(f == FC - 1))
                last.then_inc(sem("down"), 1)

        def act_up(act, r, i, h):
            q = 4 * r + (2 * i + h)
            if not (isinstance(q, int) and q < 2):
                act.wait_ge(sem("down"), q * HT - HT)
            for f in range(FC):
                act.wait_ge(sem("up"), q * FC + (f + 1))
                act.activation(hT[h][:, f, :], bank[f % 4][:, :], ACT.Gelu).then_inc(sem("hidden"), 1)

        def dve_down(dve, r, i, h):
            q = 4 * r + (2 * i + h)
            for m in range(HT):
                tile = h * HT + m
                acc = x_all[:, tile * D:(tile + 1) * D]
                if not (isinstance(q, int) and q < 2):
                    dve.wait_ge(sem("acc_done"), q * HT + (m + 1 - 2 * HT))
                dve.wait_ge(sem("down"), q * HT + (m + 1))
                w = comb[:, bass.ds(r * 2 + (i + tile * E), 1)]
                dve.scalar_tensor_tensor(out=acc, in0=bank[4 + m][:, 0:D], scalar=w, in1=acc, op0=ALU.mult, op1=ALU.add)\
                   .then_inc(sem("acc_done"), 1)

        def sp_experts(sp):
            with sp.Fori(1, E // 2) as r:
                for i in range(2):
                    sp.wait_ge(sem("down"), r * (4 * HT) + (2 * HT * i - 2 * HT))
                    sp.dma_start(wup[i][:, :, :], up_d[:, :, bass.ds(r * 2 + i, 1), :].rearrange("p c e f -> p c (e f)")).then_inc(sem(f"w_exp{i}"), 16)
                    sp.dma_start(wdn[i][:, :, :], dn_d[:, :, bass.ds(r * 2 + i, 1), :].rearrange("p c e d -> p c (e d)")).then_inc(sem(f"w_exp{i}"), 16)
            sp.wait_ge(sem("acc_done"), E * T)
            sp.dma_start(out_d, x_all[:, :].rearrange("p (t d) -> p t d", t=T)).then_inc(sem("out"), 16)
            sp.wait_ge(sem("out"), 16)

        def weights_arrived(eng):
            eng.wait_ge(sem("w_q"), 16 * len(loads_q))
            eng.wait_ge(sem("w_kv"), 16 * len(loads_kv))
            eng.wait_ge(sem("w_back"), 16 * len(loads_back))

        @block.sync
        def _(sp):
            sp_front(sp, 0, 0)
            for dst, src in loads_q:
                sp.dma_start(whole(dst), src).then_inc(sem("w_q"), 16)
            for dst, src in loads_kv:
                sp.dma_start(whole(dst), src).then_inc(sem("w_kv"), 16)
            sp_front(sp, 0, 1)
            for dst, src in loads_back:
                sp.dma_start(whole(dst), src).then_inc(sem("w_back"), 16)
            for e in range(2):
                sp.dma_start(wup[e][:, :, :], up_d[:, :, e, :]).then_inc(sem(f"w_exp{e}"), 16)
                sp.dma_start(wdn[e][:, :, :], dn_d[:, :, e, :]).then_inc(sem(f"w_exp{e}"), 16)
            with sp.Fori(1, T // 2) as n:
                for i in range(2):
                    sp_front(sp, n, i)
            sp_experts(sp)

        @block.tensor
        def _(pe):
            weights_arrived(pe)
            passes(pe, pe_pass)
            pe.wait_ge(*due("xT_kept", T - 1))
            expert_loop(pe, pe_up, pe_down)

        @block.scalar
        def _(act):
            weights_arrived(act)
            passes(act, act_pass)
            act.wait_ge(sem("bank4_full"), len(FILLS[4]) * T)
            expert_loop(act, act_up, lambda *_: None)

        @block.vector
        def _(dve):
            dve.memset(zeros[:, :], 0.0).then_inc(sem("zeros"), 1)
            weights_arrived(dve)
            dve.wait_ge(sem("zeros"), 1)
            dve.wait_ge(sem("zeroed"), ZEROED)
            passes(dve, dve_pass)
            dve.wait_ge(*due("x_kept", T - 1))
            dve.wait_ge(*due("router_step", T - 1, PER["router_step"]))
            expert_loop(dve, lambda *_: None, dve_down)

        @block.gpsimd
        def _(pool):
            for dst, value in ((nhalf, -0.5), (phalf, 0.5), (vz[0], 0.0), (vz[1], 0.0), (vz2, 0.0)):
                pool.memset(whole(dst), value).then_inc(sem("zeroed"), 1)
            pool.wait_ge(sem("zeroed"), ZEROED)
            weights_arrived(pool)
            passes(pool, pool_pass)


INPUTS = ["x", "ctxT", "wq", "wk", "wv", "wo", "wqkv", "wproj", "wlat", "wr", "bqk", "bqkv", "blatk",
          "bv", "bo", "blatv", "bproj", "br", "ident", "parity", "wbias", "iota8", "upT", "downT"]


def layouts(i):
    def c(x):
        return np.ascontiguousarray(x)

    def column(b):
        return c(b.reshape(-1, P).T)

    def rows(b):
        return c(np.broadcast_to(b.reshape(1, -1), (P, b.size)))

    heads = P // HD
    wlat = np.zeros((heads, HD, heads, HD), np.float32)
    for h in range(heads):
        wlat[h, :, h, :] = i["L0_attn_W_lat"].T
    p = np.arange(P)
    parity = np.where((p[:, None] // HD) % 2 == np.arange(2)[None, :], SCALE, 0.0).astype(np.float32)
    count = np.zeros((L, L))
    for q in range(L):
        win = list(range(max(0, q - 3), min(L, q + 4)))
        win += [L - 1 if q < 3 else 0] * (7 - len(win))
        for k in win:
            count[q, k] += 1
    wbias = np.full((L, L), MASKED, np.float32)
    wbias[count > 0] = np.log(count[count > 0])
    return {
        "x": i["x"].reshape(B * L, D), "ctxT": c(i["ctx_1024"].reshape(B * LC, D).T),
        "wq": i["L0_xattn_Wq"], "wk": i["L0_xattn_Wk"], "wv": i["L0_xattn_Wv"], "wo": i["L0_xattn_Wo"],
        "wqkv": c(i["L0_attn_W_qkv"].T), "wproj": c(i["L0_attn_W_proj"].T), "wlat": wlat.reshape(P, P),
        "wr": i["L0_ffn_router_w"],
        "bqk": column(np.concatenate([i["L0_xattn_bq"], i["L0_xattn_bk"]])), "bqkv": column(i["L0_attn_b_qkv"]),
        "blatk": c(np.tile(i["L0_attn_b_lat"], heads).reshape(P, 1)),
        "bv": rows(i["L0_xattn_bv"]), "bo": rows(i["L0_xattn_bo"]), "blatv": rows(np.tile(i["L0_attn_b_lat"], H)),
        "bproj": rows(i["L0_attn_b_proj"]), "br": rows(i["L0_ffn_router_b"]),
        "ident": np.eye(P, dtype=np.float32), "parity": parity, "wbias": c(np.tile(wbias, (2, 1))),
        "iota8": np.tile(np.arange(E, dtype=np.float32), (P, 1)),
        "upT": c(i["L0_ffn_expert_up"].transpose(0, 2, 1)), "downT": c(i["L0_ffn_expert_down"].transpose(0, 2, 1)),
    }


def kernel(**inputs):
    import concourse.bacc as bacc
    from concourse.bass_utils import run_bass_kernel_spmd

    arrays = layouts({k: np.asarray(v) for k, v in inputs.items()})
    nc = bacc.Bacc("TRN2", target_bir_lowering=False, num_devices=1)
    aps = {n: nc.dram_tensor(f"in_{n}", arrays[n].shape, F32, kind="ExternalInput").ap() for n in INPUTS}
    out = nc.dram_tensor("out", (B * L, D), F32, kind="ExternalOutput").ap()
    program(nc, aps, out)
    got = run_bass_kernel_spmd(nc, [{f"in_{n}": arrays[n] for n in INPUTS}], core_ids=[0])
    return got.results[0]["out"].reshape(B, L, D)
```

```python
from contextlib import ExitStack

import numpy as np

import concourse.bass as bass
from concourse import mybir

F32 = mybir.dt.float32
BF16 = mybir.dt.bfloat16
U32 = mybir.dt.uint32
ALU = mybir.AluOpType
ACT = mybir.ActivationFunctionType
AX_X = mybir.AxisListType.X

P = 128
B, L, D = 16, 64, 256
LC = 256
H = 16
HD = D // H
T = B * L // P
BT = P // L
KC = D // P
G = 4
NJ = KC * G
E, DFF = 8, 1024
FC = DFF // P
EPS = 1e-5
SCALE = HD ** -0.5
MASKED = -1e30
EVALS = 5
ND = 6
MAX_BLOCKS = 2 * B * L // P + E - 1
NEWTON = 24
OFF_BY = 1e-6
C3 = 2.0

PASS = [
    ("M", "sums00"), ("B", "clip0"), ("C", "turn2"), ("M", "sums01"), ("M", "update0"), ("C", "attend2"),
    ("B", "clip1"), ("B", "weights0"), ("M", "sums10"), ("B", "weights1"), ("F", "stats"), ("C", "proj"),
    ("M", "sums11"), ("M", "update1"), ("C", "norm3"), ("B", "attend"), ("F", "norm"), ("F", "queries"),
    ("M", "sums20"), ("B", "out"), ("F", "keys"), ("B", "norm2"), ("M", "sums21"), ("M", "update2"),
    ("F", "scores0"), ("C", "router"), ("B", "qkv"), ("F", "xb"), ("M", "sums30"), ("F", "scores1"),
    ("M", "sums31"), ("M", "update3"), ("B", "latent"), ("F", "scores2"), ("C", "logits"), ("F", "scores3"),
    ("M", "sums40"), ("F", "start0"), ("B", "windows"), ("B", "exp2"), ("F", "start1"), ("B", "sum2"),
    ("M", "sums41"), ("M", "update4"), ("M", "general"), ("F", "v0"), ("F", "v1"),
]
LAG = {"F": 0, "M": 1, "B": 2, "C": 3}

BANKS = {
    "norm": {"xnT": 0}, "queries": {"q": 1}, "keys": {"k0": 2, "k1": 3}, "v0": {"v0": 0}, "v1": {"v1": 1},
    "scores0": {"s0": 0, "s1": 1}, "scores1": {"s2": 2, "s3": 3}, "scores2": {"s4": 0, "s5": 1}, "scores3": {"s6": 2, "s7": 3},
    "weights0": {"t0": 4, "t1": 5, "t2": 6, "t3": 7}, "weights1": {"t4": 4, "t5": 5, "t6": 6, "t7": 7},
    "attend": {"av": 4}, "out": {"wo": 5}, "norm2": {"x2T": 6}, "qkv": {"qk": 7, "v": 4},
    "latent": {"kl": 5, "vl": 6}, "windows": {"l0": 7, "l1": 4, "l2": 5, "l3": 6},
    "turn2": {"u0": 4, "u1": 5, "u2": 6, "u3": 7}, "attend2": {"av2": 7}, "proj": {"pr": 6},
    "router": {"x3T": 5}, "logits": {"rt": 4},
}
FILLS = {bank: [(stage, name) for stage, step in PASS for name, at in BANKS.get(step, {}).items() if at == bank] for bank in range(8)}
WHERE = {name: (bank, k, stage) for bank, fills in FILLS.items() for k, (stage, name) in enumerate(fills)}


def fills_till(name, t):
    bank, k, stage = WHERE[name]
    ahead = [LAG[stage] - LAG[other] + (i <= k) for i, (other, _) in enumerate(FILLS[bank])]
    if isinstance(t, int):
        return sum(min(max(t + x, 0), T) for x in ahead)
    return len(ahead) * t + sum(ahead)


STARTS = 9
LEVELS = [2] + [7] * (EVALS - 1)


def level(it, k):
    return sum(LEVELS[:it]) + k + 1


PER = {"update_step": sum(LEVELS), "start_step": 2 * STARTS, "stats": 2, "clip": 2,
       "sum_act": 2 * EVALS, "sum_dve": 2 * EVALS, "off_step": 4}
ZEROED = 6
SELECTED = 16
A0, A1, A2 = -0.0272, 1.527, 1.368
G0, G1 = 0.00693, 0.4176



def program(nc, a, out, debug=None):
    with ExitStack() as ctx:
        def sb(name, shape, dt=F32):
            return ctx.enter_context(nc.sbuf_tensor(name, shape, dt))

        sems = {}

        def sem(name):
            if name not in sems:
                sems[name] = ctx.enter_context(nc.semaphore(name))
            return sems[name]

        def due(name, t, k=1):
            return sem(name), PER.get(name, 1) * t + k

        bank = [ctx.enter_context(nc.psum_tensor(f"bank{i}", [P, 512], F32)) for i in range(8)]

        def ps(name):
            return bank[WHERE[name][0]]

        def full(name, t):
            return sem(f"bank{WHERE[name][0]}_full"), fills_till(name, t)

        def filled(name):
            return sem(f"bank{WHERE[name][0]}_full"), 1

        def emptied(name):
            return sem(f"bank{WHERE[name][0]}_free"), 1

        def read_out(name, t):
            return sem(f"bank{WHERE[name][0]}_free"), fills_till(name, t)

        def wait_free(pe, name, t):
            before = fills_till(name, t) - 1
            if not (isinstance(before, int) and before == 0):
                pe.wait_ge(sem(f"bank{WHERE[name][0]}_free"), before)

        wq = sb("wq", [P, KC, D])
        wk = sb("wk", [P, KC, D])
        wv = sb("wv", [P, KC, D])
        wo = sb("wo", [P, KC, D])
        wqkv = sb("wqkv", [P, KC, 3 * D])
        wproj = sb("wproj", [P, KC, D])
        wlat = sb("wlat", [P, P])
        wr = sb("wr", [P, KC, E])
        bqk = sb("bqk", [P, 2 * KC])
        bqkv = sb("bqkv", [P, 3 * KC])
        blatk = sb("blatk", [P, 1])
        bvr = sb("bvr", [P, D])
        bor = sb("bor", [P, D])
        blatv = sb("blatv", [P, D])
        bpr = sb("bpr", [P, D])
        brr = sb("brr", [P, E])
        ident = sb("ident", [P, P])
        parity = sb("parity", [P, 2])
        wbias = sb("wbias", [P, L])
        order8 = sb("order8", [P, E])
        nhalf = sb("nhalf", [P, 1])
        phalf = sb("phalf", [P, NJ])
        zeros = sb("zeros", [P, LC])
        xin = [sb(f"xin{i}", [P, D]) for i in range(2)]
        xb = [sb(f"xb{i}", [P, D]) for i in range(2)]
        ctxT = [sb(f"ctxT{i}", [P, KC, BT * LC]) for i in range(2)]
        xn1 = sb("xn1", [P, D])
        xn1T = sb("xn1T", [P, KC, P])
        q_bd = sb("q_bd", [P, KC, BT, 2, L])
        kT = sb("kT", [P, KC, BT * LC])
        vz = [sb(f"vz{i}", [P, 2 * BT, 2, D]) for i in range(2)]
        s_sb = [sb(f"scores{i}", [P, BT, NJ, LC]) for i in range(2)]
        ln = [{n: sb(f"{n}{i}", [P, w]) for n, w in (("st", 6), ("mv", 2), ("ve", 1), ("rstd", 1))}
              for i in range(3)]
        st = [sb(f"st_scores{i}", [P, BT, NJ, 6]) for i in range(2)]
        guess = sb("guess", [P, BT, 7, NJ])
        reach0 = sb("reach0", [P, BT, NJ])
        u_it = sb("u_it", [P, EVALS + 1, BT, NJ])
        f_it = sb("f_it", [P, EVALS, BT, NJ])
        phi = sb("phi", [P, EVALS, BT, NJ])
        tmp = sb("tmp", [P, 10, BT * NJ])
        junk = sb("junk", [P, BT, NJ, LC], BF16)
        off = sb("off", [P, 1])
        off16 = sb("off16", [P, BT * NJ])
        off16b = sb("off16b", [P, BT * NJ])
        offmax = sb("offmax", [P, 1])
        flag = sb("flag", [P, 1], U32)
        aT = sb("aT", [P, BT * G, KC, 2, P])
        oT = sb("oT", [P, KC, P])
        x1 = sb("x1", [P, D])
        x1b = sb("x1b", [P, D])
        xn2 = sb("xn2", [P, D])
        xn2T = sb("xn2T", [P, KC, P])
        q2 = sb("q2", [P, KC, BT, 2, L])
        k2T = sb("k2T", [P, KC, P])
        v2T = sb("v2T", [P, KC, P])
        klT = sb("klT", [P, KC, P])
        vz2 = sb("vz2", [L, BT, 2, D])
        a2 = sb("a2", [P, G, BT * KC, L])
        mx2 = sb("mx2", [P, G, BT * KC])
        e2 = sb("e2", [P, G, BT * KC, L])
        sm2 = sb("sm2", [P, G, BT * KC])
        rs2 = sb("rs2", [P, G, BT * KC])
        a2T = sb("a2T", [L, G, BT * KC, P])
        o2T = sb("o2T", [P, KC, P])
        x2 = sb("x2", [P, D])
        xn3 = sb("xn3", [P, D])
        xn3T = sb("xn3T", [P, KC, P])
        logits = sb("logits", [P, T, E])
        ex3 = sb("ex3", [P, T, E])
        probs = sb("probs", [P, T, E])
        rt_a = sb("rt_a", [P, T, E])
        rt_b = sb("rt_b", [P, T, E])
        chosen = sb("chosen", [P, 2, T, E])
        rt_r = sb("rt_r", [P, 8, T])
        x_all = sb("x_all", [P, T * D])
        x3_all = sb("x3_all", [P, T, D])
        selected = sb("selected", [P, T * E])
        earlier = sb("earlier", [P, P])
        ones = sb("ones", [P, P])
        steps = sb("steps", [P, T - 1])
        before8 = sb("before8", [P, E, E])
        count = sb("count", [P, 6, E])
        over = sb("over", [P, E, T - 1])
        summed = sb("summed", [P, E, E])
        blocks = sb("blocks", [P, 2 * E], U32)
        slot_f = sb("slot_f", [P, 2, T])
        slot = sb("slot", [P, 2, T], U32)
        xe, xeT, ye = xn1, xn1T, xn2
        reach = MAX_BLOCKS + T - 1
        lists = nc.dram_tensor("lists", ((reach + 2) * P, D), F32).ap()
        results = nc.dram_tensor("results", (reach * P, D), F32).ap()
        wup = [sb(f"wup{i}", [P, KC, DFF]) for i in range(2)]
        wdn = [sb(f"wdn{i}", [P, FC, D]) for i in range(2)]

        x_d = a["x"].rearrange("(t p) d -> t p d", p=P)
        c_d = a["ctxT"].rearrange("(c p) n -> p c n", p=P)
        lists_d = lists.rearrange("(n p) d -> n p d", p=P)
        results_d = results.rearrange("(n p) d -> n p d", p=P)
        out_d = out.rearrange("(t p) d -> p t d", p=P)
        up_d = a["upT"].rearrange("e (c p) f -> p c e f", p=P)
        dn_d = a["downT"].rearrange("e (c p) d -> p c e d", p=P)

        def w_d(name):
            return a[name].rearrange("(c p) n -> p c n", p=P)

        loads_q = [(wq, w_d("wq")), (bqk, a["bqk"]), (parity, a["parity"]), (ident, a["ident"]), (bor, a["bo"])]
        loads_kv = [(wk, w_d("wk")), (wv, w_d("wv")), (bvr, a["bv"])]
        loads_back = [(wo, w_d("wo")), (wqkv, w_d("wqkv")), (wproj, w_d("wproj")), (wlat, a["wlat"]),
                      (wr, w_d("wr")), (bqkv, a["bqkv"]), (blatk, a["blatk"]), (blatv, a["blatv"]),
                      (bpr, a["bproj"]), (brr, a["br"]), (wbias, a["wbias"]), (order8, a["order8"]),
                      (earlier, a["earlier"]), (steps, a["steps"]), (before8, a["before8"])]

        block = ctx.enter_context(nc.Block())

        def whole(x):
            return x[tuple(slice(None) for _ in x.shape)]

        def sp_front(sp, n, i):
            t = 2 * n + i
            if not (isinstance(n, int) and n == 0):
                sp.wait_ge(*due("xb", t - 2))
                sp.wait_ge(*due("xn1", t - 2))
                sp.wait_ge(*full("v1", t - 2))
            sp.dma_start(xin[i][:, :], x_d[bass.ds(t, 1), :, :].rearrange("t p d -> p (t d)")).then_inc(sem(f"x_in{i}"), 16)
            sp.dma_start(ctxT[i][:, :, :], c_d[:, :, bass.ds(t * (BT * LC), BT * LC)]).then_inc(sem(f"ctx_in{i}"), 16)

        def ln_stats(dve, n, x, t):
            dve.bn_stats(out=ln[n]["st"][:, :], in_=x).then_inc(sem(f"ln{n}_stats"), 1)
            dve.wait_ge(*due(f"ln{n}_stats", t))
            parted(dve)
            dve.bn_aggr(out=ln[n]["mv"][:, :], in_=ln[n]["st"][:, :]).then_inc(sem(f"ln{n}_mean"), 1)

        def ln_rstd(pool, n, t):
            pool.wait_ge(*due(f"ln{n}_mean", t))
            parted(pool)
            pool.tensor_scalar(ln[n]["ve"][:, :], ln[n]["mv"][:, 1:2], EPS, 1.0, ALU.add, ALU.mult).then_inc(sem(f"ln{n}_var"), 1)
            pool.wait_ge(*due(f"ln{n}_var", t))
            pool.tensor_tensor(ln[n]["rstd"][:, :], ln[n]["ve"][:, :], nhalf[:, :], op=ALU.pow).then_inc(sem(f"ln{n}_rstd"), 1)

        def ln_apply(dve, n, y, x, t, done):
            dve.wait_ge(*due(f"ln{n}_rstd", t))
            dve.tensor_scalar(y, x, ln[n]["mv"][:, 0:1], ln[n]["rstd"][:, :], ALU.subtract, ALU.mult).then_inc(sem(done), 1)

        def after_first(t):
            return not (isinstance(t, int) and t == 0)

        mm = nc.tensor.matmul

        def transposed(dst, src):
            for c in range(KC):
                last = nc.tensor.transpose(dst[:, c * P:(c + 1) * P], src[:, c * P:(c + 1) * P], ident[:, :])
            return last

        def times(dst, xT, w, width=D):
            for c in range(KC):
                last = mm(dst[:, 0:width], xT[:, c, :], w[:, c, :], start=(c == 0), stop=(c == KC - 1))
            return last

        def parted(eng):
            eng.sem_inc(sem(f"parted_{eng.engine.name}"), 1)

        def pe_front(pe, step, t, n, i):
            if step == "norm":
                pe.wait_ge(*due("xn1", t))
                wait_free(pe, "xnT", t)
                transposed(ps("xnT"), xn1).then_inc(*filled("xnT"))
            if step == "queries":
                pe.wait_ge(*read_out("xnT", t))
                wait_free(pe, "q", t)
                for c in range(KC):
                    for kk in range(KC):
                        last = mm(ps("q")[:, c * P:(c + 1) * P], wq[:, kk, c * P:(c + 1) * P], xn1T[:, kk, :],
                                  start=(kk == 0), stop=(kk == KC - 1))
                last.then_inc(*filled("q"))
            if step == "keys":
                pe.wait_ge(sem(f"ctx_in{i}"), n * 16 + 16)
                for c in range(KC):
                    wait_free(pe, f"k{c}", t)
                    for kk in range(KC):
                        last = mm(ps(f"k{c}")[:, :], wk[:, kk, c * P:(c + 1) * P], ctxT[i][:, kk, :],
                                  start=(kk == 0), stop=(kk == KC - 1))
                    last.then_inc(*filled(f"k{c}"))
            if step in ("v0", "v1"):
                b = int(step[-1])
                wait_free(pe, step, t)
                for j in range(2):
                    m = (2 * b + j) * P
                    for kk in range(KC):
                        last = mm(ps(step)[:, j * D:(j + 1) * D], ctxT[i][:, kk, m:m + P], wv[:, kk, :],
                                  start=(kk == 0), stop=(kk == KC - 1))
                last.then_inc(*filled(step))
            if step.startswith("scores"):
                half = int(step[-1])
                if half == 0:
                    pe.wait_ge(*read_out("q", t))
                    pe.wait_ge(*read_out("k0", t))
                    pe.wait_ge(*read_out("k1", t))
                for m in (2 * half, 2 * half + 1):
                    b, g = divmod(m, G)
                    wait_free(pe, f"s{m}", t)
                    for c in range(KC):
                        last = mm(ps(f"s{m}")[:, c * LC:(c + 1) * LC],
                                  q_bd[32 * g:32 * g + 32, c, b, :, :].rearrange("p h q -> p (h q)"),
                                  kT[32 * g:32 * g + 32, c, b * LC:(b + 1) * LC], start=True, stop=True)
                    last.then_inc(*filled(f"s{m}"))

        def pe_back(pe, step, t, i):
            if step in ("weights0", "weights1"):
                b = int(step[-1])
                pe.wait_ge(*due("clip", t, b + 1))
                for g in range(G):
                    m = b * G + g
                    wait_free(pe, f"t{m}", t)
                    for c in range(KC):
                        for kk in range(2):
                            n = (c * 2 + kk) * P
                            last = nc.tensor.transpose(ps(f"t{m}")[:, n:n + P],
                                                       s_sb[i][:, b, 2 * g + c, kk * P:(kk + 1) * P], ident[:, :])
                    last.then_inc(*filled(f"t{m}"))
            if step == "attend":
                for m in range(G, 2 * G):
                    pe.wait_ge(*read_out(f"t{m}", t))
                wait_free(pe, "av", t)
                for b in range(BT):
                    for c in range(KC):
                        for g in range(G):
                            for par in range(2):
                                for kk in range(2):
                                    last = mm(ps("av")[32 * g:32 * g + 32, c * P + b * L:c * P + (b + 1) * L],
                                              vz[i][:, 2 * b + kk, par, c * P + 32 * g:c * P + 32 * g + 32],
                                              aT[:, b * G + g, c, kk, par * L:(par + 1) * L],
                                              start=(par + kk == 0), stop=(par + kk == 2))
                last.then_inc(*filled("av"))
            if step == "out":
                pe.wait_ge(*read_out("av", t))
                wait_free(pe, "wo", t)
                times(ps("wo"), oT, wo).then_inc(*filled("wo"))
            if step == "norm2":
                pe.wait_ge(*due("xn2", t))
                wait_free(pe, "x2T", t)
                transposed(ps("x2T"), xn2).then_inc(*filled("x2T"))
            if step == "qkv":
                pe.wait_ge(*read_out("x2T", t))
                for f, first, count in (("qk", 0, 2 * KC), ("v", 2 * KC, KC)):
                    wait_free(pe, f, t)
                    for n in range(count):
                        for kk in range(KC):
                            last = mm(ps(f)[:, n * P:(n + 1) * P], wqkv[:, kk, (first + n) * P:(first + n + 1) * P],
                                      xn2T[:, kk, :], start=(kk == 0), stop=(kk == KC - 1))
                    last.then_inc(*filled(f))
            if step == "latent":
                pe.wait_ge(*read_out("qk", t))
                wait_free(pe, "kl", t)
                mm(ps("kl")[:, 0:D], wlat[:, :], k2T[:, :, :].rearrange("p c n -> p (c n)"),
                   start=True, stop=True).then_inc(*filled("kl"))
                pe.wait_ge(*read_out("v", t))
                wait_free(pe, "vl", t)
                for b in range(BT):
                    for c in range(KC):
                        n = b * D + c * P
                        last = mm(ps("vl")[0:L, n:n + P], v2T[:, c, b * L:(b + 1) * L], wlat[:, :], start=True, stop=True)
                last.then_inc(*filled("vl"))
            if step == "windows":
                pe.wait_ge(*read_out("qk", t))
                pe.wait_ge(*read_out("kl", t))
                for g in range(G):
                    wait_free(pe, f"l{g}", t)
                    for b in range(BT):
                        for c in range(KC):
                            n = (b * KC + c) * L
                            last = mm(ps(f"l{g}")[:, n:n + L],
                                      q2[32 * g:32 * g + 32, c, b, :, :].rearrange("p h q -> p (h q)"),
                                      klT[32 * g:32 * g + 32, c, b * L:(b + 1) * L], start=True, stop=True)
                    last.then_inc(*filled(f"l{g}"))
            if step == "turn2":
                pe.wait_ge(*due("weights2", t))
                parted(pe)
                for g in range(G):
                    wait_free(pe, f"u{g}", t)
                    parted(pe)
                    for n in range(BT * KC):
                        last = nc.tensor.transpose(ps(f"u{g}")[0:L, n * P:(n + 1) * P], a2[:, g, n, :], ident[:, :])
                    last.then_inc(*filled(f"u{g}"))
            if step == "attend2":
                pe.wait_ge(*read_out("vl", t))
                parted(pe)
                for g in range(G):
                    pe.wait_ge(*read_out(f"u{g}", t))
                parted(pe)
                wait_free(pe, "av2", t)
                parted(pe)
                for b in range(BT):
                    for c in range(KC):
                        for g in range(G):
                            for par in range(2):
                                last = mm(ps("av2")[32 * g:32 * g + 32, c * P + b * L:c * P + (b + 1) * L],
                                          vz2[:, b, par, c * P + 32 * g:c * P + 32 * g + 32],
                                          a2T[:, g, b * KC + c, par * L:(par + 1) * L],
                                          start=(par == 0), stop=(par == 1))
                last.then_inc(*filled("av2"))
            if step == "proj":
                pe.wait_ge(*read_out("av2", t))
                wait_free(pe, "pr", t)
                times(ps("pr"), o2T, wproj).then_inc(*filled("pr"))
            if step == "router":
                pe.wait_ge(*due("xn3", t))
                wait_free(pe, "x3T", t)
                transposed(ps("x3T"), xn3).then_inc(*filled("x3T"))
            if step == "logits":
                pe.wait_ge(*read_out("x3T", t))
                wait_free(pe, "rt", t)
                times(ps("rt"), xn3T, wr, E).then_inc(*filled("rt"))

        def flat(x):
            return x.rearrange("p a b -> p (a b)")

        def flat3(x):
            return x.rearrange("p a b c -> p (a b c)")

        def act_front(act, step, t, i):
            if step == "norm":
                act.wait_ge(*full("xnT", t))
                if after_first(t):
                    act.wait_ge(*full("q", t - 1))
                act.activation(flat(xn1T[:, :, :]), ps("xnT")[:, 0:D], ACT.Copy).then_inc(*emptied("xnT"))
            if step == "keys":
                for c in range(KC):
                    act.wait_ge(*full(f"k{c}", t))
                    if c == 0 and after_first(t):
                        for f in ("s4", "s5", "s6", "s7"):
                            act.wait_ge(*full(f, t - 1))
                    act.activation(kT[:, c, :], ps(f"k{c}")[:, :], ACT.Identity, bias=bqk[:, KC + c:KC + c + 1]).then_inc(*emptied(f"k{c}"))
            if step.startswith("scores"):
                for m in (2 * int(step[-1]), 2 * int(step[-1]) + 1):
                    b, g = divmod(m, G)
                    act.wait_ge(*full(f"s{m}", t))
                    act.activation(flat(s_sb[i][:, b, 2 * g:2 * g + 2, :]), ps(f"s{m}")[:, :], ACT.Copy).then_inc(*emptied(f"s{m}"))

        def act_back(act, step, t, i):
            if step in ("weights0", "weights1"):
                for m in range(G * int(step[-1]), G * int(step[-1]) + G, 2):
                    act.wait_ge(*full(f"t{m}", t))
                    if m == 0 and after_first(t):
                        act.wait_ge(*full("av", t - 1))
                    act.activation(flat3(aT[:, m, :, :, :]), ps(f"t{m}")[:, :], ACT.Copy).then_inc(*emptied(f"t{m}"))
            if step == "attend":
                act.wait_ge(*full("av", t))
                if after_first(t):
                    act.wait_ge(*full("wo", t - 1))
                act.activation(flat(oT[:, :, :]), ps("av")[:, 0:D], ACT.Copy).then_inc(*emptied("av"))
            if step == "norm2":
                act.wait_ge(*full("x2T", t))
                if after_first(t):
                    act.wait_ge(*full("v", t - 1))
                act.activation(flat(xn2T[:, :, :]), ps("x2T")[:, 0:D], ACT.Copy).then_inc(*emptied("x2T"))
            if step == "qkv":
                act.wait_ge(*full("v", t))
                if after_first(t):
                    act.wait_ge(*full("vl", t - 1))
                for c in range(KC):
                    last = act.activation(v2T[:, c, :], ps("v")[:, c * P:(c + 1) * P], ACT.Identity,
                                          bias=bqkv[:, 2 * KC + c:2 * KC + c + 1])
                last.then_inc(*emptied("v"))
            if step == "latent":
                act.wait_ge(*full("kl", t))
                if after_first(t):
                    for g in range(G):
                        act.wait_ge(*full(f"l{g}", t - 1))
                act.activation(flat(klT[:, :, :]), ps("kl")[:, 0:D], ACT.Identity, bias=blatk[:, :]).then_inc(*emptied("kl"))
            if step == "exp2":
                act.wait_ge(*due("shifted2", t))
                act.activation(flat3(e2[:, :, :, :]), flat3(e2[:, :, :, :]), ACT.Exp).then_inc(sem("exp2"), 1)
            if step == "turn2":
                for g in range(G):
                    act.wait_ge(*full(f"u{g}", t))
                    if g == 0 and after_first(t):
                        act.wait_ge(*full("av2", t - 1))
                    act.activation(flat(a2T[:, g, :, :]), ps(f"u{g}")[0:L, :], ACT.Copy).then_inc(*emptied(f"u{g}"))
            if step == "attend2":
                act.wait_ge(*full("av2", t))
                if after_first(t):
                    act.wait_ge(*full("pr", t - 1))
                act.activation(flat(o2T[:, :, :]), ps("av2")[:, 0:D], ACT.Copy).then_inc(*emptied("av2"))
            if step == "router":
                act.wait_ge(*full("x3T", t))
                if after_first(t):
                    act.wait_ge(*full("rt", t - 1))
                act.activation(flat(xn3T[:, :, :]), ps("x3T")[:, 0:D], ACT.Copy).then_inc(*emptied("x3T"))

        def act_evals(act, it, half, t, i):
            middle = (ND + BT * NJ) // 2
            if half == 1:
                pass
            elif it == 0:
                act.wait_ge(*due("start_step", t, PER["start_step"]))
                if after_first(t):
                    act.wait_ge(*due("sum_act", t, 0))
            else:
                act.wait_ge(*due("update_step", t, level(it - 1, LEVELS[it - 1] - 1)))
            for m in range(middle, BT * NJ) if half else range(ND, middle):
                b, j = divmod(m, NJ)
                last = act.activation(junk[:, b, j, :], s_sb[i][:, b, j, :], ACT.Relu, bias=u_it[:, it, b, j:j + 1],
                                      accum_out=f_it[:, it, b, j:j + 1])
            last.then_inc(sem("sum_act"), 1)

        def masked_queries(dve, dst, name, bias):
            for c in range(KC):
                for par in range(2):
                    last = dve.tensor_scalar(dst[:, c, :, par, :], ps(name)[:, c * P:(c + 1) * P].rearrange("p (b q) -> p b q", b=BT),
                                             bias[:, c:c + 1], parity[:, par:par + 1], ALU.add, ALU.mult)
            return last

        def heads_of(x, par):
            return x.rearrange("p (h two d) -> p h two d", two=2, d=HD)[:, :, par, :]

        def dve_front(dve, step, t, n, i):
            if step == "stats":
                dve.wait_ge(sem(f"x_in{i}"), n * 16 + 16)
                ln_stats(dve, 0, xin[i][:, :], t)
            if step in ("start0", "start1"):
                dve_stats(dve, int(step[-1]), t, i)
            if step == "norm":
                if after_first(t):
                    dve.wait_ge(*full("xnT", t - 1))
                ln_apply(dve, 0, xn1[:, :], xin[i][:, :], t, "xn1")
            if step == "queries":
                dve.wait_ge(*full("q", t))
                if after_first(t):
                    for f in ("s4", "s5", "s6", "s7"):
                        dve.wait_ge(*full(f, t - 1))
                masked_queries(dve, q_bd, "q", bqk).then_inc(*emptied("q"))
            if step in ("v0", "v1"):
                b = int(step[-1])
                dve.wait_ge(*full(step, t))
                for par in range(2):
                    for j in range(2):
                        last = dve.tensor_tensor(heads_of(vz[i][:, 2 * b + j, par, :], par),
                                                 heads_of(ps(step)[:, j * D:(j + 1) * D], par),
                                                 heads_of(bvr[:, :], par), op=ALU.add)
                last.then_inc(*emptied(step))

        def dve_back(dve, step, t, n, i):
            if step in ("clip0", "clip1"):
                if step == "clip0":
                    dve_general_run(dve, t, i)
                dve_clip(dve, int(step[-1]), t, i)
            if step in ("weights0", "weights1"):
                for m in range(G * int(step[-1]) + 1, G * int(step[-1]) + G, 2):
                    dve.wait_ge(*full(f"t{m}", t))
                    if m == 1 and after_first(t):
                        dve.wait_ge(*full("av", t - 1))
                    dve.tensor_copy(flat3(aT[:, m, :, :, :]), ps(f"t{m}")[:, :]).then_inc(*emptied(f"t{m}"))
            if step == "out":
                dve.wait_ge(*full("wo", t))
                dve.wait_ge(*due("xb", t))
                dve.tensor_tensor(x1[:, :], ps("wo")[:, 0:D], xb[i][:, :], op=ALU.add).then_inc(*emptied("wo"))
                dve.wait_ge(*read_out("wo", t))
                ln_stats(dve, 1, x1[:, :], t)
            if step == "norm2":
                ln_apply(dve, 1, xn2[:, :], x1[:, :], t, "xn2")
            if step == "qkv":
                dve.wait_ge(*full("qk", t))
                masked_queries(dve, q2, "qk", bqkv)
                for c in range(KC):
                    last = dve.tensor_scalar(k2T[:, c, :], ps("qk")[:, (KC + c) * P:(KC + c + 1) * P],
                                             bqkv[:, KC + c:KC + c + 1], 0.0, ALU.add, ALU.add)
                last.then_inc(*emptied("qk"))
            if step == "latent":
                dve.wait_ge(*full("vl", t))
                for b in range(BT):
                    for par in range(2):
                        last = dve.tensor_tensor(heads_of(vz2[:, b, par, :], par), heads_of(ps("vl")[0:L, b * D:(b + 1) * D], par),
                                                 heads_of(blatv[0:L, :], par), op=ALU.add)
                last.then_inc(*emptied("vl"))
            if step == "windows":
                for g in range(G):
                    dve.wait_ge(*full(f"l{g}", t))
                    if after_first(t):
                        dve.wait_ge(*full(f"u{g}", t - 1))
                    dve.tensor_tensor(a2[:, g, :, :], ps(f"l{g}")[:, 0:BT * KC * L].rearrange("p (n k) -> p n k", k=L),
                                      wbias[:, :].unsqueeze(1).to_broadcast([P, BT * KC, L]), op=ALU.add).then_inc(*emptied(f"l{g}"))
                for g in range(G):
                    dve.wait_ge(*read_out(f"l{g}", t))
                dve.tensor_reduce(mx2[:, :, :], a2[:, :, :, :], axis=AX_X, op=ALU.max).then_inc(sem("max2"), 1)
            if step == "sum2":
                dve.wait_ge(*due("exp2", t))
                dve.tensor_reduce(sm2[:, :, :], e2[:, :, :, :], axis=AX_X, op=ALU.add).then_inc(sem("sum2"), 1)
                dve.wait_ge(*due("sum2", t))
                dve.reciprocal(rs2[:, :, :], sm2[:, :, :]).then_inc(sem("rsum2"), 1)
            if step == "proj":
                dve.wait_ge(*full("pr", t))
                dve.wait_ge(*due("x1b", t))
                if after_first(t):
                    dve.wait_ge(*due("x_kept", t - 1))
                dve.tensor_tensor(x2[:, :], ps("pr")[:, 0:D], x1b[:, :], op=ALU.add).then_inc(*emptied("pr"))
                dve.wait_ge(*read_out("pr", t))
                ln_stats(dve, 2, x2[:, :], t)
            if step == "norm3":
                if after_first(t):
                    dve.wait_ge(*full("x3T", t - 1))
                    dve.wait_ge(*due("x3_kept", t - 1))
                ln_apply(dve, 2, xn3[:, :], x2[:, :], t, "xn3")
            if step == "logits":
                dve.wait_ge(*full("rt", t))
                dve.tensor_tensor(logits[:, bass.ds(t, 1), :].rearrange("p t e -> p (t e)"), ps("rt")[:, 0:E], brr[:, :], op=ALU.add).then_inc(*emptied("rt"))

        def dve_stats(dve, b, t, i):
            for g in range(G):
                dve.wait_ge(*read_out(f"s{b * G + g}", t))
            for j in range(NJ):
                last = dve.bn_stats(out=st[i][:, b, j, :], in_=s_sb[i][:, b, j, :])
            last.then_inc(sem("stats"), 1)

        def dve_evals(dve, it, half, t, i):
            if half == 1:
                pass
            elif it == 0:
                dve.wait_ge(*due("start_step", t, PER["start_step"]))
                if after_first(t):
                    dve.wait_ge(*due("sum_dve", t, 0))
            else:
                dve.wait_ge(*due("update_step", t, level(it - 1, LEVELS[it - 1] - 1)))
            for m in range(ND // 2, ND) if half else range(ND // 2):
                b, j = divmod(m, NJ)
                last = dve.scalar_tensor_tensor(out=junk[:, b, j, :], in0=s_sb[i][:, b, j, :], scalar=u_it[:, it, b, j:j + 1],
                                                in1=zeros[:, :], op0=ALU.add, op1=ALU.max, accum_out=f_it[:, it, b, j:j + 1])
            last.then_inc(sem("sum_dve"), 1)

        def dve_update(dve, it, t):
            def rows(x):
                return x.rearrange("p b j -> p (b j)")

            def link(k, ins):
                ins.then_inc(sem("update_step"), 1)
                dve.wait_ge(*due("update_step", t, level(it, k)))

            u, f, psi = rows(u_it[:, it, :, :]), rows(f_it[:, it, :, :]), rows(phi[:, it, :, :])
            after = rows(u_it[:, it + 1, :, :])
            shifted, du, size, fell, rose, error, slope, scaled, inverse, step = [tmp[:, m, :] for m in range(10)]
            dve.wait_ge(*due("sum_dve", t, 2 * it + 2))
            dve.wait_ge(*due("sum_act", t, 2 * it + 2))
            dve.tensor_scalar(shifted, f, C3, 1.0, ALU.add, ALU.mult)
            if it == 0:
                link(0, dve.scalar_tensor_tensor(out=step, in0=f, scalar=-1.0, in1=rows(reach0[:, :, :]), op0=ALU.add, op1=ALU.mult))
                dve.reciprocal(psi, shifted)
                dve.tensor_tensor(after, u, step, op=ALU.subtract).then_inc(sem("update_step"), 1)
                return
            u_prev, psi_prev = rows(u_it[:, it - 1, :, :]), rows(phi[:, it - 1, :, :])
            link(0, dve.tensor_tensor(du, u, u_prev, op=ALU.subtract))
            dve.reciprocal(psi, shifted)
            link(1, dve.scalar_tensor_tensor(out=size, in0=du, scalar=-1.0, in1=du, op0=ALU.mult, op1=ALU.max))
            dve.tensor_tensor(rose, psi, psi_prev, op=ALU.subtract)
            dve.tensor_tensor(fell, psi_prev, psi, op=ALU.subtract)
            link(2, dve.tensor_scalar(error, psi, 1.0 / (1.0 + C3), 1.0, ALU.subtract, ALU.mult))
            dve.scalar_tensor_tensor(out=slope, in0=rose, scalar=1e-8, in1=fell, op0=ALU.max, op1=ALU.max)
            link(3, dve.tensor_tensor(scaled, error, size, op=ALU.mult))
            link(4, dve.reciprocal(inverse, slope))
            link(5, dve.tensor_tensor(step, scaled, inverse, op=ALU.mult))
            dve.tensor_tensor(after, u, step, op=ALU.add).then_inc(sem("update_step"), 1)

        def dve_general(dve, t, i):
            dve.wait_ge(*due("update_step", t, level(EVALS - 1, LEVELS[-1] - 1)))
            dve.tensor_scalar(off16[:, :], f_it[:, EVALS - 1, :, :].rearrange("p b j -> p (b j)"), 1.0, 1.0, ALU.subtract, ALU.mult).then_inc(sem("off_step"), 1)
            dve.wait_ge(*due("off_step", t, 1))
            dve.tensor_tensor(off16b[:, :], off16[:, :], off16[:, :], op=ALU.mult).then_inc(sem("off_step"), 1)
            dve.wait_ge(*due("off_step", t, 2))
            dve.tensor_reduce(off[:, :], off16b[:, :], axis=AX_X, op=ALU.max).then_inc(sem("off_step"), 1)

        def dve_general_run(dve, t, i):
            dve.wait_ge(*due("off_all", t))
            dve.tensor_scalar(flag[:, :], offmax[:, :], OFF_BY, 1.0, ALU.is_gt, ALU.mult).then_inc(sem("off_step"), 1)
            dve.wait_ge(*due("off_step", t, 4))
            parted(dve)
            far = dve.value_load(flag[0:1, 0:1], min_val=0, max_val=1)
            with dve.If(far > 0):
                u = u_it[:, EVALS, :, :].rearrange("p b j -> p (b j)")
                s = s_sb[i][:, :, :, :].rearrange("p b j k -> p (b j) k")
                jk = [junk[:, m // NJ, m % NJ, :] for m in range(ND)]
                gt = tmp[:, :, :].rearrange("p m j -> p (m j)")
                dve.tensor_tensor(gt[:, 0:BT * NJ], st[i][:, :, :, 1].rearrange("p b j -> p (b j)"), st[i][:, :, :, 4].rearrange("p b j -> p (b j)"), op=ALU.add)
                dve.drain()
                dve.tensor_scalar(u, gt[:, 0:BT * NJ], -0.5, 1.0 / LC, ALU.mult, ALU.add)
                dve.drain()
                with dve.Fori(0, NEWTON):
                    for j0 in range(0, BT * NJ, len(jk)):
                        js = range(j0, min(j0 + len(jk), BT * NJ))
                        for j in js:
                            dve.scalar_tensor_tensor(out=jk[j - j0], in0=s[:, j, :], scalar=u[:, j:j + 1], in1=zeros[:, :],
                                                     op0=ALU.add, op1=ALU.max, accum_out=gt[:, j:j + 1])
                        dve.drain()
                        for j in js:
                            dve.tensor_scalar(jk[j - j0], jk[j - j0], 0.0, 0.0, ALU.is_gt, ALU.add, accum_out=gt[:, 16 + j:17 + j])
                        dve.drain()
                    dve.tensor_scalar(gt[:, 32:48], gt[:, 16:32], 1.0, 1.0, ALU.max, ALU.mult)
                    dve.drain()
                    dve.reciprocal(gt[:, 48:64], gt[:, 32:48])
                    dve.drain()
                    dve.scalar_tensor_tensor(out=gt[:, 64:80], in0=gt[:, 0:16], scalar=-1.0, in1=gt[:, 48:64], op0=ALU.add, op1=ALU.mult)
                    dve.drain()
                    dve.tensor_tensor(u, u, gt[:, 64:80], op=ALU.subtract)
                    dve.drain()

        def dve_clip(dve, b, t, i):
            for j in range(NJ):
                last = dve.tensor_scalar(s_sb[i][:, b, j, :], s_sb[i][:, b, j, :], u_it[:, EVALS, b, j:j + 1], 0.0, ALU.add, ALU.max)
            last.then_inc(sem("clip"), 1)

        def pool_start(pool, b, t, i):
            def link(k, ins):
                ins.then_inc(sem("start_step"), 1)
                pool.wait_ge(*due("start_step", t, STARTS * b + k))
                parted(pool)

            w = [guess[:, b, m, :] for m in range(7)]
            pool.wait_ge(*due("stats", t, b + 1))
            link(1, pool.tensor_tensor(w[0], st[i][:, b, :, 1], st[i][:, b, :, 4], op=ALU.add))
            link(2, pool.tensor_tensor(w[1], st[i][:, b, :, 2], st[i][:, b, :, 5], op=ALU.add))
            link(3, pool.tensor_tensor(w[2], w[1], phalf[:, :], op=ALU.pow))
            link(4, pool.tensor_scalar(reach0[:, b, :], w[2], G1 / LC ** 0.5, G0, ALU.mult, ALU.add))
            link(5, pool.tensor_scalar(w[3], w[1], -A2 / LC, -A0, ALU.mult, ALU.add))
            link(6, pool.tensor_scalar(w[4], w[0], -0.5, 0.0, ALU.mult, ALU.add))
            link(7, pool.tensor_tensor(w[5], w[3], w[4], op=ALU.add))
            link(8, pool.tensor_scalar(w[6], w[2], -A1 / LC ** 0.5, 0.0, ALU.mult, ALU.add))
            pool.tensor_tensor(u_it[:, 0, b, :], w[5], w[6], op=ALU.add).then_inc(sem("start_step"), 1)

        def pool_front(pool, step, t, n, i):
            if step == "stats":
                ln_rstd(pool, 0, t)
            if step in ("start0", "start1"):
                pool_start(pool, int(step[-1]), t, i)
            if step == "xb":
                pool.wait_ge(sem(f"x_in{i}"), n * 16 + 16)
                if not (isinstance(n, int) and n == 0):
                    pool.wait_ge(*read_out("wo", t - 2))
                pool.tensor_tensor(xb[i][:, :], xin[i][:, :], bor[:, :], op=ALU.add).then_inc(sem("xb"), 1)

        def pool_back(pool, step, t, n, i):
            if step == "out":
                ln_rstd(pool, 1, t)
                pool.tensor_tensor(x1b[:, :], x1[:, :], bpr[:, :], op=ALU.add).then_inc(sem("x1b"), 1)
            if step == "windows":
                pool.wait_ge(*due("max2", t))
                pool.tensor_tensor(e2[:, :, :, :].rearrange("p g n k -> p (g n) k"), a2[:, :, :, :].rearrange("p g n k -> p (g n) k"),
                                   mx2[:, :, :].rearrange("p g n -> p (g n)").unsqueeze(2).to_broadcast([P, G * BT * KC, L]),
                                   op=ALU.subtract).then_inc(sem("shifted2"), 1)
            if step == "sum2":
                pool.wait_ge(*due("rsum2", t))
                pool.tensor_tensor(a2[:, :, :, :].rearrange("p g n k -> p (g n) k"), e2[:, :, :, :].rearrange("p g n k -> p (g n) k"),
                                   rs2[:, :, :].rearrange("p g n -> p (g n)").unsqueeze(2).to_broadcast([P, G * BT * KC, L]),
                                   op=ALU.mult).then_inc(sem("weights2"), 1)
            if step == "proj":
                ln_rstd(pool, 2, t)
                pool.tensor_copy(x_all[:, bass.ds(t * D, D)], x2[:, :]).then_inc(sem("x_kept"), 1)
            if step == "router":
                pool.wait_ge(*due("xn3", t))
                pool.tensor_copy(x3_all[:, bass.ds(t, 1), :].rearrange("p t d -> p (t d)"), xn3[:, :]).then_inc(sem("x3_kept"), 1)

        def pool_off(pool, t):
            pool.wait_ge(*due("off_step", t, 3))
            parted(pool)
            pool.partition_all_reduce(offmax[:, :], off[:, :], P, bass.bass_isa.ReduceOp.max).then_inc(sem("off_all"), 1)

        def steps_of(tiles, stages):
            for stage, step in PASS:
                if stage in stages and tiles[stage]:
                    n, i = tiles[stage]
                    yield stage, step, n, i, 2 * n + i

        def pe_pass(pe, **tiles):
            for stage, step, n, i, t in steps_of(tiles, "FBC"):
                if stage == "F":
                    pe_front(pe, step, t, n, i)
                else:
                    pe_back(pe, step, t, i)

        def act_pass(act, **tiles):
            for stage, step, n, i, t in steps_of(tiles, "FMBC"):
                if stage == "F":
                    act_front(act, step, t, i)
                elif stage == "M":
                    if step.startswith("sums"):
                        act_evals(act, int(step[4]), int(step[5]), t, i)
                else:
                    act_back(act, step, t, i)

        def dve_pass(dve, **tiles):
            for stage, step, n, i, t in steps_of(tiles, "FMBC"):
                if stage == "F":
                    dve_front(dve, step, t, n, i)
                elif stage == "M":
                    if step.startswith("sums"):
                        dve_evals(dve, int(step[4]), int(step[5]), t, i)
                    elif step.startswith("update"):
                        dve_update(dve, int(step[6]), t)
                    else:
                        dve_general(dve, t, i)
                else:
                    dve_back(dve, step, t, n, i)

        def pool_pass(pool, **tiles):
            for stage, step, n, i, t in steps_of(tiles, "FMBC"):
                if stage == "F":
                    pool_front(pool, step, t, n, i)
                elif stage == "M":
                    if step == "general":
                        pool_off(pool, t)
                else:
                    pool_back(pool, step, t, n, i)

        def passes(eng, one_pass):
            one_pass(eng, F=(0, 0), M=None, B=None, C=None)
            one_pass(eng, F=(0, 1), M=(0, 0), B=None, C=None)
            eng.wait_ge(sem("w_back"), 16 * len(loads_back))
            one_pass(eng, F=(1, 0), M=(0, 1), B=(0, 0), C=None)
            one_pass(eng, F=(1, 1), M=(1, 0), B=(0, 1), C=(0, 0))
            with eng.Fori(2, T // 2) as n:
                one_pass(eng, F=(n, 0), M=(n - 1, 1), B=(n - 1, 0), C=(n - 2, 1))
                one_pass(eng, F=(n, 1), M=(n, 0), B=(n - 1, 1), C=(n - 1, 0))
            last = T // 2 - 1
            one_pass(eng, F=None, M=(last, 1), B=(last, 0), C=(last - 1, 1))
            one_pass(eng, F=None, M=None, B=(last, 1), C=(last, 0))
            one_pass(eng, F=None, M=None, B=None, C=(last, 1))

        def dve_route(dve):
            step = [0]

            def link(ins):
                ins.then_inc(sem("route_step"), 1)
                step[0] += 1
                dve.wait_ge(sem("route_step"), step[0])

            def per_tile(k):
                return rt_r[:, k, :]

            def spread(k):
                return rt_r[:, k, :].unsqueeze(2).to_broadcast([P, T, E])

            order = order8[:, :].unsqueeze(1).to_broadcast([P, T, E])
            dve.wait_ge(*read_out("rt", T - 1))
            link(dve.tensor_reduce(per_tile(0), logits[:, :, :], axis=AX_X, op=ALU.max))
            dve.tensor_tensor(rt_a[:, :, :], logits[:, :, :], spread(0), op=ALU.subtract).then_inc(sem("logits_shifted"), 1)
            dve.wait_ge(sem("router_exp"), 1)
            link(dve.tensor_reduce(per_tile(1), ex3[:, :, :], axis=AX_X, op=ALU.add))
            link(dve.reciprocal(per_tile(2), per_tile(1)))
            link(dve.tensor_tensor(probs[:, :, :], ex3[:, :, :], spread(2), op=ALU.mult))
            left = probs
            for k in range(2):
                link(dve.tensor_reduce(per_tile(3 + 2 * k), left[:, :, :], axis=AX_X, op=ALU.max))
                link(dve.tensor_tensor(rt_b[:, :, :], left[:, :, :], spread(3 + 2 * k), op=ALU.is_equal))
                link(dve.tensor_tensor(ex3[:, :, :], rt_b[:, :, :], order, op=ALU.mult))
                link(dve.tensor_reduce(per_tile(4 + 2 * k), ex3[:, :, :], axis=AX_X, op=ALU.max))
                link(dve.tensor_tensor(chosen[:, k, :, :], order, spread(4 + 2 * k), op=ALU.is_equal))
                if k == 0:
                    link(dve.scalar_tensor_tensor(out=rt_a[:, :, :], in0=chosen[:, 0, :, :], scalar=-2.0, in1=probs[:, :, :],
                                                  op0=ALU.mult, op1=ALU.add))
                    left = rt_a
            link(dve.tensor_tensor(selected[:, :].rearrange("p (t e) -> p t e", t=T), chosen[:, 0, :, :], chosen[:, 1, :, :], op=ALU.add))
            dve.wait_ge(sem("ranked"), 1)
            link(dve.tensor_reduce(count[:, 0, :], bank[1][:, 0:T * E].rearrange("p (t e) -> p e t", t=T), axis=AX_X, op=ALU.add))
            link(dve.tensor_tensor(over[:, :, :], count[:, 0, :].unsqueeze(2).to_broadcast([P, E, T - 1]),
                                   steps[:, :].unsqueeze(1).to_broadcast([P, E, T - 1]), op=ALU.is_gt))
            link(dve.tensor_reduce(count[:, 1, :], over[:, :, :], axis=AX_X, op=ALU.add))
            link(dve.tensor_scalar(count[:, 2, :], count[:, 1, :], 1.0, 1.0, ALU.add, ALU.mult))
            link(dve.tensor_tensor(summed[:, :, :], count[:, 2, :].unsqueeze(1).to_broadcast([P, E, E]), before8[:, :, :], op=ALU.mult))
            link(dve.tensor_reduce(count[:, 3, :], summed[:, :, :], axis=AX_X, op=ALU.add))
            link(dve.tensor_scalar(count[:, 4, :], count[:, 3, :], float(P), 1.0, ALU.mult, ALU.mult))
            link(dve.tensor_tensor(rt_b[:, :, :], bank[0][:, 0:T * E].rearrange("p (t e) -> p t e", t=T),
                                   count[:, 4, :].unsqueeze(1).to_broadcast([P, T, E]), op=ALU.add))
            for k in range(2):
                link(dve.tensor_tensor(ex3[:, :, :], chosen[:, k, :, :], rt_b[:, :, :], op=ALU.mult))
                link(dve.tensor_reduce(slot_f[:, k, :], ex3[:, :, :], axis=AX_X, op=ALU.add))
                dve.tensor_copy(slot[:, k, :], slot_f[:, k, :]).then_inc(sem("slots"), 1)
            dve.tensor_copy(blocks[:, 0:E], count[:, 2, :]).then_inc(sem("blocks"), 1)
            dve.tensor_copy(blocks[:, E:2 * E], count[:, 3, :]).then_inc(sem("blocks"), 1)

        hT = s_sb[0][:, 0, :, :].rearrange("p j k -> p (j k)")[:, 0:FC * P].rearrange("p (f n) -> p f n", f=FC)
        gathered = s_sb[1]
        SEEDS = {"result_ready": 1, "result_stored": 16}

        def expert_loop(eng, each_block, at_expert=None, after_expert=None):
            eng.wait_ge(sem("blocks"), 2)

            def expert(r, i):
                if at_expert:
                    at_expert(eng, r, i)
                n = eng.value_load(blocks[0:1, bass.ds(r * 2 + i, 1)], min_val=1, max_val=T)
                first = eng.value_load(blocks[0:1, bass.ds(r * 2 + (E + i), 1)], min_val=0, max_val=MAX_BLOCKS - 1)
                with eng.Fori(0, n) as j:
                    each_block(eng, first + j, i)

            with eng.Fori(0, E // 2 - 1) as r:
                for i in range(2):
                    expert(r, i)
                    if after_expert:
                        after_expert(eng, r * 2 + (i + 2), i)
            for i in range(2):
                expert(E // 2 - 1, i)

        def pe_turn():
            return transposed(bank[3], xe)

        def pe_expert_weights(pe, r, i):
            pe.wait_ge(sem(f"w_exp{i}"), r * 32 + 32)
            parted(pe)

        def pe_block(pe, g, i):
            pe.wait_ge(sem("rows_turned"), g + 1)
            for f in range(FC):
                for kk in range(KC):
                    last = mm(bank[f // 4][:, (f % 4) * P:(f % 4 + 1) * P], wup[i][:, kk, f * P:(f + 1) * P], xeT[:, kk, :],
                              start=(kk == 0), stop=(kk == KC - 1))
                if f % 4 == 3:
                    last.then_inc(sem("up"), 1)
            pe.wait_ge(sem("rows_in"), g * 16 + 32)
            pe_turn().then_inc(sem("turned"), 1)
            pe.wait_ge(sem("result_ready"), g + SEEDS["result_ready"])
            for f in range(FC):
                if f % 4 == 0:
                    pe.wait_ge(sem("hidden"), g * 2 + (f // 4 + 1))
                last = mm(bank[2][:, 0:D], hT[:, f, :], wdn[i][:, f, :], start=(f == 0), stop=(f == FC - 1))
            last.then_inc(sem("down"), 1)

        def act_block(act, g, i):
            for h in range(2):
                act.wait_ge(sem("up"), g * 2 + (h + 1))
                act.activation(flat(hT[:, 4 * h:4 * h + 4, :]), bank[h][:, :], ACT.Gelu).then_inc(sem("hidden"), 1)

        def dve_turned(dve, g):
            dve.wait_ge(sem("turned"), g + 1)
            dve.tensor_copy(flat(xeT[:, :, :]), bank[3][:, 0:D]).then_inc(sem("rows_turned"), 1)

        def dve_block(dve, g, i):
            dve_turned(dve, g + 1)
            dve.wait_ge(sem("down"), g + 1)
            dve.wait_ge(sem("result_stored"), g * 16 + SEEDS["result_stored"])
            dve.tensor_copy(ye[:, :], bank[2][:, 0:D]).then_inc(sem("result_ready"), 1)

        def sp_rows(sp, g):
            sp.dma_start(xe[:, :], lists_d[bass.ds(g, 1), :, :].rearrange("t p d -> p (t d)")).then_inc(sem("rows_in"), 16)

        def sp_block(sp, g, i):
            sp.wait_ge(sem("turned"), g + 2)
            parted(sp)
            sp_rows(sp, g + 2)
            sp.wait_ge(sem("result_ready"), g + (1 + SEEDS["result_ready"]))
            parted(sp)
            sp.dma_start(results_d[bass.ds(g, 1), :, :].rearrange("t p d -> p (t d)"), ye[:, :]).then_inc(sem("result_stored"), 16)

        def weights_of(sp, e, i):
            sp.dma_start(wup[i][:, :, :], up_d[:, :, bass.ds(e, 1), :].rearrange("p c e f -> p c (e f)")).then_inc(sem(f"w_exp{i}"), 16)
            sp.dma_start(wdn[i][:, :, :], dn_d[:, :, bass.ds(e, 1), :].rearrange("p c e d -> p c (e d)")).then_inc(sem(f"w_exp{i}"), 16)

        def sp_experts(sp):
            sp.wait_ge(sem("scattered"), 16 * 2 * T)
            sp.wait_ge(sem("results_zeroed"), 16)
            sp_rows(sp, 0)
            sp.wait_ge(sem("turned"), 1)
            sp_rows(sp, 1)
            expert_loop(sp, sp_block, after_expert=weights_of)
            total = sp.value_load(blocks[0:1, E - 1:E], min_val=1, max_val=T) + \
                sp.value_load(blocks[0:1, 2 * E - 1:2 * E], min_val=0, max_val=MAX_BLOCKS - 1)
            sp.wait_ge(sem("result_stored"), total * 16 + SEEDS["result_stored"])
            parted(sp)
            sp.wait_ge(sem("rows_in"), total * 16 + 32)
            parted(sp)
            sp.sem_inc(sem("results_stored"), 1)
            for t in range(T):
                sp.wait_ge(sem(f"added{t}"), 2)
                sp.dma_start(out_d[:, t, :], x_all[:, t * D:(t + 1) * D]).then_inc(sem("out"), 16)
            sp.wait_ge(sem("out"), 16 * T)

        def pe_rank(pe):
            for i in range(4):
                pe.wait_ge(sem(f"bank{i}_free"), len(FILLS[i]) * T)
            pe.wait_ge(sem("route_step"), SELECTED)
            for s in range(T):
                mm(bank[0][:, s * E:T * E], ones[:, :] if s else earlier[:, :], selected[:, 0:(T - s) * E],
                   start=(s == 0), stop=(s == T - 1))
            mm(bank[1][:, 0:T * E], ones[:, :], selected[:, :], start=True, stop=True).then_inc(sem("ranked"), 1)

        def pool_scatter(pool):
            pool.wait_ge(sem("lists_zeroed"), 16)
            pool.wait_ge(*due("x3_kept", T - 1))
            for k in range(2):
                pool.wait_ge(sem("slots"), k + 1)
                for t in range(T):
                    pool.indirect_dma_start(out=lists, out_offset=bass.IndirectOffsetOnAxis(ap=slot[:, k, t:t + 1], axis=0),
                                            in_=x3_all[:, t, :], in_offset=None).then_inc(sem("scattered"), 16)

        def pool_gather(pool):
            pool.wait_ge(sem("results_stored"), 1)
            for t in range(T):
                for k in range(2):
                    pool.indirect_dma_start(out=gathered[:, k, t, :], out_offset=None, in_=results,
                                            in_offset=bass.IndirectOffsetOnAxis(ap=slot[:, k, t:t + 1], axis=0)).then_inc(sem(f"gathered{t}"), 16)

        def dve_combine(dve):
            def add(t, k):
                acc = x_all[:, t * D:(t + 1) * D]
                if k == 0:
                    dve.wait_ge(sem(f"gathered{t}"), 32)
                else:
                    dve.wait_ge(sem(f"added{t}"), 1)
                dve.scalar_tensor_tensor(out=acc, in0=gathered[:, k, t, :], scalar=rt_r[:, 3 + 2 * k, t:t + 1], in1=acc,
                                         op0=ALU.mult, op1=ALU.add).then_inc(sem(f"added{t}"), 1)
            for t in range(T + 1):
                if t < T:
                    add(t, 0)
                if t:
                    add(t - 1, 1)

        def weights_arrived(eng):
            eng.wait_ge(sem("w_q"), 16 * len(loads_q))
            eng.wait_ge(sem("w_kv"), 16 * len(loads_kv))

        @block.sync
        def _(sp):
            sp_front(sp, 0, 0)
            for dst, src in loads_q:
                sp.dma_start(whole(dst), src).then_inc(sem("w_q"), 16)
            for dst, src in loads_kv:
                sp.dma_start(whole(dst), src).then_inc(sem("w_kv"), 16)
            sp_front(sp, 0, 1)
            for dst, src in loads_back:
                sp.dma_start(whole(dst), src).then_inc(sem("w_back"), 16)
            for e in range(2):
                sp.dma_start(wup[e][:, :, :], up_d[:, :, e, :]).then_inc(sem(f"w_exp{e}"), 16)
                sp.dma_start(wdn[e][:, :, :], dn_d[:, :, e, :]).then_inc(sem(f"w_exp{e}"), 16)
            with sp.Fori(1, T // 2) as n:
                for i in range(2):
                    sp_front(sp, n, i)
            sp.wait_ge(sem("zeros"), 1)
            sp.dma_start(lists.rearrange("(n p) d -> p n d", p=P)[:, 0:MAX_BLOCKS + 2, :],
                         zeros[:, :].unsqueeze(1).to_broadcast([P, MAX_BLOCKS + 2, D])).then_inc(sem("lists_zeroed"), 16)
            sp.dma_start(results.rearrange("(n p) d -> p n d", p=P),
                         zeros[:, :].unsqueeze(1).to_broadcast([P, reach, D])).then_inc(sem("results_zeroed"), 16)
            sp_experts(sp)

        @block.tensor
        def _(pe):
            weights_arrived(pe)
            passes(pe, pe_pass)
            pe_rank(pe)
            pe.wait_ge(sem("rows_in"), 16)
            pe_turn().then_inc(sem("turned"), 1)
            expert_loop(pe, pe_block, at_expert=pe_expert_weights)

        @block.scalar
        def _(act):
            weights_arrived(act)
            passes(act, act_pass)
            act.wait_ge(sem("logits_shifted"), 1)
            act.activation(flat(ex3[:, :, :]), flat(rt_a[:, :, :]), ACT.Exp).then_inc(sem("router_exp"), 1)
            expert_loop(act, act_block)

        @block.vector
        def _(dve):
            dve.memset(zeros[:, :], 0.0).then_inc(sem("zeros"), 1)
            weights_arrived(dve)
            dve.wait_ge(sem("zeros"), 1)
            dve.wait_ge(sem("zeroed"), ZEROED)
            passes(dve, dve_pass)
            dve.wait_ge(*due("x_kept", T - 1))
            dve_route(dve)
            dve.sem_inc(sem("result_ready"), SEEDS["result_ready"])
            dve.sem_inc(sem("result_stored"), SEEDS["result_stored"])
            dve_turned(dve, 0)
            expert_loop(dve, dve_block)
            dve_combine(dve)

        @block.gpsimd
        def _(pool):
            for dst, value in ((nhalf, -0.5), (phalf, 0.5), (vz[0], 0.0), (vz[1], 0.0), (vz2, 0.0), (ones, 1.0)):
                pool.memset(whole(dst), value).then_inc(sem("zeroed"), 1)
            pool.wait_ge(sem("zeroed"), ZEROED)
            weights_arrived(pool)
            passes(pool, pool_pass)
            pool_scatter(pool)
            pool_gather(pool)


INPUTS = ["x", "ctxT", "wq", "wk", "wv", "wo", "wqkv", "wproj", "wlat", "wr", "bqk", "bqkv", "blatk",
          "bv", "bo", "blatv", "bproj", "br", "ident", "parity", "wbias", "order8", "earlier", "steps", "before8", "upT", "downT"]


def layouts(i):
    def c(x):
        return np.ascontiguousarray(x)

    def column(b):
        return c(b.reshape(-1, P).T)

    def rows(b):
        return c(np.broadcast_to(b.reshape(1, -1), (P, b.size)))

    heads = P // HD
    wlat = np.zeros((heads, HD, heads, HD), np.float32)
    for h in range(heads):
        wlat[h, :, h, :] = i["L0_attn_W_lat"].T
    p = np.arange(P)
    parity = np.where((p[:, None] // HD) % 2 == np.arange(2)[None, :], SCALE, 0.0).astype(np.float32)
    count = np.zeros((L, L))
    for q in range(L):
        win = list(range(max(0, q - 3), min(L, q + 4)))
        win += [L - 1 if q < 3 else 0] * (7 - len(win))
        for k in win:
            count[q, k] += 1
    wbias = np.full((L, L), MASKED, np.float32)
    wbias[count > 0] = np.log(count[count > 0])
    return {
        "x": i["x"].reshape(B * L, D), "ctxT": c(i["ctx_1024"].reshape(B * LC, D).T),
        "wq": i["L0_xattn_Wq"], "wk": i["L0_xattn_Wk"], "wv": i["L0_xattn_Wv"], "wo": i["L0_xattn_Wo"],
        "wqkv": c(i["L0_attn_W_qkv"].T), "wproj": c(i["L0_attn_W_proj"].T), "wlat": wlat.reshape(P, P),
        "wr": i["L0_ffn_router_w"],
        "bqk": column(np.concatenate([i["L0_xattn_bq"], i["L0_xattn_bk"]])), "bqkv": column(i["L0_attn_b_qkv"]),
        "blatk": c(np.tile(i["L0_attn_b_lat"], heads).reshape(P, 1)),
        "bv": rows(i["L0_xattn_bv"]), "bo": rows(i["L0_xattn_bo"]), "blatv": rows(np.tile(i["L0_attn_b_lat"], H)),
        "bproj": rows(i["L0_attn_b_proj"]), "br": rows(i["L0_ffn_router_b"]),
        "ident": np.eye(P, dtype=np.float32), "parity": parity, "wbias": c(np.tile(wbias, (2, 1))),
        "order8": np.tile(np.arange(E, 0, -1, dtype=np.float32), (P, 1)),
        "earlier": np.triu(np.ones((P, P), np.float32), 1),
        "steps": np.tile(P * np.arange(1, T, dtype=np.float32), (P, 1)),
        "before8": c(np.broadcast_to(np.tril(np.ones((E, E), np.float32), -1), (P, E, E))),
        "upT": c(i["L0_ffn_expert_up"].transpose(0, 2, 1)), "downT": c(i["L0_ffn_expert_down"].transpose(0, 2, 1)),
    }


def kernel(**inputs):
    import concourse.bacc as bacc
    from concourse.bass_utils import run_bass_kernel_spmd

    arrays = layouts({k: np.asarray(v) for k, v in inputs.items()})
    nc = bacc.Bacc("TRN2", target_bir_lowering=False, num_devices=1)
    aps = {n: nc.dram_tensor(f"in_{n}", arrays[n].shape, F32, kind="ExternalInput").ap() for n in INPUTS}
    out = nc.dram_tensor("out", (B * L, D), F32, kind="ExternalOutput").ap()
    program(nc, aps, out)
    got = run_bass_kernel_spmd(nc, [{f"in_{n}": arrays[n] for n in INPUTS}], core_ids=[0])
    return got.results[0]["out"].reshape(B, L, D)
```

```python
from contextlib import ExitStack

import numpy as np

import concourse.bass as bass
from concourse import mybir

F32 = mybir.dt.float32
BF16 = mybir.dt.bfloat16
U32 = mybir.dt.uint32
ALU = mybir.AluOpType
ACT = mybir.ActivationFunctionType
AX_X = mybir.AxisListType.X

P = 128
B, L, D = 16, 64, 256
LC = 256
H = 16
HD = D // H
T = B * L // P
BT = P // L
KC = D // P
G = 4
NJ = KC * G
E, DFF = 8, 1024
FC = DFF // P
EPS = 1e-5
SCALE = HD ** -0.5
MASKED = -1e30
EVALS = 5
ND = 5
MAX_BLOCKS = 2 * B * L // P + E - 1
NEWTON = 24
OFF_BY = 1e-6
C3 = 2.0

PASS = [
    ("B", "clip0"), ("M", "sums00"), ("C", "turn2"), ("M", "sums01"), ("M", "update0"), ("C", "attend2"),
    ("B", "clip1"), ("B", "weights0"), ("M", "sums10"), ("B", "weights1"), ("F", "stats"), ("C", "proj"),
    ("M", "sums11"), ("B", "attend"), ("F", "norm"), ("M", "update1"), ("M", "sums20"), ("F", "queries"),
    ("B", "out"), ("C", "norm3"), ("F", "keys"), ("B", "norm2"), ("M", "sums21"), ("M", "update2"),
    ("F", "scores0"), ("C", "router"), ("B", "qkv"), ("F", "xb"), ("M", "sums30"), ("F", "scores1"),
    ("M", "sums31"), ("B", "latent"), ("C", "logits"), ("F", "scores2"), ("F", "scores3"), ("M", "update3"),
    ("M", "sums40"), ("F", "start0"), ("B", "windows"), ("F", "start1"), ("M", "sums41"), ("B", "exp2"),
    ("B", "sum2"), ("M", "update4"), ("F", "v0"), ("M", "general"), ("F", "v1"),
]
LAG = {"F": 0, "M": 1, "B": 2, "C": 3}

BANKS = {
    "norm": {"xnT": 0}, "queries": {"q": 1}, "keys": {"k0": 2, "k1": 3}, "v0": {"v0": 2}, "v1": {"v1": 1},
    "scores0": {"s0": 0, "s1": 1}, "scores1": {"s2": 2, "s3": 3}, "scores2": {"s4": 0, "s5": 1},
    "scores3": {"s6": 2, "s7": 3}, "weights0": {"t0": 4, "t1": 5, "t2": 6, "t3": 7},
    "weights1": {"t4": 4, "t5": 5, "t6": 6, "t7": 7}, "attend": {"av": 4}, "out": {"wo": 5},
    "norm2": {"x2T": 6}, "qkv": {"qk": 7, "v": 4}, "latent": {"kl": 5, "vl": 6},
    "windows": {"l0": 7, "l1": 4, "l2": 5, "l3": 6}, "turn2": {"u0": 4, "u1": 5, "u2": 6, "u3": 7},
    "attend2": {"av2": 6}, "proj": {"pr": 6}, "router": {"x3T": 5}, "logits": {"rt": 4},
}
FILLS = {bank: [(stage, name) for stage, step in PASS for name, at in BANKS.get(step, {}).items() if at == bank] for bank in range(8)}
WHERE = {name: (bank, k, stage) for bank, fills in FILLS.items() for k, (stage, name) in enumerate(fills)}


def fills_till(name, t):
    bank, k, stage = WHERE[name]
    ahead = [LAG[stage] - LAG[other] + (i <= k) for i, (other, _) in enumerate(FILLS[bank])]
    if isinstance(t, int):
        return sum(min(max(t + x, 0), T) for x in ahead)
    return len(ahead) * t + sum(ahead)


STARTS = 4
LEVELS = [2] + [7] * (EVALS - 1)


def level(it, k):
    return sum(LEVELS[:it]) + k + 1


PER = {"update_step": sum(LEVELS), "start_step": 2 * STARTS, "stats": 2, "clip": 2,
       "sum_act": 2 * EVALS, "sum_dve": 2 * EVALS, "off_step": 4}
ZEROED = 6
PARTS = [(0, T - 1), (T - 1, T)]
EARLY = 8
A0, A1, A2 = -0.0272, 1.527, 1.368
G0, G1 = 0.00693, 0.4176


def program(nc, a, out):
    with ExitStack() as ctx:
        def sb(name, shape, dt=F32):
            return ctx.enter_context(nc.sbuf_tensor(name, shape, dt))

        sems = {}

        def sem(name):
            if name not in sems:
                sems[name] = ctx.enter_context(nc.semaphore(name))
            return sems[name]

        def due(name, t, k=1):
            return sem(name), PER.get(name, 1) * t + k

        bank = [ctx.enter_context(nc.psum_tensor(f"bank{i}", [P, 512], F32)) for i in range(8)]

        def ps(name):
            return bank[WHERE[name][0]]

        def full(name, t):
            return sem(f"bank{WHERE[name][0]}_full"), fills_till(name, t)

        def filled(name):
            return sem(f"bank{WHERE[name][0]}_full"), 1

        def emptied(name):
            return sem(f"bank{WHERE[name][0]}_free"), 1

        def read_out(name, t):
            return sem(f"bank{WHERE[name][0]}_free"), fills_till(name, t)

        def wait_free(pe, name, t):
            before = fills_till(name, t) - 1
            if not (isinstance(before, int) and before == 0):
                pe.wait_ge(sem(f"bank{WHERE[name][0]}_free"), before)

        wq = sb("wq", [P, KC, D])
        wk = sb("wk", [P, KC, D])
        wv = sb("wv", [P, KC, D])
        wo = sb("wo", [P, KC, D])
        wqkv = sb("wqkv", [P, KC, 3 * D])
        wproj = sb("wproj", [P, KC, D])
        wlat = sb("wlat", [P, P])
        wr = sb("wr", [P, KC, E])
        bqk = sb("bqk", [P, 2 * KC])
        bqkv = sb("bqkv", [P, 3 * KC])
        blatk = sb("blatk", [P, 1])
        bvr = sb("bvr", [P, D])
        bor = sb("bor", [P, D])
        blatv = sb("blatv", [P, D])
        bpr = sb("bpr", [P, D])
        brr = sb("brr", [P, E])
        ident = sb("ident", [P, P])
        parity = sb("parity", [P, 2])
        wbias = sb("wbias", [P, L])
        order8 = sb("order8", [P, E])
        nhalf = sb("nhalf", [P, 1])
        phalf = sb("phalf", [P, NJ])
        zeros = sb("zeros", [P, LC])
        xin = [sb(f"xin{i}", [P, D]) for i in range(2)]
        xb = [sb(f"xb{i}", [P, D]) for i in range(2)]
        ctxT = [sb(f"ctxT{i}", [P, KC, BT * LC]) for i in range(2)]
        xn1 = sb("xn1", [P, D])
        xn1T = sb("xn1T", [P, KC, P])
        q_bd = sb("q_bd", [P, KC, BT, 2, L])
        kT = sb("kT", [P, KC, BT * LC])
        vz = [sb(f"vz{i}", [P, 2 * BT, 2, D]) for i in range(2)]
        s_sb = [sb(f"scores{i}", [P, BT, NJ, LC]) for i in range(2)]
        ln = [{n: sb(f"{n}{i}", [P, w]) for n, w in (("st", 6), ("mv", 2), ("ve", 1), ("rstd", 1))}
              for i in range(3)]
        st = [sb(f"st_scores{i}", [P, BT, NJ, 6]) for i in range(2)]
        guess = sb("guess", [P, BT, 7, NJ])
        reach0 = sb("reach0", [P, BT, NJ])
        u_it = sb("u_it", [P, EVALS + 1, BT, NJ])
        f_it = sb("f_it", [P, EVALS, BT, NJ])
        phi = sb("phi", [P, EVALS, BT, NJ])
        tmp = sb("tmp", [P, 10, BT * NJ])
        junk = sb("junk", [P, BT, NJ, LC], BF16)
        off = sb("off", [P, 1])
        off16 = sb("off16", [P, BT * NJ])
        off16b = sb("off16b", [P, BT * NJ])
        offmax = sb("offmax", [P, 1])
        flag = sb("flag", [P, 1], U32)
        aT = sb("aT", [P, BT * G, KC, 2, P])
        oT = sb("oT", [P, KC, P])
        x1 = sb("x1", [P, D])
        x1b = sb("x1b", [P, D])
        xn2 = sb("xn2", [P, D])
        xn2T = sb("xn2T", [P, KC, P])
        q2 = sb("q2", [P, KC, BT, 2, L])
        k2T = sb("k2T", [P, KC, P])
        v2T = sb("v2T", [P, KC, P])
        klT = sb("klT", [P, KC, P])
        vz2 = sb("vz2", [L, BT, 2, D])
        a2 = sb("a2", [P, G, BT * KC, L])
        mx2 = sb("mx2", [P, G, BT * KC])
        e2 = sb("e2", [P, G, BT * KC, L])
        sm2 = sb("sm2", [P, G, BT * KC])
        rs2 = sb("rs2", [P, G, BT * KC])
        a2T = sb("a2T", [L, G, BT * KC, P])
        o2T = sb("o2T", [P, KC, P])
        x2 = sb("x2", [P, D])
        xn3 = sb("xn3", [P, D])
        xn3T = sb("xn3T", [P, KC, P])
        logits = sb("logits", [P, T, E])
        ex3 = sb("ex3", [P, T, E])
        probs = sb("probs", [P, T, E])
        rt_a = sb("rt_a", [P, T, E])
        rt_b = sb("rt_b", [P, T, E])
        chosen = sb("chosen", [P, 2, T, E])
        rt_r = sb("rt_r", [P, 8, T])
        x_all = sb("x_all", [P, T * D])
        x3_all = sb("x3_all", [P, T, D])
        selected = sb("selected", [P, T * E])
        earlier = sb("earlier", [P, P])
        ones = sb("ones", [P, P])
        steps = sb("steps", [P, T - 1])
        home = sb("home", [P, 2, E])
        before8 = sb("before8", [P, E, E])
        count = sb("count", [P, 8, E])
        over = sb("over", [P, E, T - 1])
        summed = sb("summed", [P, E, E])
        blocks = sb("blocks", [P, 2 * E], U32)
        slot_f = sb("slot_f", [P, 2, T])
        place = sb("place", [P, T, E])
        list_slot = sb("list_slot", [P, 2, T], U32)
        slot = sb("slot", [P, 2, T], U32)
        xe, xeT, ye = xn1, xn1T, xn2
        reach = MAX_BLOCKS + T
        lists = nc.dram_tensor("lists", (E * T * P, D), F32).ap()
        results = nc.dram_tensor("results", (reach * P, D), F32).ap()
        wup = [sb(f"wup{i}", [P, KC, DFF]) for i in range(2)]
        wdn = [sb(f"wdn{i}", [P, FC, D]) for i in range(2)]

        x_d = a["x"].rearrange("(t p) d -> t p d", p=P)
        c_d = a["ctxT"].rearrange("(c p) n -> p c n", p=P)
        lists_d = lists.rearrange("(n p) d -> n p d", p=P)
        results_d = results.rearrange("(n p) d -> n p d", p=P)
        out_d = out.rearrange("(t p) d -> p t d", p=P)
        up_d = a["upT"].rearrange("e (c p) f -> p c e f", p=P)
        dn_d = a["downT"].rearrange("e (c p) d -> p c e d", p=P)

        def w_d(name):
            return a[name].rearrange("(c p) n -> p c n", p=P)

        loads_q = [(wq, w_d("wq")), (bqk, a["bqk"]), (parity, a["parity"]), (ident, a["ident"]), (bor, a["bo"])]
        loads_kv = [(wk, w_d("wk")), (wv, w_d("wv")), (bvr, a["bv"])]
        loads_back = [(wo, w_d("wo")), (wqkv, w_d("wqkv")), (wproj, w_d("wproj")), (wlat, a["wlat"]),
                      (wr, w_d("wr")), (bqkv, a["bqkv"]), (blatk, a["blatk"]), (blatv, a["blatv"]),
                      (bpr, a["bproj"]), (brr, a["br"]), (wbias, a["wbias"]), (order8, a["order8"]),
                      (earlier, a["earlier"]), (steps, a["steps"]), (before8, a["before8"]),
                      (home[:, 0, :], a["home"])]

        block = ctx.enter_context(nc.Block())

        def whole(x):
            return x[tuple(slice(None) for _ in x.shape)]

        def sp_front(sp, n, i):
            t = 2 * n + i
            if not (isinstance(n, int) and n == 0):
                sp.wait_ge(*due("xb", t - 2))
                sp.wait_ge(*due("xn1", t - 2))
                sp.wait_ge(*full("v1", t - 2))
            sp.dma_start(xin[i][:, :], x_d[bass.ds(t, 1), :, :].rearrange("t p d -> p (t d)")).then_inc(sem(f"x_in{i}"), 16)
            sp.dma_start(ctxT[i][:, :, :], c_d[:, :, bass.ds(t * (BT * LC), BT * LC)]).then_inc(sem(f"ctx_in{i}"), 16)

        def ln_stats(dve, n, x, t):
            dve.bn_stats(out=ln[n]["st"][:, :], in_=x).then_inc(sem(f"ln{n}_stats"), 1)
            dve.wait_ge(*due(f"ln{n}_stats", t))
            parted(dve)
            dve.bn_aggr(out=ln[n]["mv"][:, :], in_=ln[n]["st"][:, :]).then_inc(sem(f"ln{n}_mean"), 1)

        def ln_rstd(pool, n, t):
            pool.wait_ge(*due(f"ln{n}_mean", t))
            parted(pool)
            pool.tensor_scalar(ln[n]["ve"][:, :], ln[n]["mv"][:, 1:2], EPS, 1.0, ALU.add, ALU.mult).then_inc(sem(f"ln{n}_var"), 1)
            pool.wait_ge(*due(f"ln{n}_var", t))
            pool.tensor_tensor(ln[n]["rstd"][:, :], ln[n]["ve"][:, :], nhalf[:, :], op=ALU.pow).then_inc(sem(f"ln{n}_rstd"), 1)

        def ln_apply(dve, n, y, x, t, done):
            dve.wait_ge(*due(f"ln{n}_rstd", t))
            dve.tensor_scalar(y, x, ln[n]["mv"][:, 0:1], ln[n]["rstd"][:, :], ALU.subtract, ALU.mult).then_inc(sem(done), 1)

        def after_first(t):
            return not (isinstance(t, int) and t == 0)

        mm = nc.tensor.matmul

        def transposed(dst, src):
            for c in range(KC):
                last = nc.tensor.transpose(dst[:, c * P:(c + 1) * P], src[:, c * P:(c + 1) * P], ident[:, :])
            return last

        def times(dst, xT, w, width=D):
            for c in range(KC):
                last = mm(dst[:, 0:width], xT[:, c, :], w[:, c, :], start=(c == 0), stop=(c == KC - 1))
            return last

        def parted(eng):
            eng.sem_inc(sem(f"parted_{eng.engine.name}"), 1)

        def pe_front(pe, step, t, n, i):
            if step == "norm":
                pe.wait_ge(*due("xn1", t))
                wait_free(pe, "xnT", t)
                transposed(ps("xnT"), xn1).then_inc(*filled("xnT"))
            if step == "queries":
                pe.wait_ge(*read_out("xnT", t))
                wait_free(pe, "q", t)
                for c in range(KC):
                    for kk in range(KC):
                        last = mm(ps("q")[:, c * P:(c + 1) * P], wq[:, kk, c * P:(c + 1) * P], xn1T[:, kk, :],
                                  start=(kk == 0), stop=(kk == KC - 1))
                last.then_inc(*filled("q"))
            if step == "keys":
                pe.wait_ge(sem(f"ctx_in{i}"), n * 16 + 16)
                for c in range(KC):
                    wait_free(pe, f"k{c}", t)
                    for kk in range(KC):
                        last = mm(ps(f"k{c}")[:, :], wk[:, kk, c * P:(c + 1) * P], ctxT[i][:, kk, :],
                                  start=(kk == 0), stop=(kk == KC - 1))
                    last.then_inc(*filled(f"k{c}"))
            if step in ("v0", "v1"):
                b = int(step[-1])
                wait_free(pe, step, t)
                for j in range(2):
                    m = (2 * b + j) * P
                    for kk in range(KC):
                        last = mm(ps(step)[:, j * D:(j + 1) * D], ctxT[i][:, kk, m:m + P], wv[:, kk, :],
                                  start=(kk == 0), stop=(kk == KC - 1))
                last.then_inc(*filled(step))
            if step.startswith("scores"):
                half = int(step[-1])
                if half == 0:
                    pe.wait_ge(*read_out("q", t))
                    pe.wait_ge(*read_out("k0", t))
                    pe.wait_ge(*read_out("k1", t))
                for m in (2 * half, 2 * half + 1):
                    b, g = divmod(m, G)
                    wait_free(pe, f"s{m}", t)
                    for c in range(KC):
                        last = mm(ps(f"s{m}")[:, c * LC:(c + 1) * LC],
                                  q_bd[32 * g:32 * g + 32, c, b, :, :].rearrange("p h q -> p (h q)"),
                                  kT[32 * g:32 * g + 32, c, b * LC:(b + 1) * LC], start=True, stop=True)
                    last.then_inc(*filled(f"s{m}"))

        def pe_back(pe, step, t, i):
            if step in ("weights0", "weights1"):
                b = int(step[-1])
                pe.wait_ge(*due("clip", t, b + 1))
                for g in range(G):
                    m = b * G + g
                    wait_free(pe, f"t{m}", t)
                    for c in range(KC):
                        for kk in range(2):
                            n = (c * 2 + kk) * P
                            last = nc.tensor.transpose(ps(f"t{m}")[:, n:n + P],
                                                       s_sb[i][:, b, 2 * g + c, kk * P:(kk + 1) * P], ident[:, :])
                    last.then_inc(*filled(f"t{m}"))
            if step == "attend":
                for m in range(G, 2 * G):
                    pe.wait_ge(*read_out(f"t{m}", t))
                wait_free(pe, "av", t)
                for b in range(BT):
                    for c in range(KC):
                        for g in range(G):
                            for par in range(2):
                                for kk in range(2):
                                    last = mm(ps("av")[32 * g:32 * g + 32, c * P + b * L:c * P + (b + 1) * L],
                                              vz[i][:, 2 * b + kk, par, c * P + 32 * g:c * P + 32 * g + 32],
                                              aT[:, b * G + g, c, kk, par * L:(par + 1) * L],
                                              start=(par + kk == 0), stop=(par + kk == 2))
                last.then_inc(*filled("av"))
            if step == "out":
                pe.wait_ge(*read_out("av", t))
                wait_free(pe, "wo", t)
                times(ps("wo"), oT, wo).then_inc(*filled("wo"))
            if step == "norm2":
                pe.wait_ge(*due("xn2", t))
                wait_free(pe, "x2T", t)
                transposed(ps("x2T"), xn2).then_inc(*filled("x2T"))
            if step == "qkv":
                pe.wait_ge(*read_out("x2T", t))
                for f, first, count in (("qk", 0, 2 * KC), ("v", 2 * KC, KC)):
                    wait_free(pe, f, t)
                    for n in range(count):
                        for kk in range(KC):
                            last = mm(ps(f)[:, n * P:(n + 1) * P], wqkv[:, kk, (first + n) * P:(first + n + 1) * P],
                                      xn2T[:, kk, :], start=(kk == 0), stop=(kk == KC - 1))
                    last.then_inc(*filled(f))
            if step == "latent":
                pe.wait_ge(*read_out("qk", t))
                wait_free(pe, "kl", t)
                mm(ps("kl")[:, 0:D], wlat[:, :], k2T[:, :, :].rearrange("p c n -> p (c n)"),
                   start=True, stop=True).then_inc(*filled("kl"))
                pe.wait_ge(*read_out("v", t))
                wait_free(pe, "vl", t)
                for b in range(BT):
                    for c in range(KC):
                        n = b * D + c * P
                        last = mm(ps("vl")[0:L, n:n + P], v2T[:, c, b * L:(b + 1) * L], wlat[:, :], start=True, stop=True)
                last.then_inc(*filled("vl"))
            if step == "windows":
                pe.wait_ge(*read_out("qk", t))
                pe.wait_ge(*read_out("kl", t))
                for g in range(G):
                    wait_free(pe, f"l{g}", t)
                    for b in range(BT):
                        for c in range(KC):
                            n = (b * KC + c) * L
                            last = mm(ps(f"l{g}")[:, n:n + L],
                                      q2[32 * g:32 * g + 32, c, b, :, :].rearrange("p h q -> p (h q)"),
                                      klT[32 * g:32 * g + 32, c, b * L:(b + 1) * L], start=True, stop=True)
                    last.then_inc(*filled(f"l{g}"))
            if step == "turn2":
                pe.wait_ge(*due("weights2", t))
                parted(pe)
                for g in range(G):
                    wait_free(pe, f"u{g}", t)
                    parted(pe)
                    for n in range(BT * KC):
                        last = nc.tensor.transpose(ps(f"u{g}")[0:L, n * P:(n + 1) * P], a2[:, g, n, :], ident[:, :])
                    last.then_inc(*filled(f"u{g}"))
            if step == "attend2":
                pe.wait_ge(*read_out("vl", t))
                parted(pe)
                for g in range(G):
                    pe.wait_ge(*read_out(f"u{g}", t))
                parted(pe)
                wait_free(pe, "av2", t)
                parted(pe)
                for b in range(BT):
                    for c in range(KC):
                        for g in range(G):
                            for par in range(2):
                                last = mm(ps("av2")[32 * g:32 * g + 32, c * P + b * L:c * P + (b + 1) * L],
                                          vz2[:, b, par, c * P + 32 * g:c * P + 32 * g + 32],
                                          a2T[:, g, b * KC + c, par * L:(par + 1) * L],
                                          start=(par == 0), stop=(par == 1))
                last.then_inc(*filled("av2"))
            if step == "proj":
                pe.wait_ge(*read_out("av2", t))
                wait_free(pe, "pr", t)
                times(ps("pr"), o2T, wproj).then_inc(*filled("pr"))
            if step == "router":
                pe.wait_ge(*due("xn3", t))
                wait_free(pe, "x3T", t)
                transposed(ps("x3T"), xn3).then_inc(*filled("x3T"))
            if step == "logits":
                pe.wait_ge(*read_out("x3T", t))
                wait_free(pe, "rt", t)
                times(ps("rt"), xn3T, wr, E).then_inc(*filled("rt"))

        def flat(x):
            return x.rearrange("p a b -> p (a b)")

        def flat3(x):
            return x.rearrange("p a b c -> p (a b c)")

        def act_front(act, step, t, i):
            if step == "norm":
                act.wait_ge(*full("xnT", t))
                if after_first(t):
                    act.wait_ge(*full("q", t - 1))
                act.activation(flat(xn1T[:, :, :]), ps("xnT")[:, 0:D], ACT.Copy).then_inc(*emptied("xnT"))
            if step == "keys":
                for c in range(KC):
                    act.wait_ge(*full(f"k{c}", t))
                    if c == 0 and after_first(t):
                        for f in ("s4", "s5", "s6", "s7"):
                            act.wait_ge(*full(f, t - 1))
                    act.activation(kT[:, c, :], ps(f"k{c}")[:, :], ACT.Identity, bias=bqk[:, KC + c:KC + c + 1]).then_inc(*emptied(f"k{c}"))
            if step.startswith("scores"):
                for m in (2 * int(step[-1]), 2 * int(step[-1]) + 1):
                    b, g = divmod(m, G)
                    act.wait_ge(*full(f"s{m}", t))
                    act.activation(flat(s_sb[i][:, b, 2 * g:2 * g + 2, :]), ps(f"s{m}")[:, :], ACT.Copy).then_inc(*emptied(f"s{m}"))

        def act_back(act, step, t, i):
            if step in ("weights0", "weights1"):
                for m in range(G * int(step[-1]), G * int(step[-1]) + G, 2):
                    act.wait_ge(*full(f"t{m}", t))
                    if m == 0 and after_first(t):
                        act.wait_ge(*full("av", t - 1))
                    act.activation(flat3(aT[:, m, :, :, :]), ps(f"t{m}")[:, :], ACT.Copy).then_inc(*emptied(f"t{m}"))
            if step == "attend":
                act.wait_ge(*full("av", t))
                if after_first(t):
                    act.wait_ge(*full("wo", t - 1))
                act.activation(flat(oT[:, :, :]), ps("av")[:, 0:D], ACT.Copy).then_inc(*emptied("av"))
            if step == "norm2":
                act.wait_ge(*full("x2T", t))
                if after_first(t):
                    act.wait_ge(*full("v", t - 1))
                act.activation(flat(xn2T[:, :, :]), ps("x2T")[:, 0:D], ACT.Copy).then_inc(*emptied("x2T"))
            if step == "qkv":
                act.wait_ge(*full("v", t))
                if after_first(t):
                    act.wait_ge(*full("vl", t - 1))
                for c in range(KC):
                    last = act.activation(v2T[:, c, :], ps("v")[:, c * P:(c + 1) * P], ACT.Identity,
                                          bias=bqkv[:, 2 * KC + c:2 * KC + c + 1])
                last.then_inc(*emptied("v"))
            if step == "latent":
                act.wait_ge(*full("kl", t))
                if after_first(t):
                    for g in range(G):
                        act.wait_ge(*full(f"l{g}", t - 1))
                act.activation(flat(klT[:, :, :]), ps("kl")[:, 0:D], ACT.Identity, bias=blatk[:, :]).then_inc(*emptied("kl"))
            if step == "exp2":
                act.wait_ge(*due("shifted2", t))
                act.activation(flat3(e2[:, :, :, :]), flat3(e2[:, :, :, :]), ACT.Exp).then_inc(sem("exp2"), 1)
            if step == "turn2":
                for g in range(G):
                    act.wait_ge(*full(f"u{g}", t))
                    if g == 0 and after_first(t):
                        act.wait_ge(*full("av2", t - 1))
                    act.activation(flat(a2T[:, g, :, :]), ps(f"u{g}")[0:L, :], ACT.Copy).then_inc(*emptied(f"u{g}"))
            if step == "attend2":
                act.wait_ge(*full("av2", t))
                if after_first(t):
                    act.wait_ge(*full("pr", t - 1))
                act.activation(flat(o2T[:, :, :]), ps("av2")[:, 0:D], ACT.Copy).then_inc(*emptied("av2"))
            if step == "router":
                act.wait_ge(*full("x3T", t))
                if after_first(t):
                    act.wait_ge(*full("rt", t - 1))
                act.activation(flat(xn3T[:, :, :]), ps("x3T")[:, 0:D], ACT.Copy).then_inc(*emptied("x3T"))

        def act_evals(act, it, half, t, i):
            middle = (ND + BT * NJ) // 2
            if half == 0 and it == 0:
                act.wait_ge(*due("start_step", t, PER["start_step"]))
                if after_first(t):
                    act.wait_ge(*due("sum_act", t, 0))
            elif half == 0:
                act.wait_ge(*due("update_step", t, level(it - 1, LEVELS[it - 1] - 1)))
            for m in range(middle, BT * NJ) if half else range(ND, middle):
                b, j = divmod(m, NJ)
                last = act.activation(junk[:, b, j, :], s_sb[i][:, b, j, :], ACT.Relu, bias=u_it[:, it, b, j:j + 1],
                                      accum_out=f_it[:, it, b, j:j + 1])
            last.then_inc(sem("sum_act"), 1)

        def masked_queries(dve, dst, name, bias):
            for c in range(KC):
                for par in range(2):
                    last = dve.tensor_scalar(dst[:, c, :, par, :], ps(name)[:, c * P:(c + 1) * P].rearrange("p (b q) -> p b q", b=BT),
                                             bias[:, c:c + 1], parity[:, par:par + 1], ALU.add, ALU.mult)
            return last

        def heads_of(x, par):
            return x.rearrange("p (h two d) -> p h two d", two=2, d=HD)[:, :, par, :]

        def dve_front(dve, step, t, n, i):
            if step == "stats":
                dve.wait_ge(sem(f"x_in{i}"), n * 16 + 16)
                ln_stats(dve, 0, xin[i][:, :], t)
            if step in ("start0", "start1"):
                dve_stats(dve, int(step[-1]), t, i)
            if step == "norm":
                if after_first(t):
                    dve.wait_ge(*full("xnT", t - 1))
                ln_apply(dve, 0, xn1[:, :], xin[i][:, :], t, "xn1")
            if step == "queries":
                dve.wait_ge(*full("q", t))
                if after_first(t):
                    for f in ("s4", "s5", "s6", "s7"):
                        dve.wait_ge(*full(f, t - 1))
                masked_queries(dve, q_bd, "q", bqk).then_inc(*emptied("q"))
            if step in ("v0", "v1"):
                b = int(step[-1])
                dve.wait_ge(*full(step, t))
                for par in range(2):
                    for j in range(2):
                        last = dve.tensor_tensor(heads_of(vz[i][:, 2 * b + j, par, :], par),
                                                 heads_of(ps(step)[:, j * D:(j + 1) * D], par),
                                                 heads_of(bvr[:, :], par), op=ALU.add)
                last.then_inc(*emptied(step))

        def dve_back(dve, step, t, n, i):
            if step in ("clip0", "clip1"):
                if step == "clip0":
                    dve_general_run(dve, t, i)
                dve_clip(dve, int(step[-1]), t, i)
            if step in ("weights0", "weights1"):
                for m in range(G * int(step[-1]) + 1, G * int(step[-1]) + G, 2):
                    dve.wait_ge(*full(f"t{m}", t))
                    if m == 1 and after_first(t):
                        dve.wait_ge(*full("av", t - 1))
                    dve.tensor_copy(flat3(aT[:, m, :, :, :]), ps(f"t{m}")[:, :]).then_inc(*emptied(f"t{m}"))
            if step == "out":
                dve.wait_ge(*full("wo", t))
                dve.wait_ge(*due("xb", t))
                dve.tensor_tensor(x1[:, :], ps("wo")[:, 0:D], xb[i][:, :], op=ALU.add).then_inc(*emptied("wo"))
                dve.wait_ge(*read_out("wo", t))
                ln_stats(dve, 1, x1[:, :], t)
            if step == "norm2":
                ln_apply(dve, 1, xn2[:, :], x1[:, :], t, "xn2")
            if step == "qkv":
                dve.wait_ge(*full("qk", t))
                masked_queries(dve, q2, "qk", bqkv)
                for c in range(KC):
                    last = dve.tensor_scalar(k2T[:, c, :], ps("qk")[:, (KC + c) * P:(KC + c + 1) * P],
                                             bqkv[:, KC + c:KC + c + 1], 0.0, ALU.add, ALU.add)
                last.then_inc(*emptied("qk"))
            if step == "latent":
                dve.wait_ge(*full("vl", t))
                for b in range(BT):
                    for par in range(2):
                        last = dve.tensor_tensor(heads_of(vz2[:, b, par, :], par), heads_of(ps("vl")[0:L, b * D:(b + 1) * D], par),
                                                 heads_of(blatv[0:L, :], par), op=ALU.add)
                last.then_inc(*emptied("vl"))
            if step == "windows":
                for g in range(G):
                    dve.wait_ge(*full(f"l{g}", t))
                    if after_first(t):
                        dve.wait_ge(*full(f"u{g}", t - 1))
                    dve.tensor_tensor(a2[:, g, :, :], ps(f"l{g}")[:, 0:BT * KC * L].rearrange("p (n k) -> p n k", k=L),
                                      wbias[:, :].unsqueeze(1).to_broadcast([P, BT * KC, L]), op=ALU.add).then_inc(*emptied(f"l{g}"))
                for g in range(G):
                    dve.wait_ge(*read_out(f"l{g}", t))
                dve.tensor_reduce(mx2[:, :, :], a2[:, :, :, :], axis=AX_X, op=ALU.max).then_inc(sem("max2"), 1)
            if step == "sum2":
                dve.wait_ge(*due("exp2", t))
                dve.tensor_reduce(sm2[:, :, :], e2[:, :, :, :], axis=AX_X, op=ALU.add).then_inc(sem("sum2"), 1)
                dve.wait_ge(*due("sum2", t))
                dve.reciprocal(rs2[:, :, :], sm2[:, :, :]).then_inc(sem("rsum2"), 1)
            if step == "proj":
                dve.wait_ge(*full("pr", t))
                dve.wait_ge(*due("x1b", t))
                if after_first(t):
                    dve.wait_ge(*due("x_kept", t - 1))
                dve.tensor_tensor(x2[:, :], ps("pr")[:, 0:D], x1b[:, :], op=ALU.add).then_inc(*emptied("pr"))
                dve.wait_ge(*read_out("pr", t))
                ln_stats(dve, 2, x2[:, :], t)
            if step == "norm3":
                if after_first(t):
                    dve.wait_ge(*full("x3T", t - 1))
                    dve.wait_ge(*due("x3_kept", t - 1))
                ln_apply(dve, 2, xn3[:, :], x2[:, :], t, "xn3")
            if step == "logits":
                dve.wait_ge(*full("rt", t))
                dve.tensor_tensor(logits[:, bass.ds(t, 1), :].rearrange("p t e -> p (t e)"), ps("rt")[:, 0:E], brr[:, :], op=ALU.add).then_inc(*emptied("rt"))

        def dve_stats(dve, b, t, i):
            for g in range(G):
                dve.wait_ge(*read_out(f"s{b * G + g}", t))
            for j in range(NJ):
                last = dve.bn_stats(out=st[i][:, b, j, :], in_=s_sb[i][:, b, j, :])
            last.then_inc(sem("stats"), 1)

        def dve_evals(dve, it, half, t, i):
            if half == 0 and it == 0:
                dve.wait_ge(*due("start_step", t, PER["start_step"]))
                if after_first(t):
                    dve.wait_ge(*due("sum_dve", t, 0))
            elif half == 0:
                dve.wait_ge(*due("update_step", t, level(it - 1, LEVELS[it - 1] - 1)))
            for m in range(ND // 2, ND) if half else range(ND // 2):
                b, j = divmod(m, NJ)
                last = dve.scalar_tensor_tensor(out=junk[:, b, j, :], in0=s_sb[i][:, b, j, :], scalar=u_it[:, it, b, j:j + 1],
                                                in1=zeros[:, :], op0=ALU.add, op1=ALU.max, accum_out=f_it[:, it, b, j:j + 1])
            last.then_inc(sem("sum_dve"), 1)

        def dve_update(dve, it, t):
            def rows(x):
                return x.rearrange("p b j -> p (b j)")

            def link(k, ins):
                ins.then_inc(sem("update_step"), 1)
                dve.wait_ge(*due("update_step", t, level(it, k)))

            u, f, psi = rows(u_it[:, it, :, :]), rows(f_it[:, it, :, :]), rows(phi[:, it, :, :])
            after = rows(u_it[:, it + 1, :, :])
            shifted, du, size, fell, rose, error, slope, scaled, inverse, step = [tmp[:, m, :] for m in range(10)]
            dve.wait_ge(*due("sum_dve", t, 2 * it + 2))
            dve.wait_ge(*due("sum_act", t, 2 * it + 2))
            dve.tensor_scalar(shifted, f, C3, 1.0, ALU.add, ALU.mult)
            if it == 0:
                link(0, dve.scalar_tensor_tensor(out=step, in0=f, scalar=-1.0, in1=rows(reach0[:, :, :]), op0=ALU.add, op1=ALU.mult))
                dve.reciprocal(psi, shifted)
                dve.tensor_tensor(after, u, step, op=ALU.subtract).then_inc(sem("update_step"), 1)
                return
            u_prev, psi_prev = rows(u_it[:, it - 1, :, :]), rows(phi[:, it - 1, :, :])
            link(0, dve.tensor_tensor(du, u, u_prev, op=ALU.subtract))
            dve.reciprocal(psi, shifted)
            link(1, dve.scalar_tensor_tensor(out=size, in0=du, scalar=-1.0, in1=du, op0=ALU.mult, op1=ALU.max))
            dve.tensor_tensor(rose, psi, psi_prev, op=ALU.subtract)
            dve.tensor_tensor(fell, psi_prev, psi, op=ALU.subtract)
            link(2, dve.tensor_scalar(error, psi, 1.0 / (1.0 + C3), 1.0, ALU.subtract, ALU.mult))
            dve.scalar_tensor_tensor(out=slope, in0=rose, scalar=1e-8, in1=fell, op0=ALU.max, op1=ALU.max)
            link(3, dve.tensor_tensor(scaled, error, size, op=ALU.mult))
            link(4, dve.reciprocal(inverse, slope))
            link(5, dve.tensor_tensor(step, scaled, inverse, op=ALU.mult))
            dve.tensor_tensor(after, u, step, op=ALU.add).then_inc(sem("update_step"), 1)

        def dve_general(dve, t, i):
            dve.wait_ge(*due("update_step", t, level(EVALS - 1, LEVELS[-1] - 1)))
            dve.tensor_scalar(off16[:, :], f_it[:, EVALS - 1, :, :].rearrange("p b j -> p (b j)"), 1.0, 1.0, ALU.subtract, ALU.mult).then_inc(sem("off_step"), 1)
            dve.wait_ge(*due("off_step", t, 1))
            dve.tensor_tensor(off16b[:, :], off16[:, :], off16[:, :], op=ALU.mult).then_inc(sem("off_step"), 1)
            dve.wait_ge(*due("off_step", t, 2))
            dve.tensor_reduce(off[:, :], off16b[:, :], axis=AX_X, op=ALU.max).then_inc(sem("off_step"), 1)

        def dve_general_run(dve, t, i):
            dve.wait_ge(*due("off_all", t))
            dve.tensor_scalar(flag[:, :], offmax[:, :], OFF_BY, 1.0, ALU.is_gt, ALU.mult).then_inc(sem("off_step"), 1)
            dve.wait_ge(*due("off_step", t, 4))
            parted(dve)
            far = dve.value_load(flag[0:1, 0:1], min_val=0, max_val=1)
            with dve.If(far > 0):
                u = u_it[:, EVALS, :, :].rearrange("p b j -> p (b j)")
                s = s_sb[i][:, :, :, :].rearrange("p b j k -> p (b j) k")
                jk = [junk[:, m // NJ, m % NJ, :] for m in range(ND)]
                gt = tmp[:, :, :].rearrange("p m j -> p (m j)")
                dve.tensor_tensor(gt[:, 0:BT * NJ], st[i][:, :, :, 1].rearrange("p b j -> p (b j)"), st[i][:, :, :, 4].rearrange("p b j -> p (b j)"), op=ALU.add)
                dve.drain()
                dve.tensor_scalar(u, gt[:, 0:BT * NJ], -0.5, 1.0 / LC, ALU.mult, ALU.add)
                dve.drain()
                with dve.Fori(0, NEWTON):
                    for j0 in range(0, BT * NJ, len(jk)):
                        js = range(j0, min(j0 + len(jk), BT * NJ))
                        for j in js:
                            dve.scalar_tensor_tensor(out=jk[j - j0], in0=s[:, j, :], scalar=u[:, j:j + 1], in1=zeros[:, :],
                                                     op0=ALU.add, op1=ALU.max, accum_out=gt[:, j:j + 1])
                        dve.drain()
                        for j in js:
                            dve.tensor_scalar(jk[j - j0], jk[j - j0], 0.0, 0.0, ALU.is_gt, ALU.add, accum_out=gt[:, 16 + j:17 + j])
                        dve.drain()
                    dve.tensor_scalar(gt[:, 32:48], gt[:, 16:32], 1.0, 1.0, ALU.max, ALU.mult)
                    dve.drain()
                    dve.reciprocal(gt[:, 48:64], gt[:, 32:48])
                    dve.drain()
                    dve.scalar_tensor_tensor(out=gt[:, 64:80], in0=gt[:, 0:16], scalar=-1.0, in1=gt[:, 48:64], op0=ALU.add, op1=ALU.mult)
                    dve.drain()
                    dve.tensor_tensor(u, u, gt[:, 64:80], op=ALU.subtract)
                    dve.drain()

        def dve_clip(dve, b, t, i):
            for j in range(NJ):
                last = dve.tensor_scalar(s_sb[i][:, b, j, :], s_sb[i][:, b, j, :], u_it[:, EVALS, b, j:j + 1], 0.0, ALU.add, ALU.max)
            last.then_inc(sem("clip"), 1)

        def pool_start(pool, b, t, i):
            def link(k, ins):
                ins.then_inc(sem("start_step"), 1)
                pool.wait_ge(*due("start_step", t, STARTS * b + k))
                parted(pool)

            mean2, squares, root, curved, center, near, far = [guess[:, b, m, :] for m in range(7)]
            halves = st[i][:, b, :, :]
            pool.wait_ge(*due("stats", t, b + 1))
            pool.tensor_tensor(mean2, halves[:, :, 1], halves[:, :, 4], op=ALU.add)
            link(1, pool.tensor_tensor(squares, halves[:, :, 2], halves[:, :, 5], op=ALU.add))
            pool.tensor_scalar(curved, squares, -A2 / LC, -A0, ALU.mult, ALU.add)
            pool.tensor_scalar(center, mean2, -0.5, 0.0, ALU.mult, ALU.add)
            link(2, pool.tensor_tensor(root, squares, phalf[:, :], op=ALU.pow))
            pool.tensor_scalar(reach0[:, b, :], root, G1 / LC ** 0.5, G0, ALU.mult, ALU.add)
            pool.tensor_scalar(far, root, -A1 / LC ** 0.5, 0.0, ALU.mult, ALU.add)
            link(3, pool.tensor_tensor(near, curved, center, op=ALU.add))
            pool.tensor_tensor(u_it[:, 0, b, :], near, far, op=ALU.add).then_inc(sem("start_step"), 1)

        def pool_front(pool, step, t, n, i):
            if step == "stats":
                ln_rstd(pool, 0, t)
            if step in ("start0", "start1"):
                pool_start(pool, int(step[-1]), t, i)
            if step == "xb":
                pool.wait_ge(sem(f"x_in{i}"), n * 16 + 16)
                if not (isinstance(n, int) and n == 0):
                    pool.wait_ge(*read_out("wo", t - 2))
                pool.tensor_tensor(xb[i][:, :], xin[i][:, :], bor[:, :], op=ALU.add).then_inc(sem("xb"), 1)

        def pool_back(pool, step, t, n, i):
            if step == "out":
                ln_rstd(pool, 1, t)
                pool.tensor_tensor(x1b[:, :], x1[:, :], bpr[:, :], op=ALU.add).then_inc(sem("x1b"), 1)
            if step == "windows":
                pool.wait_ge(*due("max2", t))
                pool.tensor_tensor(e2[:, :, :, :].rearrange("p g n k -> p (g n) k"), a2[:, :, :, :].rearrange("p g n k -> p (g n) k"),
                                   mx2[:, :, :].rearrange("p g n -> p (g n)").unsqueeze(2).to_broadcast([P, G * BT * KC, L]),
                                   op=ALU.subtract).then_inc(sem("shifted2"), 1)
            if step == "sum2":
                pool.wait_ge(*due("rsum2", t))
                pool.tensor_tensor(a2[:, :, :, :].rearrange("p g n k -> p (g n) k"), e2[:, :, :, :].rearrange("p g n k -> p (g n) k"),
                                   rs2[:, :, :].rearrange("p g n -> p (g n)").unsqueeze(2).to_broadcast([P, G * BT * KC, L]),
                                   op=ALU.mult).then_inc(sem("weights2"), 1)
            if step == "proj":
                ln_rstd(pool, 2, t)
                pool.tensor_copy(x_all[:, bass.ds(t * D, D)], x2[:, :]).then_inc(sem("x_kept"), 1)
            if step == "router":
                pool.wait_ge(*due("xn3", t))
                pool.tensor_copy(x3_all[:, bass.ds(t, 1), :].rearrange("p t d -> p (t d)"), xn3[:, :]).then_inc(sem("x3_kept"), 1)

        def pool_off(pool, t):
            pool.wait_ge(*due("off_step", t, 3))
            parted(pool)
            pool.partition_all_reduce(offmax[:, :], off[:, :], P, bass.bass_isa.ReduceOp.max).then_inc(sem("off_all"), 1)

        def steps_of(tiles, stages):
            for stage, step in PASS:
                if stage in stages and tiles[stage]:
                    n, i = tiles[stage]
                    yield stage, step, n, i, 2 * n + i

        def pe_pass(pe, ahead={}, **tiles):
            for stage, step, n, i, t in steps_of(tiles, "FBC"):
                if step in ahead:
                    ahead[step](pe)
                if stage == "F":
                    pe_front(pe, step, t, n, i)
                else:
                    pe_back(pe, step, t, i)

        def act_pass(act, ahead={}, **tiles):
            for stage, step, n, i, t in steps_of(tiles, "FMBC"):
                if step in ahead:
                    ahead[step](act)
                if stage == "F":
                    act_front(act, step, t, i)
                elif stage == "M":
                    if step.startswith("sums"):
                        act_evals(act, int(step[4]), int(step[5]), t, i)
                else:
                    act_back(act, step, t, i)

        def dve_pass(dve, ahead={}, **tiles):
            for stage, step, n, i, t in steps_of(tiles, "FMBC"):
                if step in ahead:
                    ahead[step](dve)
                if stage == "F":
                    dve_front(dve, step, t, n, i)
                elif stage == "M":
                    if step.startswith("sums"):
                        dve_evals(dve, int(step[4]), int(step[5]), t, i)
                    elif step.startswith("update"):
                        dve_update(dve, int(step[6]), t)
                    else:
                        dve_general(dve, t, i)
                else:
                    dve_back(dve, step, t, n, i)

        def pool_pass(pool, ahead={}, **tiles):
            for stage, step, n, i, t in steps_of(tiles, "FMBC"):
                if step in ahead:
                    ahead[step](pool)
                if stage == "F":
                    pool_front(pool, step, t, n, i)
                elif stage == "M":
                    if step == "general":
                        pool_off(pool, t)
                else:
                    pool_back(pool, step, t, n, i)

        def passes(eng, one_pass, before_back=None, ahead_in_back={}, before_last=None, ahead_in_last={}):
            one_pass(eng, F=(0, 0), M=None, B=None, C=None)
            one_pass(eng, F=(0, 1), M=(0, 0), B=None, C=None)
            eng.wait_ge(sem("w_back"), 16 * len(loads_back))
            if before_back:
                before_back(eng)
            one_pass(eng, F=(1, 0), M=(0, 1), B=(0, 0), C=None)
            one_pass(eng, F=(1, 1), M=(1, 0), B=(0, 1), C=(0, 0))
            with eng.Fori(2, T // 2) as n:
                one_pass(eng, F=(n, 0), M=(n - 1, 1), B=(n - 1, 0), C=(n - 2, 1))
                one_pass(eng, F=(n, 1), M=(n, 0), B=(n - 1, 1), C=(n - 1, 0))
            last = T // 2 - 1
            one_pass(eng, F=None, M=(last, 1), B=(last, 0), C=(last - 1, 1))
            one_pass(eng, F=None, M=None, B=(last, 1), C=(last, 0), ahead=ahead_in_back)
            if before_last:
                before_last(eng)
            one_pass(eng, F=None, M=None, B=None, C=(last, 1), ahead=ahead_in_last)

        route_steps = [0]

        def link(dve, ins):
            ins.then_inc(sem("route_step"), 1)
            route_steps[0] += 1
            dve.wait_ge(sem("route_step"), route_steps[0])

        def tiled(x):
            return x.rearrange("p (t e) -> p t e", e=E)

        def act_exp(act, part):
            t0, t1 = PARTS[part]
            act.wait_ge(sem("logits_shifted"), part + 1)
            act.activation(flat(ex3[:, t0:t1, :]), flat(rt_a[:, t0:t1, :]), ACT.Exp).then_inc(sem("router_exp"), 1)

        def dve_choose(dve, part):
            t0, t1 = PARTS[part]

            def per_tile(k):
                return rt_r[:, k, t0:t1]

            def spread(k):
                return rt_r[:, k, t0:t1].unsqueeze(2).to_broadcast([P, t1 - t0, E])

            def of(x):
                return x[:, t0:t1, :]

            order = order8[:, :].unsqueeze(1).to_broadcast([P, t1 - t0, E])
            dve.wait_ge(*read_out("rt", t1 - 1))
            link(dve, dve.tensor_reduce(per_tile(0), of(logits), axis=AX_X, op=ALU.max))
            dve.tensor_tensor(of(rt_a), of(logits), spread(0), op=ALU.subtract).then_inc(sem("logits_shifted"), 1)
            dve.wait_ge(sem("router_exp"), part + 1)
            link(dve, dve.tensor_reduce(per_tile(1), of(ex3), axis=AX_X, op=ALU.add))
            link(dve, dve.reciprocal(per_tile(2), per_tile(1)))
            link(dve, dve.tensor_tensor(of(probs), of(ex3), spread(2), op=ALU.mult))
            left = probs
            for k in range(2):
                link(dve, dve.tensor_reduce(per_tile(3 + 2 * k), of(left), axis=AX_X, op=ALU.max))
                link(dve, dve.tensor_tensor(of(rt_b), of(left), spread(3 + 2 * k), op=ALU.is_equal))
                link(dve, dve.tensor_tensor(of(ex3), of(rt_b), order, op=ALU.mult))
                link(dve, dve.tensor_reduce(per_tile(4 + 2 * k), of(ex3), axis=AX_X, op=ALU.max))
                link(dve, dve.tensor_tensor(chosen[:, k, t0:t1, :], order, spread(4 + 2 * k), op=ALU.is_equal))
                if k == 0:
                    link(dve, dve.scalar_tensor_tensor(out=of(rt_a), in0=chosen[:, 0, t0:t1, :], scalar=-2.0, in1=of(probs),
                                                       op0=ALU.mult, op1=ALU.add))
                    left = rt_a
            dve.tensor_tensor(tiled(selected[:, t0 * E:t1 * E]), chosen[:, 0, t0:t1, :], chosen[:, 1, t0:t1, :], op=ALU.add)\
               .then_inc(sem("selected"), 1)

        def dve_place(dve, part):
            t0, t1 = PARTS[part]
            dve.wait_ge(sem("ranked"), part + 1)
            link(dve, dve.tensor_tensor(place[:, t0:t1, :], tiled(bank[2 * part][:, 0:(t1 - t0) * E]),
                                        home[:, part, :].unsqueeze(1).to_broadcast([P, t1 - t0, E]), op=ALU.add))
            for k in range(2):
                link(dve, dve.tensor_tensor(ex3[:, t0:t1, :], chosen[:, k, t0:t1, :], place[:, t0:t1, :], op=ALU.mult))
                link(dve, dve.tensor_reduce(slot_f[:, k, t0:t1], ex3[:, t0:t1, :], axis=AX_X, op=ALU.add))
                dve.tensor_copy(list_slot[:, k, t0:t1], slot_f[:, k, t0:t1]).then_inc(sem("slots"), 1)
            link(dve, dve.tensor_reduce(count[:, 5 + part, :], bank[2 * part + 1][:, 0:(t1 - t0) * E].rearrange("p (t e) -> p e t", e=E),
                                        axis=AX_X, op=ALU.add))
            if part == 0:
                dve.tensor_tensor(home[:, 1, :], home[:, 0, :], count[:, 5, :], op=ALU.add).then_inc(sem("home_moved"), 1)

        def dve_blocks(dve):
            link(dve, dve.tensor_tensor(count[:, 0, :], count[:, 5, :], count[:, 6, :], op=ALU.add))
            link(dve, dve.tensor_tensor(over[:, :, :], count[:, 0, :].unsqueeze(2).to_broadcast([P, E, T - 1]),
                                        steps[:, :].unsqueeze(1).to_broadcast([P, E, T - 1]), op=ALU.is_gt))
            link(dve, dve.tensor_reduce(count[:, 1, :], over[:, :, :], axis=AX_X, op=ALU.add))
            link(dve, dve.tensor_scalar(count[:, 2, :], count[:, 1, :], 1.0, 1.0, ALU.add, ALU.mult))
            link(dve, dve.tensor_tensor(summed[:, :, :], count[:, 2, :].unsqueeze(1).to_broadcast([P, E, E]), before8[:, :, :], op=ALU.mult))
            link(dve, dve.tensor_reduce(count[:, 3, :], summed[:, :, :], axis=AX_X, op=ALU.add))
            dve.tensor_copy(blocks[:, 0:E], count[:, 2, :]).then_inc(sem("blocks"), 1)
            dve.tensor_copy(blocks[:, E:2 * E], count[:, 3, :]).then_inc(sem("blocks"), 1)
            link(dve, dve.tensor_scalar(count[:, 7, :], count[:, 3, :], float(P), float(P), ALU.mult, ALU.add))
            link(dve, dve.tensor_tensor(count[:, 4, :], count[:, 7, :], home[:, 0, :], op=ALU.subtract))
            link(dve, dve.tensor_tensor(rt_b[:, :, :], place[:, :, :], count[:, 4, :].unsqueeze(1).to_broadcast([P, T, E]), op=ALU.add))
            for k in range(2):
                link(dve, dve.tensor_tensor(ex3[:, :, :], chosen[:, k, :, :], rt_b[:, :, :], op=ALU.mult))
                link(dve, dve.tensor_reduce(slot_f[:, k, :], ex3[:, :, :], axis=AX_X, op=ALU.add))
                dve.tensor_copy(slot[:, k, :], slot_f[:, k, :]).then_inc(sem("result_slots"), 1)

        hT = s_sb[0][:, 0, :, :].rearrange("p j k -> p (j k)")[:, 0:FC * P].rearrange("p (f n) -> p f n", f=FC)
        gathered = s_sb[1]
        SEEDS = {"result_ready": 1, "turned": 1}

        def expert_loop(eng, each_block, at_expert=None):
            eng.wait_ge(sem("blocks"), 2)

            def expert(r, i):
                if at_expert:
                    at_expert(eng, r, i)
                n = eng.value_load(blocks[0:1, bass.ds(r * 2 + i, 1)], min_val=1, max_val=T)
                first = eng.value_load(blocks[0:1, bass.ds(r * 2 + (E + i), 1)], min_val=0, max_val=MAX_BLOCKS - 1)
                with eng.Fori(0, n) as j:
                    each_block(eng, first + j, i, r * (2 * T) + (i * T + j))

            with eng.Fori(0, E // 2 - 1) as r:
                for i in range(2):
                    expert(r, i)
            for i in range(2):
                expert(E // 2 - 1, i)

        def pe_turn():
            return transposed(bank[3], xe)

        def pe_expert_weights(pe, r, i):
            pe.wait_ge(sem(f"w_exp{i}"), r * 32 + 32)
            parted(pe)

        def pe_block(pe, g, i, _):
            pe.wait_ge(sem("rows_turned"), g + 1)
            for f in range(FC):
                for kk in range(KC):
                    last = mm(bank[f // 4][:, (f % 4) * P:(f % 4 + 1) * P], wup[i][:, kk, f * P:(f + 1) * P], xeT[:, kk, :],
                              start=(kk == 0), stop=(kk == KC - 1))
                if f % 4 == 3:
                    last.then_inc(sem("up"), 1)
            pe.wait_ge(sem("rows_in"), g * 16 + 32)
            pe_turn().then_inc(sem("turned"), 1)
            pe.wait_ge(sem("result_ready"), g + SEEDS["result_ready"])
            for f in range(FC):
                if f % 4 == 0:
                    pe.wait_ge(sem("hidden"), g * 2 + (f // 4 + 1))
                last = mm(bank[2][:, 0:D], hT[:, f, :], wdn[i][:, f, :], start=(f == 0), stop=(f == FC - 1))
            last.then_inc(sem("down"), 1)

        def act_block(act, g, i, _):
            for h in range(2):
                act.wait_ge(sem("up"), g * 2 + (h + 1))
                act.activation(flat(hT[:, 4 * h:4 * h + 4, :]), bank[h][:, :], ACT.Gelu).then_inc(sem("hidden"), 1)
            act_store(act, g)

        def act_store(act, g):
            act.wait_ge(sem("result_ready"), g + SEEDS["result_ready"])
            parted(act)
            act.dma_start(results_d[bass.ds(g, 1), :, :].rearrange("t p d -> p (t d)"), ye[:, :]).then_inc(sem("result_stored"), 16)

        def dve_turned(dve, g):
            dve.wait_ge(sem("turned"), g + (1 + SEEDS["turned"]))
            dve.tensor_copy(flat(xeT[:, :, :]), bank[3][:, 0:D]).then_inc(sem("rows_turned"), 1)

        def dve_block(dve, g, i, _):
            dve_turned(dve, g + 1)
            dve.wait_ge(sem("down"), g + 1)
            dve.wait_ge(sem("result_stored"), g * 16 + 16)
            dve.tensor_copy(ye[:, :], bank[2][:, 0:D]).then_inc(sem("result_ready"), 1)

        def sp_block(sp, g, i, at):
            sp.wait_ge(sem("turned"), g + SEEDS["turned"])
            parted(sp)
            sp.dma_start(xe[:, :], lists_d[bass.ds(at, 1), :, :].rearrange("t p d -> p (t d)")).then_inc(sem("rows_in"), 16)

        def blocks_till(eng):
            return eng.value_load(blocks[0:1, E - 1:E], min_val=1, max_val=T) + \
                eng.value_load(blocks[0:1, 2 * E - 1:2 * E], min_val=0, max_val=MAX_BLOCKS - 1)

        def pool_expert(pool, e, i):
            pool.dma_start(wup[i][:, :, :], up_d[:, :, bass.ds(e, 1), :].rearrange("p c e f -> p c (e f)")).then_inc(sem(f"w_exp{i}"), 16)
            pool.dma_start(wdn[i][:, :, :], dn_d[:, :, bass.ds(e, 1), :].rearrange("p c e d -> p c (e d)")).then_inc(sem(f"w_exp{i}"), 16)

        def pool_first_experts(pool):
            parted(pool)
            for e in range(2):
                pool_expert(pool, e, e)

        def pool_weights(pool):
            pool.wait_ge(sem("blocks"), 2)
            parted(pool)
            with pool.Fori(0, E // 2 - 1) as r:
                for i in range(2):
                    first_behind = pool.value_load(blocks[0:1, bass.ds(r * 2 + (E + i + 1), 1)], min_val=0, max_val=MAX_BLOCKS - 1)
                    pool.wait_ge(sem("down"), first_behind)
                    parted(pool)
                    pool_expert(pool, r * 2 + (i + 2), i)

        def sp_experts(sp):
            sp.wait_ge(sem("scattered"), 16 * 2 * T)
            expert_loop(sp, sp_block)
            total = blocks_till(sp)
            sp.wait_ge(sem("turned"), total + SEEDS["turned"])
            parted(sp)
            sp.dma_start(xe[:, :], lists_d[0, :, :]).then_inc(sem("rows_in"), 16)
            sp.wait_ge(sem("result_stored"), total * 16 + 16)
            parted(sp)
            sp.wait_ge(sem("rows_in"), total * 16 + 16)
            parted(sp)
            sp.sem_inc(sem("results_stored"), 1)
            for t in range(T):
                sp.wait_ge(sem(f"added{t}"), 2)
                sp.dma_start(out_d[:, t, :], x_all[:, t * D:(t + 1) * D]).then_inc(sem("out"), 16)
            sp.wait_ge(sem("out"), 16 * T)

        def pe_rank(pe, part):
            t0, t1 = PARTS[part]
            if part == 0:
                for i in range(4):
                    pe.wait_ge(sem(f"bank{i}_free"), len(FILLS[i]) * T)
            pe.wait_ge(sem("selected"), part + 1)
            for s in range(t1 - t0):
                last = mm(bank[2 * part][:, s * E:(t1 - t0) * E], ones[:, :] if s else earlier[:, :], selected[:, t0 * E:(t1 - s) * E],
                          start=(s == 0), stop=(s == t1 - t0 - 1))
            mm(bank[2 * part + 1][:, 0:(t1 - t0) * E], ones[:, :], selected[:, t0 * E:t1 * E], start=True, stop=True)\
                .then_inc(sem("ranked"), 1)

        def pool_scatter(pool, part, first=0, end=None):
            t0, t1 = PARTS[part]
            rows = [(k, t) for k in range(2) for t in range(t0, t1)][first:end]
            pool.wait_ge(sem("lists_zeroed"), 16)
            pool.wait_ge(*due("x3_kept", t1 - 1))
            pool.wait_ge(sem("slots"), 2 * part + 2)
            for k, t in rows:
                pool.indirect_dma_start(out=lists, out_offset=bass.IndirectOffsetOnAxis(ap=list_slot[:, k, t:t + 1], axis=0),
                                        in_=x3_all[:, t, :], in_offset=None).then_inc(sem("scattered"), 16)

        def pool_gather(pool):
            pool.wait_ge(sem("result_slots"), 2)
            pool.wait_ge(sem("results_stored"), 1)
            for t in range(T):
                for k in range(2):
                    pool.indirect_dma_start(out=gathered[:, k, t, :], out_offset=None, in_=results,
                                            in_offset=bass.IndirectOffsetOnAxis(ap=slot[:, k, t:t + 1], axis=0)).then_inc(sem(f"gathered{t}"), 16)

        def dve_combine(dve):
            def add(t, k):
                acc = x_all[:, t * D:(t + 1) * D]
                if k == 0:
                    dve.wait_ge(sem(f"gathered{t}"), 32)
                else:
                    dve.wait_ge(sem(f"added{t}"), 1)
                dve.scalar_tensor_tensor(out=acc, in0=gathered[:, k, t, :], scalar=rt_r[:, 3 + 2 * k, t:t + 1], in1=acc,
                                         op0=ALU.mult, op1=ALU.add).then_inc(sem(f"added{t}"), 1)
            for t in range(T + 1):
                if t < T:
                    add(t, 0)
                if t:
                    add(t - 1, 1)

        def weights_arrived(eng):
            eng.wait_ge(sem("w_q"), 16 * len(loads_q))
            eng.wait_ge(sem("w_kv"), 16 * len(loads_kv))

        @block.sync
        def _(sp):
            sp_front(sp, 0, 0)
            for dst, src in loads_q:
                sp.dma_start(whole(dst), src).then_inc(sem("w_q"), 16)
            for dst, src in loads_kv:
                sp.dma_start(whole(dst), src).then_inc(sem("w_kv"), 16)
            sp_front(sp, 0, 1)
            for dst, src in loads_back:
                sp.dma_start(dst if dst is loads_back[-1][0] else whole(dst), src).then_inc(sem("w_back"), 16)
            with sp.Fori(1, T // 2) as n:
                for i in range(2):
                    sp_front(sp, n, i)
            sp.wait_ge(sem("zeros"), 1)
            sp.dma_start(lists.rearrange("(n p) d -> p n d", p=P),
                         zeros[:, :].unsqueeze(1).to_broadcast([P, E * T, D])).then_inc(sem("lists_zeroed"), 16)
            sp.dma_start(results.rearrange("(n p) d -> p n d", p=P),
                         zeros[:, :].unsqueeze(1).to_broadcast([P, reach, D])).then_inc(sem("results_zeroed"), 16)
            sp_experts(sp)

        @block.tensor
        def _(pe):
            weights_arrived(pe)
            passes(pe, pe_pass, before_last=lambda pe: pe_rank(pe, 0))
            pe_rank(pe, 1)
            pe.wait_ge(sem("blocks"), 2)
            pe.wait_ge(sem("rows_in"), 16)
            pe_turn().then_inc(sem("turned"), 1)
            expert_loop(pe, pe_block, at_expert=pe_expert_weights)

        @block.scalar
        def _(act):
            weights_arrived(act)
            passes(act, act_pass, ahead_in_back={"exp2": lambda act: act_exp(act, 0)})
            act_exp(act, 1)
            act.wait_ge(sem("results_zeroed"), 16)
            expert_loop(act, act_block)
            act_store(act, blocks_till(act))

        @block.vector
        def _(dve):
            dve.memset(zeros[:, :], 0.0).then_inc(sem("zeros"), 1)
            weights_arrived(dve)
            dve.wait_ge(sem("zeros"), 1)
            dve.wait_ge(sem("zeroed"), ZEROED)
            passes(dve, dve_pass, ahead_in_back={"sum2": lambda dve: dve_choose(dve, 0)},
                   before_last=lambda dve: dve_place(dve, 0))
            dve.wait_ge(*due("x_kept", T - 1))
            dve_choose(dve, 1)
            dve.wait_ge(sem("home_moved"), 1)
            dve_place(dve, 1)
            dve_blocks(dve)
            dve.sem_inc(sem("result_ready"), SEEDS["result_ready"])
            dve.sem_inc(sem("turned"), SEEDS["turned"])
            dve_turned(dve, 0)
            expert_loop(dve, dve_block)
            dve_combine(dve)

        @block.gpsimd
        def _(pool):
            for dst, value in ((nhalf, -0.5), (phalf, 0.5), (vz[0], 0.0), (vz[1], 0.0), (vz2, 0.0), (ones, 1.0)):
                pool.memset(whole(dst), value).then_inc(sem("zeroed"), 1)
            pool.wait_ge(sem("zeroed"), ZEROED)
            weights_arrived(pool)
            passes(pool, pool_pass, before_back=pool_first_experts, before_last=lambda pool: pool_scatter(pool, 0, end=EARLY),
                   ahead_in_last={"logits": lambda pool: pool_scatter(pool, 0, first=EARLY)})
            pool_scatter(pool, 1)
            pool_weights(pool)
            pool_gather(pool)


INPUTS = ["x", "ctxT", "wq", "wk", "wv", "wo", "wqkv", "wproj", "wlat", "wr", "bqk", "bqkv", "blatk",
          "bv", "bo", "blatv", "bproj", "br", "ident", "parity", "wbias", "order8", "earlier", "steps", "before8", "home", "upT", "downT"]


def layouts(i):
    def c(x):
        return np.ascontiguousarray(x)

    def column(b):
        return c(b.reshape(-1, P).T)

    def rows(b):
        return c(np.broadcast_to(b.reshape(1, -1), (P, b.size)))

    heads = P // HD
    wlat = np.zeros((heads, HD, heads, HD), np.float32)
    for h in range(heads):
        wlat[h, :, h, :] = i["L0_attn_W_lat"].T
    p = np.arange(P)
    parity = np.where((p[:, None] // HD) % 2 == np.arange(2)[None, :], SCALE, 0.0).astype(np.float32)
    count = np.zeros((L, L))
    for q in range(L):
        win = list(range(max(0, q - 3), min(L, q + 4)))
        win += [L - 1 if q < 3 else 0] * (7 - len(win))
        for k in win:
            count[q, k] += 1
    wbias = np.full((L, L), MASKED, np.float32)
    wbias[count > 0] = np.log(count[count > 0])
    return {
        "x": i["x"].reshape(B * L, D), "ctxT": c(i["ctx_1024"].reshape(B * LC, D).T),
        "wq": i["L0_xattn_Wq"], "wk": i["L0_xattn_Wk"], "wv": i["L0_xattn_Wv"], "wo": i["L0_xattn_Wo"],
        "wqkv": c(i["L0_attn_W_qkv"].T), "wproj": c(i["L0_attn_W_proj"].T), "wlat": wlat.reshape(P, P),
        "wr": i["L0_ffn_router_w"],
        "bqk": column(np.concatenate([i["L0_xattn_bq"], i["L0_xattn_bk"]])), "bqkv": column(i["L0_attn_b_qkv"]),
        "blatk": c(np.tile(i["L0_attn_b_lat"], heads).reshape(P, 1)),
        "bv": rows(i["L0_xattn_bv"]), "bo": rows(i["L0_xattn_bo"]), "blatv": rows(np.tile(i["L0_attn_b_lat"], H)),
        "bproj": rows(i["L0_attn_b_proj"]), "br": rows(i["L0_ffn_router_b"]),
        "ident": np.eye(P, dtype=np.float32), "parity": parity, "wbias": c(np.tile(wbias, (2, 1))),
        "order8": np.tile(np.arange(E, 0, -1, dtype=np.float32), (P, 1)),
        "earlier": np.triu(np.ones((P, P), np.float32), 1),
        "steps": np.tile(P * np.arange(1, T, dtype=np.float32), (P, 1)),
        "home": np.tile(P * T * np.arange(E, dtype=np.float32), (P, 1)),
        "before8": c(np.broadcast_to(np.tril(np.ones((E, E), np.float32), -1), (P, E, E))),
        "upT": c(i["L0_ffn_expert_up"].transpose(0, 2, 1)), "downT": c(i["L0_ffn_expert_down"].transpose(0, 2, 1)),
    }


def kernel(**inputs):
    import concourse.bacc as bacc
    from concourse.bass_utils import run_bass_kernel_spmd

    arrays = layouts({k: np.asarray(v) for k, v in inputs.items()})
    nc = bacc.Bacc("TRN2", target_bir_lowering=False, num_devices=1)
    aps = {n: nc.dram_tensor(f"in_{n}", arrays[n].shape, F32, kind="ExternalInput").ap() for n in INPUTS}
    out = nc.dram_tensor("out", (B * L, D), F32, kind="ExternalOutput").ap()
    program(nc, aps, out)
    got = run_bass_kernel_spmd(nc, [{f"in_{n}": arrays[n] for n in INPUTS}], core_ids=[0])
    return got.results[0]["out"].reshape(B, L, D)
```
